# Optimizing a Trainium2 kernel written in Bass

```python
import numpy as np
import jax
import jax.numpy as jnp

def _softmax(x, axis=-1):
    return jax.nn.softmax(x, axis=axis)

def _gelu(x):
    return jax.nn.gelu(x, approximate=True)

def _silu(x):
    return jax.nn.silu(x)

def _sigmoid(x):
    return jax.nn.sigmoid(x)

def _layernorm(x, axis=-1, eps=1e-05):
    m = jnp.mean(x, axis=axis, keepdims=True)
    v = jnp.var(x, axis=axis, keepdims=True)
    return (x - m) / jnp.sqrt(v + eps)

def _scatter_add(tgt, idx, src, axis=0):
    return tgt.at[idx].add(src)

def _segment_sum(src, seg, n):
    return jax.ops.segment_sum(src, seg, n)
kernel_name = 'mk_gnn_ffn_d2_gnn_r8_206b7a'

def setup_inputs(seed: int=0):
    np.random.seed(seed)
    _w = jnp.asarray

    def _rec_inputs():
        import jax
        import jax.numpy as jnp
        _gk = jax.random.key(seed)
        x = -0.0003713 + 1 * jax.random.normal(jax.random.fold_in(_gk, 1), (6250, 256), jnp.float32)
        src = jax.random.randint(jax.random.fold_in(_gk, 2), (100000,), 0, 6250, jnp.int32)
        dst = jax.random.randint(jax.random.fold_in(_gk, 3), (100000,), 0, 6250, jnp.int32)
        _o = jnp.argsort(dst, stable=True)
        src = src[_o]
        dst = dst[_o]
        return (x, src, dst)
    x, src, dst = _rec_inputs()

    def _L0_gnn_setup():
        import jax, jax.numpy as jnp
        import numpy as np
        N, E, D, K, L = (6250, 200000, 256, 4, 2)
        TAU = 1.0

        def _scatter_mean(src, row, num_segments):
            sums = jax.ops.segment_sum(src, row, num_segments=num_segments)
            cnt = jax.ops.segment_sum(jnp.ones((src.shape[0],), dtype=src.dtype), row, num_segments=num_segments)
            return sums / jnp.maximum(cnt, 1.0)[:, None]
        key = jax.random.key(seed)
        k1, k2, k3, k4, k5 = jax.random.split(key, 5)
        x = jax.random.normal(k1, (N, D), dtype=jnp.float32)
        edge_index = jax.random.randint(k2, (2, E), 0, N, dtype=jnp.int64)
        lim_w = float(np.sqrt(6.0 / (2 * D + D)))
        W = jax.random.uniform(k3, (L, K, 2 * D, D), minval=-lim_w, maxval=lim_w, dtype=jnp.float32)
        lim_e = float(np.sqrt(1.0 / D))
        envW = jax.random.uniform(k4, (L, D, K), minval=-lim_e, maxval=lim_e, dtype=jnp.float32)
        envb = jax.random.uniform(k5, (L, K), minval=-lim_e, maxval=lim_e, dtype=jnp.float32)
        return {'x': x, 'edge_index': edge_index, 'W': W, 'envW': envW, 'envb': envb}
    _L0_gnn_all = _L0_gnn_setup()
    _L0_gnn_in = {k: v for k, v in _L0_gnn_all.items() if k in ('W', 'envW', 'envb')}
    del _L0_gnn_all

    def _L0_ffn_setup():
        import jax, jax.numpy as jnp
        import numpy as np
        DIM = 256
        H = 8
        D = 64
        G = 64
        INNER = H * D
        SCALE = D ** (-0.5)
        key = jax.random.key(seed)
        ks = jax.random.split(key, 12)
        B, N = (4, 2048)
        x = jax.random.normal(ks[0], (B, N, DIM), dtype=jnp.float32)
        s = lambda fan_in: 1.0 / np.sqrt(fan_in)
        W_fx = jax.random.normal(ks[1], (DIM, INNER), dtype=jnp.float32) * s(DIM)
        b_fx = jnp.zeros((INNER,), dtype=jnp.float32)
        W_x = jax.random.normal(ks[2], (DIM, INNER), dtype=jnp.float32) * s(DIM)
        b_x = jnp.zeros((INNER,), dtype=jnp.float32)
        A = jax.random.normal(ks[3], (G, D), dtype=jnp.float32)
        Q, _ = jnp.linalg.qr(A.T)
        W_slice = Q[:, :G].astype(jnp.float32)
        b_slice = jnp.zeros((G,), dtype=jnp.float32)
        W_q = jax.random.normal(ks[4], (D, D), dtype=jnp.float32) * s(D)
        W_k = jax.random.normal(ks[5], (D, D), dtype=jnp.float32) * s(D)
        W_v = jax.random.normal(ks[6], (D, D), dtype=jnp.float32) * s(D)
        W_out = jax.random.normal(ks[7], (INNER, DIM), dtype=jnp.float32) * s(INNER)
        b_out = jnp.zeros((DIM,), dtype=jnp.float32)
        temperature = jnp.ones((1, H, 1, 1), dtype=jnp.float32) * 0.5
        return {'x': x, 'W_fx': W_fx, 'b_fx': b_fx, 'W_x': W_x, 'b_x': b_x, 'W_slice': W_slice, 'b_slice': b_slice, 'W_q': W_q, 'W_k': W_k, 'W_v': W_v, 'W_out': W_out, 'b_out': b_out, 'temperature': temperature}
    _L0_ffn_all = _L0_ffn_setup()
    _L0_ffn_in = {k: v for k, v in _L0_ffn_all.items() if k in ('W_fx', 'b_fx', 'W_x', 'b_x', 'W_slice', 'b_slice', 'W_q', 'W_k', 'W_v', 'W_out', 'b_out', 'temperature')}
    del _L0_ffn_all

    def _L1_gnn_setup():
        import jax, jax.numpy as jnp
        import numpy as np
        NEG_SLOPE = 0.2
        EPS = 1e-08
        N, E, IN_F, OUT_F, H = (6250, 100000, 256, 32, 8)
        key = jax.random.key(seed)
        k1, k2, k3, k4, k5 = jax.random.split(key, 5)
        x = jax.random.normal(k1, (N, IN_F), dtype=jnp.float32)
        edge_index = jax.random.randint(k2, (2, E), 0, N, dtype=jnp.int32)
        bw = float(np.sqrt(6.0 / (IN_F + OUT_F)))
        W = jax.random.uniform(k3, (H, IN_F, OUT_F), minval=-bw, maxval=bw, dtype=jnp.float32)
        ba = float(np.sqrt(6.0 / (OUT_F + 1)))
        a_src = jax.random.uniform(k4, (H, OUT_F), minval=-ba, maxval=ba, dtype=jnp.float32)
        a_dst = jax.random.uniform(k5, (H, OUT_F), minval=-ba, maxval=ba, dtype=jnp.float32)
        return {'x': x, 'edge_index': edge_index, 'W': W, 'a_src': a_src, 'a_dst': a_dst}
    _L1_gnn_all = _L1_gnn_setup()
    _L1_gnn_in = {k: v for k, v in _L1_gnn_all.items() if k in ('W', 'a_src', 'a_dst')}
    del _L1_gnn_all

    def _L1_ffn_setup():
        import jax, jax.numpy as jnp
        import numpy as np
        C = 256
        HID = 1024
        E = 8
        TEMP = 1.0
        key = jax.random.key(seed)
        ks = jax.random.split(key, 7)
        x = jax.random.normal(ks[0], (8, 2048, C), dtype=jnp.float32)
        W1 = jax.random.normal(ks[1], (C, HID), dtype=jnp.float32) * 0.02
        b1 = jnp.zeros((HID,), dtype=jnp.float32)
        Wg = jax.random.normal(ks[2], (HID, E), dtype=jnp.float32) * 0.02
        bg = jnp.zeros((E,), dtype=jnp.float32)
        Wd = jax.random.normal(ks[3], (E, HID, C), dtype=jnp.float32) * 0.02
        bd = jnp.zeros((E, C), dtype=jnp.float32)
        return {'x': x, 'W1': W1, 'b1': b1, 'Wg': Wg, 'bg': bg, 'Wd': Wd, 'bd': bd}
    _L1_ffn_all = _L1_ffn_setup()
    _L1_ffn_in = {k: v for k, v in _L1_ffn_all.items() if k in ('W1', 'b1', 'Wg', 'bg', 'Wd', 'bd')}
    del _L1_ffn_all
    return {'x': x, 'src': src, 'dst': dst, 'L0_gnn_W': _L0_gnn_in['W'], 'L0_gnn_envW': _L0_gnn_in['envW'], 'L0_gnn_envb': _L0_gnn_in['envb'], 'L0_ffn_W_fx': _L0_ffn_in['W_fx'], 'L0_ffn_b_fx': _L0_ffn_in['b_fx'], 'L0_ffn_W_x': _L0_ffn_in['W_x'], 'L0_ffn_b_x': _L0_ffn_in['b_x'], 'L0_ffn_W_slice': _L0_ffn_in['W_slice'], 'L0_ffn_b_slice': _L0_ffn_in['b_slice'], 'L0_ffn_W_q': _L0_ffn_in['W_q'], 'L0_ffn_W_k': _L0_ffn_in['W_k'], 'L0_ffn_W_v': _L0_ffn_in['W_v'], 'L0_ffn_W_out': _L0_ffn_in['W_out'], 'L0_ffn_b_out': _L0_ffn_in['b_out'], 'L0_ffn_temperature': _L0_ffn_in['temperature'], 'L1_gnn_W': _L1_gnn_in['W'], 'L1_gnn_a_src': _L1_gnn_in['a_src'], 'L1_gnn_a_dst': _L1_gnn_in['a_dst'], 'L1_ffn_W1': _L1_ffn_in['W1'], 'L1_ffn_b1': _L1_ffn_in['b1'], 'L1_ffn_Wg': _L1_ffn_in['Wg'], 'L1_ffn_bg': _L1_ffn_in['bg'], 'L1_ffn_Wd': _L1_ffn_in['Wd'], 'L1_ffn_bd': _L1_ffn_in['bd']}

def reference(x, src, dst, L0_gnn_W, L0_gnn_envW, L0_gnn_envb, L0_ffn_W_fx, L0_ffn_b_fx, L0_ffn_W_x, L0_ffn_b_x, L0_ffn_W_slice, L0_ffn_b_slice, L0_ffn_W_q, L0_ffn_W_k, L0_ffn_W_v, L0_ffn_W_out, L0_ffn_b_out, L0_ffn_temperature, L1_gnn_W, L1_gnn_a_src, L1_gnn_a_dst, L1_ffn_W1, L1_ffn_b1, L1_ffn_Wg, L1_ffn_bg, L1_ffn_Wd, L1_ffn_bd):
    import jax
    import jax.numpy as jnp

    def _L0_gnn_ref(x, edge_index, W, envW, envb):
        import jax, jax.numpy as jnp
        import numpy as np
        N, E, D, K, L = (6250, 200000, 256, 4, 2)
        TAU = 1.0

        def _scatter_mean(src, row, num_segments):
            sums = jax.ops.segment_sum(src, row, num_segments=num_segments)
            cnt = jax.ops.segment_sum(jnp.ones((src.shape[0],), dtype=src.dtype), row, num_segments=num_segments)
            return sums / jnp.maximum(cnt, 1.0)[:, None]
        row, col = (edge_index[0], edge_index[1])
        z = x
        for l in range(L):
            logits = z @ envW[l] + envb[l]
            weights = jax.nn.softmax(logits / TAU, axis=-1)
            agg = _scatter_mean(z[col], row, N)
            combined = jnp.concatenate([agg, z], axis=-1)
            outputs = jnp.einsum('nd,kdo->nko', combined, W[l]) + z[:, None, :]
            z = jnp.einsum('nk,nko->no', weights, outputs)
            z = jax.nn.relu(z)
        return z

    def _L0_ffn_ref(x, W_fx, b_fx, W_x, b_x, W_slice, b_slice, W_q, W_k, W_v, W_out, b_out, temperature):
        import jax, jax.numpy as jnp
        import numpy as np
        DIM = 256
        H = 8
        D = 64
        G = 64
        INNER = H * D
        SCALE = D ** (-0.5)
        B, N, _ = x.shape
        fx_mid = (x @ W_fx + b_fx).reshape(B, N, H, D).transpose(0, 2, 1, 3)
        x_mid = (x @ W_x + b_x).reshape(B, N, H, D).transpose(0, 2, 1, 3)
        temp = jnp.clip(temperature, 0.1, 5.0)
        slice_weights = jax.nn.softmax((x_mid @ W_slice + b_slice) / temp, axis=-1)
        slice_norm = slice_weights.sum(axis=2)
        slice_token = jnp.einsum('bhnc,bhng->bhgc', fx_mid, slice_weights)
        slice_token = slice_token / (slice_norm[..., None] + 1e-05)
        q = slice_token @ W_q
        k = slice_token @ W_k
        v = slice_token @ W_v
        attn = jax.nn.softmax(jnp.einsum('bhgc,bhkc->bhgk', q, k) * SCALE, axis=-1)
        out_slice = jnp.einsum('bhgk,bhkc->bhgc', attn, v)
        out_x = jnp.einsum('bhgc,bhng->bhnc', out_slice, slice_weights)
        out_x = out_x.transpose(0, 2, 1, 3).reshape(B, N, INNER)
        return out_x @ W_out + b_out

    def _L1_gnn_ref(x, edge_index, W, a_src, a_dst):
        import jax, jax.numpy as jnp
        import numpy as np
        NEG_SLOPE = 0.2
        EPS = 1e-08
        N, E, IN_F, OUT_F, H = (6250, 100000, 256, 32, 8)
        num_nodes = x.shape[0]
        src, dst = (edge_index[0], edge_index[1])
        h = jnp.einsum('ni,hif->hnf', x, W)
        s_src = jnp.einsum('hnf,hf->hn', h, a_src)
        s_dst = jnp.einsum('hnf,hf->hn', h, a_dst)
        ea = (s_src[:, src] + s_dst[:, dst]).T
        ea = jnp.where(ea > 0, ea, NEG_SLOPE * ea)
        m = jax.ops.segment_max(ea, dst, num_segments=num_nodes)
        ea = jnp.exp(ea - m[dst])
        s = jax.ops.segment_sum(ea, dst, num_segments=num_nodes)
        ea = ea / (s[dst] + EPS)
        hn = jnp.transpose(h, (1, 0, 2))
        wf = hn[src] * ea[:, :, None]
        out = jax.ops.segment_sum(wf, dst, num_segments=num_nodes)
        return out.reshape(num_nodes, -1)

    def _L1_ffn_ref(x, W1, b1, Wg, bg, Wd, bd):
        import jax, jax.numpy as jnp
        import numpy as np
        C = 256
        HID = 1024
        E = 8
        TEMP = 1.0
        orig_shape = x.shape
        xf = x.reshape(-1, orig_shape[-1])
        H = jax.nn.gelu(xf @ W1 + b1, approximate=False)
        probs = jax.nn.softmax((H @ Wg + bg) / TEMP, axis=-1)
        assign = jnp.argmax(probs, axis=-1)
        out = jnp.zeros_like(xf)
        for e in range(Wd.shape[0]):
            y = H @ Wd[e] + bd[e]
            sel = (assign == e)[:, None]
            out = out + jnp.where(sel, probs[:, e:e + 1] * y, 0.0)
        return out.reshape(orig_shape)
    edge_index = jnp.stack([src, dst])
    x = x + _L0_gnn_ref(_layernorm(x, axis=-1), edge_index, L0_gnn_W, L0_gnn_envW, L0_gnn_envb)
    x = x + _L0_ffn_ref(_layernorm(x, axis=-1)[None], L0_ffn_W_fx, L0_ffn_b_fx, L0_ffn_W_x, L0_ffn_b_x, L0_ffn_W_slice, L0_ffn_b_slice, L0_ffn_W_q, L0_ffn_W_k, L0_ffn_W_v, L0_ffn_W_out, L0_ffn_b_out, L0_ffn_temperature)[0]
    x = x + _L1_gnn_ref(_layernorm(x, axis=-1), edge_index, L1_gnn_W, L1_gnn_a_src, L1_gnn_a_dst)
    x = x + _L1_ffn_ref(_layernorm(x, axis=-1)[None], L1_ffn_W1, L1_ffn_b1, L1_ffn_Wg, L1_ffn_bg, L1_ffn_Wd, L1_ffn_bd)[0]
    return x

_drawn_inputs = setup_inputs


def setup_inputs(seed=0):
    import zlib

    import numpy as np

    out = dict(_drawn_inputs(seed))
    spreads = {'L0_ffn_b_fx': (0.0, 0.1),
     'L0_ffn_b_x': (0.0, 0.8),
     'L0_ffn_b_slice': (0.0, 0.8),
     'L0_ffn_b_out': (0.0, 0.1),
     'L0_ffn_temperature': (0.5, 0.6),
     'L1_ffn_b1': (0.0, 0.8),
     'L1_ffn_bg': (0.0, 0.599),
     'L1_ffn_bd': (0.0, 0.8)}
    factors = {'L0_gnn_envb': 4.227,
     'L0_ffn_W_x': 8.0,
     'L0_ffn_W_slice': 8.0,
     'L0_ffn_W_q': 8.0,
     'L0_ffn_W_k': 8.0,
     'L1_ffn_W1': 4.679,
     'L1_ffn_Wg': 4.705,
     'L1_ffn_Wd': 5.759}
    for name, (base, spread) in spreads.items():
        noise = np.random.default_rng([zlib.crc32(name.encode()), seed]).standard_normal(out[name].shape)
        drawn = base * np.exp(spread * noise) if base else spread * noise
        out[name] = jnp.asarray(drawn.astype(out[name].dtype))
    for name, factor in factors.items():
        out[name] = (out[name] * factor).astype(out[name].dtype)
    return out
```

```python
import concourse.bass as bass
from concourse import mybir
from concourse.alu_op_type import AluOpType as ALU
from contextlib import ExitStack

ACT = mybir.ActivationFunctionType
AX = mybir.AxisListType
F32 = mybir.dt.float32
BF16 = mybir.dt.bfloat16
U16 = mybir.dt.uint16
I32 = mybir.dt.int32
U32 = mybir.dt.uint32

P = 128
N = 6250
D = 256
E = 100000
NT = 50
NFULL = N // P
NREST = N - NFULL * P
LASTT = NFULL
COLS = 784
EPAD = P * COLS
EREST = E - (P - 1) * COLS
PADKEY = 49 * P
STEPS = 832
GROUPS = 7
SG = GROUPS * P
K0 = 4
HALF = 8
FAR = 1e30
ds = bass.ds


class Chain:

    def __init__(self, eng, sem, at=0):
        self.eng, self.sem, self.at, self.n = eng, sem, at, 0

    def step(self, ins):
        ins.then_inc(self.sem, 1)
        self.n += 1
        return ins

    def wait(self):
        self.eng.wait_ge(self.sem, self.at + self.n)

    def link(self, ins):
        self.step(ins)
        self.wait()
        return ins

    def enter(self, at):
        self.at, self.n = at, 0


def build(nc, out, *, x, src, dst, L0_gnn_W, L0_gnn_envW, L0_gnn_envb, L0_ffn_W_fx, L0_ffn_b_fx, L0_ffn_W_x,
          L0_ffn_b_x, L0_ffn_W_slice, L0_ffn_b_slice, L0_ffn_W_q, L0_ffn_W_k, L0_ffn_W_v, L0_ffn_W_out,
          L0_ffn_b_out, L0_ffn_temperature, L1_gnn_W, L1_gnn_a_src, L1_gnn_a_dst, L1_ffn_W1, L1_ffn_b1,
          L1_ffn_Wg, L1_ffn_bg, L1_ffn_Wd, L1_ffn_bd):
    with ExitStack() as top:
        stage_sems = []

        def sem(name):
            stage_sems.append(nc.alloc_semaphore(name=name))
            return stage_sems[-1]

        def stage_ends():
            nc.clear_and_free_semaphores(stage_sems)
            stage_sems.clear()
            nc.all_engine_barrier()

        def sb(name, shape, dt=F32, ctx=top):
            return ctx.enter_context(nc.sbuf_tensor(name, shape, dt))

        z_rows = [nc.dram_tensor(f"z_rows{l}", [NT * P, D], F32) for l in range(2)]
        pairs = [nc.dram_tensor(f"pairs_{q}", [EPAD, 2], I32) for q in ("src", "dst")]
        tile_of_step_dram = nc.dram_tensor("tile_of_step_dram", [2, SG], I32)

        key_by_dst = nc.dram_tensor("key_by_dst", [P, SG], F32)
        row_by_dst = nc.dram_tensor("row_by_dst", [P, SG], U32)

        last_by_dst = nc.dram_tensor("last_by_dst", [P, SG], F32)
        cuts_dram = nc.dram_tensor("cuts_dram", [SG, 2 * P], F32)

        X = sb("X", [P, NT, D])
        iota_row = sb("iota_row", [P, P])
        iota_part = sb("iota_part", [P, 1])
        step_index = sb("step_index", [P, GROUPS])
        ident = sb("ident", [P, P])
        before = sb("before", [P, P])
        ones = sb("ones", [P, P])
        eps_ln = sb("eps_ln", [P, 1])
        ps = [top.enter_context(nc.psum_tensor(f"bank{b}", [P, 512], F32)) for b in range(8)]

        g = dict(locals())
        constants(g)
        graph_mixture(g)
        stage_ends()
        with ExitStack() as c:
            slice_attention(g, c)
        stage_ends()
        with ExitStack() as c:
            graph_attention(g, c)
        stage_ends()
        with ExitStack() as c:
            routed_network(g, c, out)


def graph_mixture(g):
    nc, sb = g["nc"], g["sb"]
    with ExitStack() as c1:
        g["local_key"] = sb("local_key", [P, SG], ctx=c1)
        g["row_of"] = sb("row_of", [P, SG], U32, c1)
        g["tile_of"] = sb("tile_of", [1, SG], I32, c1)
        g["Z"] = sb("Z", [P, NT, D], ctx=c1)
        g["mix"] = sb("mix", [P, NT, K0], ctx=c1)
        with ExitStack() as c2:
            edge_tables(g, c2)
        with ExitStack() as c3:
            g["A"] = sb("A", [P, NT, D + 1], ctx=c3)
            for layer in range(2):
                if layer == 1:
                    with ExitStack() as c4:
                        run_block(nc, mixture(g, c4, layer, "own"))
                with ExitStack() as c4:
                    run_block(nc, gather_sum(g, c4, layer))
                with ExitStack() as c4:
                    run_block(nc, mixture(g, c4, layer, "agg"))


def constants(g):
    nc, X, sem, sb = g["nc"], g["X"], g["sem"], g["sb"]
    x_loaded, const_made, iota_made, own = (sem(n) for n in ("x_loaded", "const_made", "iota_made", "const_own"))
    with ExitStack() as c:
        irow = sb("irow", [P, P], I32, c)
        ipart = sb("ipart", [P, 1], I32, c)
        istep = sb("istep", [P, GROUPS], I32, c)
        block = c.enter_context(nc.Block())

        @block.gpsimd
        def _(pool):
            nc.gpsimd.iota(irow[:, :], [[1, P]], base=0, channel_multiplier=0).then_inc(iota_made, 1)
            nc.gpsimd.iota(ipart[:, :], [[0, 1]], base=0, channel_multiplier=1).then_inc(iota_made, 1)
            nc.gpsimd.iota(istep[:, :], [[P, GROUPS]], base=0, channel_multiplier=1).then_inc(iota_made, 1)

        @block.vector
        def _(dve):
            ch = Chain(dve, own)
            dve.memset(X[:, LASTT:NT, :], 0.0).then_inc(const_made, 1)
            dve.memset(g["ones"][:, :], 1.0)
            dve.memset(g["eps_ln"][:, :], 1e-5)
            dve.wait_ge(iota_made, 3)
            ch.step(dve.tensor_copy(g["iota_row"][:, :], irow[:, :]))
            ch.step(dve.tensor_copy(g["iota_part"][:, :], ipart[:, :]))
            dve.tensor_copy(g["step_index"][:, :], istep[:, :])
            ch.wait()
            dve.tensor_scalar(g["ident"][:, :], g["iota_row"][:, :], g["iota_part"][:, 0:1], None, ALU.is_equal)
            dve.tensor_scalar(g["before"][:, :], g["iota_row"][:, :], g["iota_part"][:, 0:1], None, ALU.is_gt)

        @block.sync
        def _(sp):
            sp.dma_start(X[:, 0:NFULL, :], g["x"][0:NFULL * P, :].rearrange("(t p) d -> p t d", p=P)).then_inc(x_loaded, 16)
            sp.wait_ge(const_made, 1)
            sp.dma_start(X[0:NREST, LASTT, :], g["x"][NFULL * P:N, :]).then_inc(x_loaded, 16)
            sp.wait_ge(x_loaded, 32)


def edge_tables(g, c):
    nc, sb, sem, ps, X = g["nc"], g["sb"], g["sem"], g["ps"], g["X"]
    ones, before, ident, iota_row = g["ones"], g["before"], g["ident"], g["iota_row"]
    keys = [sb(f"keys{q}", [P, COLS], I32, c) for q in range(2)]
    bucket_i = sb("bucket_i", [P, COLS], I32, c)
    bucket = [sb(f"bucket{q}", [P, COLS], BF16, c) for q in range(2)]
    mask = sb("mask", [P, 2, COLS], U16, c)
    rank = sb("rank", [P, 2, COLS], F32, c)
    pos = sb("pos", [P, COLS], F32, c)
    pos_u = sb("pos_u", [P, COLS], U32, c)
    pay = [sb(f"pay{q}", [P, COLS, 2], I32, c) for q in range(2)]
    count = sb("count", [P, 2, NT], F32, c)
    total = sb("total", [P, 2, NT], F32, c)
    upto_b = sb("upto_b", [P, 2, NT], F32, c)
    first = sb("first", [P, 2, NT], F32, c)
    base = sb("base", [P, NT], F32, c)
    first_i = sb("first_i", [P, 2, NT], I32, c)
    border = sb("border", [P, 2, NT], F32, c)
    ring_pos = sb("ring_pos", [P, 2, HALF], U32, c)
    ring_pay = sb("ring_pay", [P, 2, HALF, 2], I32, c)
    stats = sb("stats", [P, NT, 6], F32, c)
    edges_loaded, cleared, counted, totals_ready, pos_ready, pay_ready, own, pool_own = (
        sem(n) for n in ("edges_loaded", "cleared", "counted", "totals_ready", "pos_ready", "pay_ready", "tab_own",
                         "tab_pool_own"))
    scattered = [sem(f"scattered{h}") for h in range(2)]
    pool_passed = sem("tab_pool_passed")
    dst_stored = sem("dst_stored")
    per_half = COLS // (2 * HALF)

    mix0 = mixture(g, c, 0, "own")
    with nc.Block() as block:
        @block.scalar
        def _(act):
            mix0["scalar"](act)

        @block.sync
        def _(sp):
            sp.wait_ge(cleared, 2)
            for q, a in enumerate((g["src"], g["dst"])):
                sp.dma_start(keys[q][0:P - 1, :], a[0:(P - 1) * COLS].rearrange("(p j) -> p j", j=COLS)).then_inc(edges_loaded, 16)
                sp.dma_start(keys[q][P - 1:P, 0:EREST], a[(P - 1) * COLS:E].rearrange("(p j) -> p j", p=1)).then_inc(edges_loaded, 16)
            sp.wait_ge(pay_ready, 4)
            sp.dma_start(g["pairs"][1][:, :].rearrange("(p j) w -> p (j w)", p=P), pay[1][:, :, :].rearrange("p j w -> p (j w)")).then_inc(dst_stored, 16)
            mix0["sync"](sp)
            sp.wait_ge(dst_stored, 16)

        @block.vector
        def _(dve):
            ch = Chain(dve, own)
            for q in range(2):
                dve.memset(keys[q][:, :], PADKEY).then_inc(cleared, 1)
            dve.memset(pos[:, :], 0.0)
            dve.wait_ge(edges_loaded, 64)
            for q in range(2):
                ch.link(dve.tensor_scalar(bucket_i[:, :], keys[q][:, :], 7, None, ALU.logical_shift_right))
                ch.link(dve.tensor_copy(bucket[q][:, :], bucket_i[:, :]))
            for b in rounds_of(dve, NT):
                for q in range(2):
                    wait_from(dve, counted, b * 2 + q)
                    dve.tensor_scalar(mask[:, q, :], bucket[q][:, :], iota_row[:, ds(b, 1)], 0.0, ALU.is_equal, ALU.add,
                                      accum_out=count[:, q, ds(b, 1)]).then_inc(counted, 1)
            dve.wait_ge(totals_ready, 1)
            for q in range(2):
                ch.step(dve.tensor_copy(total[:, q, :], ps[0][:, q * NT:(q + 1) * NT]))
            ch.wait()
            for q in range(2):
                ch.step(dve.tensor_tensor_scan(upto_b[:, q, :], total[:, q, :], total[:, q, :], 0.0, ALU.add, ALU.bypass))
            ch.wait()
            ch.link(dve.tensor_tensor(first[:, :, :], upto_b[:, :, :], total[:, :, :], ALU.subtract))
            ch.link(dve.scalar_tensor_tensor(out=base[:, :], in0=ps[1][:, 0:NT], scalar=-1.0, in1=first[:, 0, :], op0=ALU.add, op1=ALU.add))
            per_b, start = 4, ch.n
            with dve.Fori(0, NT) as b:
                ch.enter(b * per_b + start)
                ch.link(dve.tensor_scalar(mask[:, 0, :], bucket[0][:, :], iota_row[:, ds(b, 1)], None, ALU.is_equal))
                ch.link(dve.tensor_tensor_scan(rank[:, 0, :], mask[:, 0, :], mask[:, 0, :], base[:, ds(b, 1)], ALU.add, ALU.bypass))
                ch.link(dve.tensor_tensor(rank[:, 0, :], rank[:, 0, :], mask[:, 0, :], ALU.mult))
                ch.link(dve.tensor_tensor(pos[:, :], pos[:, :], rank[:, 0, :], ALU.add))
            ch.enter(NT * per_b + start)
            for q in range(2):
                for w in range(2):
                    dve.tensor_copy(pay[q][:, :, w], keys[(q + w) % 2][:, :]).then_inc(pay_ready, 1)
            dve.tensor_copy(pos_u[:, :], pos[:, :]).then_inc(pos_ready, 1)
            ch.link(dve.tensor_copy(first_i[:, :, :], first[:, :, :]))
            ch.link(dve.tensor_scalar(first_i[:, :, :], first_i[:, :, :], 7, None, ALU.logical_shift_right))
            ch.link(dve.tensor_copy(border[:, :, :], first_i[:, :, :]))
            for q in range(2):
                ch.link(dve.tensor_tensor(border[:, q, :], border[:, q, :], iota_row[:, 0:NT], ALU.add))
            mix0["vector"](dve)

        @block.tensor
        def _(pe):
            pe.wait_ge(counted, 2 * NT)
            pe.matmul(ps[0][:, 0:2 * NT], ones[:, :], count[:, :, :].rearrange("p q b -> p (q b)"), start=True, stop=True)
            pe.matmul(ps[1][:, 0:NT], before[:, :], count[:, 0, :], start=True, stop=True).then_inc(totals_ready, 1)
            mix0["tensor"](pe)

        @block.gpsimd
        def _(pool):
            pool.wait_ge(pos_ready, 1)
            pool.wait_ge(pay_ready, 2)
            for i in rounds_of(pool, per_half):
                for h in range(2):
                    j = i * (2 * HALF) + h * HALF
                    wait_apart(pool, scattered[h], i * (16 * HALF), pool_passed)
                    pool.tensor_copy(ring_pos[:, h, :], pos_u[:, ds(j, HALF)]).then_inc(pool_own, 1)
                    pool.tensor_copy(ring_pay[:, h, :, :], pay[0][:, ds(j, HALF), :]).then_inc(pool_own, 1)
                    wait_apart(pool, pool_own, i * 4 + 2 * h + 2, pool_passed)
                    for k in range(HALF):
                        pool.indirect_dma_start(
                            out=g["pairs"][0][:, :], out_offset=bass.IndirectOffsetOnAxis(ap=ring_pos[:, h, k:k + 1], axis=0),
                            in_=ring_pay[:, h, k, :], in_offset=None).then_inc(scattered[h], 16)
            for h in range(2):
                pool.wait_ge(scattered[h], per_half * 16 * HALF)

    local_key = [g["local_key"], sb("local_key1", [P, SG], F32, c)]
    row_of = [g["row_of"], sb("row_of1", [P, SG], U32, c)]
    tile_f = sb("tile_f", [P, 2, GROUPS], F32, c)
    tile_i = sb("tile_i", [2 * GROUPS, P], I32, c)
    tile_key = sb("tile_key", [P, 2, GROUPS], F32, c)
    chunk_f = sb("chunk_f", [P, 2, GROUPS], F32, c)
    chunk_u = sb("chunk_u", [P, 2 * GROUPS], U32, c)
    scratch = sb("scratch", [P, NT], F32, c)
    rows = sb("rows", [P, 4, P, 2], I32, c)
    rows_f = sb("rows_f", [P, 2, 2, P], F32, c)
    last = sb("last", [P, SG], F32, c)
    cuts = sb("cuts", [P, GROUPS, 2, P], F32, c)
    cuts_made, last_turned, cuts_ready = (sem(n) for n in ("cuts_made", "last_turned", "cuts_ready"))
    chunk_ready, rows_loaded, rows_used, rows_made, turned, taken, own2, tiles_out, tiles_in = (
        sem(n) for n in ("chunk_ready", "rows_loaded", "rows_used", "rows_made", "turned", "taken", "tab_own2",
                         "tiles_out", "tiles_in"))
    tiles_turned = sem("tiles_turned")
    rows_at = [sem(f"rows_at{k}") for k in range(4)]
    n2 = 2 * GROUPS
    with nc.Block() as block:
        @block.gpsimd
        def _(pool):
            pool.wait_ge(chunk_ready, 1)
            for k in range(n2):
                q = k // GROUPS
                if k >= 4:
                    pool.wait_ge(rows_used, k - 3)
                pool.indirect_dma_start(
                    out=rows[:, k % 4, :, :].rearrange("p e w -> p (e w)"), out_offset=None,
                    in_=g["pairs"][q][:, :].rearrange("(c e) w -> c (e w)", e=P),
                    in_offset=bass.IndirectOffsetOnAxis(ap=chunk_u[:, k:k + 1], axis=0)).then_inc(rows_at[k % 4], 16)

        @block.vector
        def _(dve):
            ch = Chain(dve, own2)
            ch.link(dve.memset(cuts[:, :, :, :], 1.0))
            for q in range(2):
                for s in range(GROUPS):
                    ch.link(dve.tensor_scalar(scratch[:, 0:48], border[:, q, 1:49], g["step_index"][:, s:s + 1], 0.0, ALU.is_le,
                                              ALU.add, accum_out=tile_f[:, q, s:s + 1]))
            for q in range(2):
                ch.link(dve.tensor_tensor(chunk_f[:, q, :], g["step_index"][:, :], tile_f[:, q, :], ALU.subtract))
            ch.link(dve.tensor_scalar_min(chunk_f[:, :, :], chunk_f[:, :, :], float(COLS - 1)))
            dve.tensor_copy(chunk_u[:, :], chunk_f[:, :, :].rearrange("p q s -> p (q s)")).then_inc(chunk_ready, 1)
            dve.wait_ge(tiles_turned, 1)
            dve.tensor_copy(tile_i[:, :], ps[4][0:n2, 0:P]).then_inc(chunk_ready, 1)
            ch.link(dve.tensor_scalar(tile_key[:, :, :], tile_f[:, :, :], float(P), None, ALU.mult))
            for k in range(n2):
                q, s = k // GROUPS, k % GROUPS
                dve.wait_ge(rows_at[k % 4], 16 * (k // 4 + 1))
                if k >= 2:
                    dve.wait_ge(turned, k - 1)
                dve.tensor_scalar(rows_f[:, k % 2, 0, :], rows[:, k % 4, :, 0], tile_key[:, q, s:s + 1], None,
                                  ALU.subtract).then_inc(rows_made, 1)
                dve.tensor_copy(rows_f[:, k % 2, 1, :], rows[:, k % 4, :, 1]).then_inc(rows_made, 1)
                dve.wait_ge(rows_made, 2 * k + 2)
                dve.sem_inc(rows_used, 1)
                if q == 1:
                    here, before_ = rows_f[:, k % 2, 0, 1:P], rows_f[:, k % 2, 0, 0:P - 1]
                    dve.tensor_tensor(cuts[:, s, 0, 1:P], here, before_, ALU.not_equal).then_inc(cuts_made, 1)
                    dve.tensor_tensor(cuts[:, s, 1, 0:P - 1], here, before_, ALU.not_equal).then_inc(cuts_made, 1)
                    wait_from(dve, last_turned, s + 1)
                    ch.step(dve.tensor_copy(last[:, s * P:(s + 1) * P], ps[5][:, 0:P]))
                dve.wait_ge(turned, k + 1)
                dve.tensor_copy(local_key[q][:, s * P:(s + 1) * P], ps[2 * (k % 2)][:, 0:P])
                dve.tensor_copy(row_of[q][:, s * P:(s + 1) * P], ps[2 * (k % 2) + 1][:, 0:P]).then_inc(taken, 1)
            ch.wait()
            dve.wait_ge(cuts_made, 2 * GROUPS)
            dve.tensor_scalar(cuts[:, :, :, :], cuts[:, :, :, :], -FAR, None, ALU.mult).then_inc(cuts_ready, 1)

        @block.tensor
        def _(pe):
            pe.wait_ge(chunk_ready, 1)
            pe.transpose(ps[4][0:n2, 0:P], tile_f[:, :, :].rearrange("p q s -> p (q s)"), ident[:, :]).then_inc(tiles_turned, 1)
            for k in range(n2):
                pe.wait_ge(rows_made, 2 * k + 2)
                if k >= 2:
                    pe.wait_ge(taken, k - 1)
                pe.transpose(ps[2 * (k % 2)][:, 0:P], rows_f[:, k % 2, 0, :], ident[:, :])
                pe.transpose(ps[2 * (k % 2) + 1][:, 0:P], rows_f[:, k % 2, 1, :], ident[:, :]).then_inc(turned, 1)
                if k >= GROUPS:
                    pe.wait_ge(cuts_made, 2 * (k - GROUPS) + 2)
                    pe.wait_ge(taken, k)
                    pe.transpose(ps[5][:, 0:P], cuts[:, k - GROUPS, 1, :], ident[:, :]).then_inc(last_turned, 1)

        @block.sync
        def _(sp):
            sp.wait_ge(chunk_ready, 2)
            sp.dma_start(g["tile_of_step_dram"][:, :].rearrange("q (s p) -> (q s) p", p=P), tile_i[:, :]).then_inc(tiles_out, 16)
            sp.wait_ge(tiles_out, 16)
            sp.dma_start(g["tile_of"][:, :], g["tile_of_step_dram"][0:1, :]).then_inc(tiles_in, 16)
            sp.wait_ge(taken, n2)
            sp.dma_start(g["key_by_dst"][:, :], local_key[1][:, :]).then_inc(tiles_in, 16)
            sp.dma_start(g["row_by_dst"][:, :], row_of[1][:, :]).then_inc(tiles_in, 16)
            sp.wait_ge(cuts_ready, 1)
            sp.dma_start(g["last_by_dst"][:, :], last[:, :]).then_inc(tiles_in, 16)
            sp.dma_start(g["cuts_dram"][:, :].rearrange("(s p) w -> p s w", p=P),
                         cuts[:, :, :, :].rearrange("p s a e -> p s (a e)")).then_inc(tiles_in, 16)
            sp.wait_ge(tiles_in, 80)


def row_norm(g, c, name):
    nc, sb, sem, X = g["nc"], g["sb"], g["sem"], g["X"]
    stats = sb(name + "_stats", [P, NT, 6], F32, c)
    mean = sb(name + "_mean", [P, NT], F32, c)
    var = sb(name + "_var", [P, NT], F32, c)
    apart = sb(name + "_apart", [P, NT], F32, c)
    rstd = sb(name + "_rstd", [P, NT], F32, c)
    own, var_ready, std_ready = (sem(name + n) for n in ("_own", "_var_ready", "_std_ready"))

    def vector(dve):
        ch = Chain(dve, own)
        with dve.Fori(0, NT // 2) as i:
            for u in range(2):
                t = i * 2 + u
                dve.bn_stats(row(stats, t), row(X, t)).then_inc(own, 1)
        ch.enter(NT)
        ch.wait()
        ch.step(dve.tensor_tensor(mean[:, :], stats[:, :, 1], stats[:, :, 4], ALU.add))
        ch.step(dve.tensor_tensor(apart[:, :], stats[:, :, 1], stats[:, :, 4], ALU.subtract))
        ch.link(dve.tensor_tensor(var[:, :], stats[:, :, 2], stats[:, :, 5], ALU.add))
        ch.link(dve.tensor_scalar(mean[:, :], mean[:, :], 0.5, None, ALU.mult))
        ch.link(dve.tensor_tensor(apart[:, :], apart[:, :], apart[:, :], ALU.mult))
        ch.link(dve.tensor_scalar(apart[:, :], apart[:, :], 0.25, None, ALU.mult))
        dve.scalar_tensor_tensor(out=var[:, :], in0=var[:, :], scalar=1.0 / D, in1=apart[:, :], op0=ALU.mult, op1=ALU.add).then_inc(var_ready, 1)
        dve.wait_ge(std_ready, 1)
        ch.link(dve.reciprocal(rstd[:, :], rstd[:, :]))

    def scalar(act):
        act.wait_ge(var_ready, 1)
        act.activation(rstd[:, :], var[:, :], ACT.Sqrt, bias=g["eps_ln"][:, 0:1]).then_inc(std_ready, 1)

    return mean, rstd, vector, scalar


def rounds_of(eng, count):
    yield 0
    with eng.Fori(1, count) as i:
        yield i


def over_tiles(eng, ahead, now):
    ahead(0, 0, 0)
    for i in rounds_of(eng, NT // 2 - 1):
        ahead(i * 2 + 1, 1, i)
        now(i * 2, 0, i)
        ahead(i * 2 + 2, 0, i + 1)
        now(i * 2 + 1, 1, i)
    ahead(NT - 1, 1, NT // 2 - 1)
    now(NT - 2, 0, NT // 2 - 1)
    now(NT - 1, 1, NT // 2 - 1)


def wait_from(eng, sem, value):
    if not isinstance(value, int) or value > 0:
        eng.wait_ge(sem, value)


def wait_apart(eng, sem, value, passed):
    if isinstance(value, int) and value <= 0:
        return
    eng.wait_ge(sem, value)
    eng.sem_inc(passed, 1)


def row(a, t):
    return a[:, ds(t, 1), :].rearrange("p a d -> p (a d)")


def mixture(g, c, layer, part):
    nc, sb, sem, ps, X, Z, mix = (g[n] for n in ("nc", "sb", "sem", "ps", "X", "Z", "mix"))
    ident = g["ident"]
    own_part = part == "own"
    pre = f"{part}{layer}_"
    W0 = sb(pre + "W", [P, 2, K0, D], F32, c)
    stage = sb(pre + "stage", [P, 2, D], F32, c)
    zT = sb(pre + "zT", [P, 2, 2, P], F32, c)
    names = ("dve_ahead", "dve_now", "staged", "turned", "zt_ready", "products", "exp_in", "exp_out", "mixed", "w_loaded",
             "act_own")
    dve_ahead, dve_now, staged, turned, zt_ready, products, exp_in, exp_out, mixed, w_loaded, act_own = (
        sem(pre + n) for n in names)
    stored = [sem(pre + f"stored{u}") for u in range(2)]
    store_stage = own_part and layer == 0
    store_new = not own_part and layer == 0
    z_new = sb(pre + "z_new", [P, 2, D], F32, c) if not own_part else None
    new_ready = sem(pre + "new_ready")
    if own_part:
        envw = sb(pre + "envw", [P, 2, K0], F32, c)
        envb = sb(pre + "envb", [P, K0], F32, c)
        lg = sb(pre + "lg", [P, 2, K0], F32, c)
        ex = sb(pre + "ex", [P, 2, K0], F32, c)
        col = sb(pre + "col", [P, 2, 4], F32, c)
    if store_stage:
        mean, rstd, norm_vector, norm_scalar = row_norm(g, c, "ln0")
    if not own_part:
        per_count = sb(pre + "per_count", [P, NT], F32, c)
    first_chunk = 2 if own_part else 0

    def sync(sp):
        for k in range(K0):
            sp.dma_start(W0[:, :, k, :], g["L0_gnn_W"][layer, k].rearrange("(c p) d -> p c d", p=P)[:, first_chunk:first_chunk + 2, :]).then_inc(w_loaded, 16)
        if own_part:
            sp.dma_start(envw[:, :, :], g["L0_gnn_envW"][layer].rearrange("(c p) k -> p c k", p=P)).then_inc(w_loaded, 16)
            sp.dma_start(envb[:, :], g["L0_gnn_envb"][layer:layer + 1, :].broadcast_to([P, K0])).then_inc(w_loaded, 16)
        if store_stage or store_new:
            ready, what = (staged, stage) if store_stage else (new_ready, z_new)
            with sp.Fori(0, NT // 2) as i:
                for u in range(2):
                    wait_from(sp, ready, i * 2 + u + 1)
                    sp.dma_start(g["z_rows"][layer if store_stage else 1][ds((i * 2 + u) * P, P), :], what[:, u, :]).then_inc(stored[u], 16)
            for u in range(2):
                sp.wait_ge(stored[u], 16 * (NT // 2))

    def vector(dve):
        cha, chn = Chain(dve, dve_ahead), Chain(dve, dve_now)
        if store_stage:
            norm_vector(dve)
        if not own_part:
            cha.link(dve.tensor_scalar_max(per_count[:, :], g["A"][:, :, D], 1.0))
            cha.link(dve.reciprocal(per_count[:, :], per_count[:, :]))
        if own_part:
            dve.wait_ge(w_loaded, 16 * (K0 + 2))

        dve.sem_inc(mixed, 1)

        def ahead(t, u, pair):
            wait_from(dve, turned, t - 1)
            if store_stage:
                wait_from(dve, stored[u], pair * 16)
                dve.tensor_scalar(stage[:, u, :], row(X, t), mean[:, ds(t, 1)], rstd[:, ds(t, 1)], ALU.subtract,
                                  ALU.mult).then_inc(staged, 1)
            elif own_part:
                dve.tensor_scalar(stage[:, u, :], row(Z, t), 1.0, None, ALU.mult).then_inc(staged, 1)
            else:
                dve.tensor_scalar(stage[:, u, :], g["A"][:, ds(t, 1), 0:D].rearrange("p a d -> p (a d)"),
                                  per_count[:, ds(t, 1)], None, ALU.mult).then_inc(staged, 1)

        def now(t, u, pair):
            z = row(Z, t)
            wait_from(dve, products, t + 1)
            if own_part:
                chn.enter(t * 9)
                chn.link(dve.tensor_tensor(lg[:, u, :], ps[6 + u][:, 0:K0], envb[:, :], ALU.add))
                dve.tensor_reduce(col[:, u, 0:1], lg[:, u, :], AX.X, ALU.max, negate=True).then_inc(exp_in, 1)
                wait_from(dve, exp_out, t + 1)
                chn.link(dve.reciprocal(col[:, u, 2:3], col[:, u, 1:2]))
                chn.link(dve.tensor_scalar(ex[:, u, :], ex[:, u, :], col[:, u, 2:3], None, ALU.mult))
                chn.step(dve.tensor_scalar(row(mix, t), ex[:, u, :], 1.0, None, ALU.mult))
                chn.link(dve.tensor_reduce(col[:, u, 3:4], ex[:, u, :], AX.X, ALU.add))
                chn.link(dve.tensor_scalar(z, stage[:, u, :], col[:, u, 3:4], None, ALU.mult))
            else:
                chn.enter(t * 5)
            for k in range(K0):
                ins = dve.scalar_tensor_tensor(out=z, in0=ps[2 * u + k // 2][:, (k % 2) * D:(k % 2 + 1) * D],
                                               scalar=mix[:, ds(t, 1), k:k + 1].rearrange("p a k -> p (a k)"), in1=z,
                                               op0=ALU.mult, op1=ALU.add)
                if k == K0 - 1 and own_part:
                    ins.then_inc(mixed, 1)
                else:
                    chn.link(ins)
            if not own_part:
                if layer == 0:
                    wait_from(dve, stored[u], pair * 16)
                    dve.tensor_scalar_max(z_new[:, u, :], z, 0.0).then_inc(new_ready, 1)
                    chn.link(dve.tensor_scalar_max(z, z, 0.0))
                else:
                    chn.link(dve.scalar_tensor_tensor(out=row(X, t), in0=z, scalar=0.0, in1=row(X, t), op0=ALU.max, op1=ALU.add))
                dve.sem_inc(mixed, 1)

        over_tiles(dve, ahead, now)

    def scalar(act):
        if store_stage:
            norm_scalar(act)

        def ahead(t, u, pair):
            wait_from(act, turned, t + 1)
            act.copy(zT[:, u, :, :].rearrange("p k n -> p (k n)"), ps[4 + u][:, 0:2 * P]).then_inc(zt_ready, 1)

        def now(t, u, pair):
            if own_part:
                wait_from(act, exp_in, t + 1)
                act.activation(ex[:, u, :], lg[:, u, :], ACT.Exp, bias=col[:, u, 0:1], accum_out=col[:, u, 1:2]).then_inc(exp_out, 1)

        over_tiles(act, ahead, now)

    def tensor(pe):
        pe.wait_ge(w_loaded, 16 * (K0 + 2 * own_part))

        def ahead(t, u, pair):
            wait_from(pe, staged, t + 1)
            for k in range(2):
                mm = pe.transpose(ps[4 + u][:, k * P:(k + 1) * P], stage[:, u, k * P:(k + 1) * P], ident[:, :])
            mm.then_inc(turned, 1)

        def now(t, u, pair):
            wait_from(pe, zt_ready, t + 1)
            wait_from(pe, mixed, t)
            for k in range(2):
                for h in range(2):
                    mm = pe.matmul(ps[2 * u + h][:, :], zT[:, u, k, :],
                                   W0[:, k, 2 * h:2 * h + 2, :].rearrange("p k d -> p (k d)"),
                                   start=(k == 0), stop=(k == 1))
            if own_part:
                for k in range(2):
                    mm = pe.matmul(ps[6 + u][:, 0:K0], zT[:, u, k, :], envw[:, k, :], start=(k == 0), stop=(k == 1))
            mm.then_inc(products, 1)

        over_tiles(pe, ahead, now)

    return {"sync": sync, "vector": vector, "scalar": scalar, "tensor": tensor}


def run_block(nc, programs):
    with nc.Block() as block:
        if "sync" in programs:
            @block.sync
            def _(sp):
                programs["sync"](sp)

        if "vector" in programs:
            @block.vector
            def _(dve):
                programs["vector"](dve)

        if "scalar" in programs:
            @block.scalar
            def _(act):
                programs["scalar"](act)

        if "tensor" in programs:
            @block.tensor
            def _(pe):
                programs["tensor"](pe)

        if "gpsimd" in programs:
            @block.gpsimd
            def _(pool):
                programs["gpsimd"](pool)


def gather_sum(g, c, layer):
    nc, sb, sem, ps, A = g["nc"], g["sb"], g["sem"], g["ps"], g["A"]
    pre = f"sum{layer}_"
    ring_rows = sb(pre + "rows", [P, 2 * HALF, D + 1], F32, c)
    ring_index = sb(pre + "index", [P, 2, HALF], U32, c)
    place = sb(pre + "place", [P, 2, HALF, P], F32, c)
    indexed, placed, summed, cleared, dve_own = (
        sem(pre + n) for n in ("indexed", "placed", "summed", "cleared", "dve_own"))
    fetched = [sem(pre + f"fetched{h}") for h in range(2)]
    rounds = STEPS // (2 * HALF)
    pool_passed = sem(pre + "pool_passed")

    def gpsimd(pool):
        pool.wait_ge(cleared, 1)
        for i in rounds_of(pool, rounds):
            for h in range(2):
                wait_apart(pool, fetched[h], i * (16 * HALF), pool_passed)
                pool.tensor_copy(ring_index[:, h, :], g["row_of"][:, ds((i * 2 + h) * HALF, HALF)]).then_inc(indexed, 1)
                wait_apart(pool, indexed, i * 2 + h + 1, pool_passed)
                for k in range(HALF):
                    wait_apart(pool, summed, (i * 2 + h) * HALF + k + 1, pool_passed)
                    pool.indirect_dma_start(
                        out=ring_rows[:, h * HALF + k, 0:D], out_offset=None, in_=g["z_rows"][layer][:, :],
                        in_offset=bass.IndirectOffsetOnAxis(ap=ring_index[:, h, k:k + 1], axis=0)).then_inc(fetched[h], 16)

    def vector(dve):
        ch = Chain(dve, dve_own)
        dve.memset(ring_rows[:, :, D:D + 1], 1.0)
        dve.memset(A[:, :, :], 0.0).then_inc(cleared, 1)
        dve.wait_ge(cleared, 1)

        def places(half, h):
            wait_from(dve, summed, half * HALF + HALF)
            key = g["local_key"][:, ds(half * HALF, HALF)]
            dve.tensor_tensor(place[:, h, :, :], g["iota_row"][:, :].unsqueeze(1).broadcast_to([P, HALF, P]),
                              key.unsqueeze(2).broadcast_to([P, HALF, P]), ALU.is_equal).then_inc(placed, 1)

        dve.sem_inc(dve_own, HALF)
        places(0, 0)
        for i in rounds_of(dve, rounds):
            for h in range(2):
                places(i * 2 + h + 1, 1 - h)
                ch.enter((i * 2 + h) * HALF + HALF)
                for k in range(HALF):
                    s = (i * 2 + h) * HALF + k
                    t = dve.value_load(g["tile_of"][0:1, ds(s, 1)], min_val=0, max_val=NT - 1)
                    here = row(A, t)
                    wait_from(dve, summed, s + 1 + 2 * HALF)
                    ch.wait()
                    ch.step(dve.tensor_tensor(here, ps[k][:, 0:D + 1], here, ALU.add))

    def tensor(pe):
        pe.sem_inc(summed, 2 * HALF)
        for i in rounds_of(pe, rounds):
            for h in range(2):
                wait_from(pe, fetched[h], (i + 1) * (16 * HALF))
                wait_from(pe, placed, i * 2 + h + 1)
                for k in range(HALF):
                    s = (i * 2 + h) * HALF + k
                    wait_from(pe, dve_own, s + 1)
                    pe.matmul(ps[k][:, 0:D + 1], place[:, h, k, :], ring_rows[:, h * HALF + k, :],
                              start=True, stop=True).then_inc(summed, 1)

    return {"gpsimd": gpsimd, "vector": vector, "tensor": tensor}


NH, DH, NG = 8, 64, 64
INNER = NH * DH
PAIRS = NH // 2


def four_slots(eng, body):
    for t in range(4):
        body(t, t)
    with eng.Fori(1, NT // 4 - 1) as i:
        for v in range(4):
            body(i * 4 + v, v)
    for t in range(4 * (NT // 4 - 1), NT):
        body(t, t % 4)


def slice_attention(g, c):
    nc, sb, sem, ps, X, ident, ones = (g[n] for n in ("nc", "sb", "sem", "ps", "X", "ident", "ones"))
    logit_w = sb("logit_w", [P, 2, INNER], F32, c)
    logit_b = sb("logit_b", [P, INNER], F32, c)
    slices = sb("slices", [P, PAIRS, D + 1], F32, c)
    back = sb("back", [P, PAIRS, D], F32, c)
    b_out = sb("b_out", [P, D], F32, c)
    wT = sb("wT", [P, PAIRS, (LASTT + 1) * P], F32, c)

    mean, rstd, norm_vector, norm_scalar = row_norm(g, c, "ln1")

    with ExitStack() as c2:
        wx = sb("wx", [P, 2, INNER], F32, c2)
        wxT = sb("wxT", [DH, 2, NH, P], F32, c2)
        ws = sb("ws", [DH, NG], F32, c2)
        bx = sb("bx", [DH, NH], F32, c2)
        bxb = sb("bxb", [DH, NH, P], F32, c2)
        bs = sb("bs", [P, NG], F32, c2)
        tb = sb("tb", [P, NH], F32, c2)
        loaded, turned, copied, multiplied, widened, own = (
            sem("slw_" + n) for n in ("loaded", "turned", "copied", "multiplied", "widened", "own"))
        with nc.Block() as block:
            @block.sync
            def _(sp):
                sp.dma_start(wx[:, :, :], g["L0_ffn_W_x"].rearrange("(c p) n -> p c n", p=P)).then_inc(loaded, 16)
                sp.dma_start(ws[:, :], g["L0_ffn_W_slice"]).then_inc(loaded, 16)
                with nc.allow_non_contiguous_dma(reason="512 numbers"):
                    sp.dma_start(bx[:, :], g["L0_ffn_b_x"].rearrange("(h d) -> d h", h=NH)).then_inc(loaded, 16)
                sp.dma_start(bs[:, :], g["L0_ffn_b_slice"].rearrange("(a n) -> a n", a=1).broadcast_to([P, NG])).then_inc(loaded, 16)
                sp.dma_start(tb[:, :], g["L0_ffn_temperature"].rearrange("a h b c -> a (h b c)").broadcast_to([P, NH])).then_inc(loaded, 16)
                sp.dma_start(b_out[:, :], g["L0_ffn_b_out"].rearrange("(a n) -> a n", a=1).broadcast_to([P, D])).then_inc(loaded, 16)
                sp.wait_ge(loaded, 96)

            @block.tensor
            def _(pe):
                pe.wait_ge(loaded, 96)
                for k in range(2):
                    for h in range(NH):
                        mm = pe.transpose(ps[2 * k + h // 4][0:DH, (h % 4) * P:(h % 4 + 1) * P], wx[:, k, h * DH:(h + 1) * DH], ident[:, :])
                mm.then_inc(turned, 1)
                pe.wait_ge(copied, 4)
                for k in range(2):
                    for h in range(NH):
                        pe.matmul(ps[4 + k][:, h * NG:(h + 1) * NG], wxT[:, k, h, :], ws[:, :], start=True, stop=True)
                pe.wait_ge(widened, 1)
                for h in range(NH):
                    mm = pe.matmul(ps[6][:, h * NG:(h + 1) * NG], bxb[:, h, :], ws[:, :], start=True, stop=True)
                mm.then_inc(multiplied, 1)

            @block.vector
            def _(dve):
                ch = Chain(dve, own)
                dve.wait_ge(loaded, 96)
                dve.tensor_copy(bxb[:, :, :], bx[:, :].unsqueeze(2).broadcast_to([DH, NH, P])).then_inc(widened, 1)
                ch.link(dve.tensor_scalar(tb[:, :], tb[:, :], 0.1, 5.0, ALU.max, ALU.min))
                ch.link(dve.reciprocal(tb[:, :], tb[:, :]))
                dve.wait_ge(turned, 1)
                for k in range(4):
                    dve.tensor_copy(wxT[:, k // 2, (k % 2) * 4:(k % 2) * 4 + 4, :].rearrange("d h p -> d (h p)"), ps[k][0:DH, :]).then_inc(copied, 1)
                dve.wait_ge(multiplied, 1)
                per_head = tb[:, :].unsqueeze(2).broadcast_to([P, NH, NG])
                for k in range(2):
                    dve.tensor_tensor(logit_w[:, k, :].rearrange("p (h g) -> p h g", h=NH),
                                      ps[4 + k][:, :].rearrange("p (h g) -> p h g", h=NH), per_head, ALU.mult)
                bias = logit_b[:, :].rearrange("p (h g) -> p h g", h=NH)
                ch.link(dve.tensor_tensor(bias, ps[6][:, :].rearrange("p (h g) -> p h g", h=NH),
                                          bs[:, :].unsqueeze(1).broadcast_to([P, NH, NG]), ALU.add))
                ch.link(dve.tensor_tensor(bias, bias, per_head, ALU.mult))
                norm_vector(dve)

            @block.scalar
            def _(act):
                norm_scalar(act)

    with ExitStack() as c2:
        stage = sb("sl_stage", [P, 4, D + 1], F32, c2)
        zT = sb("sl_zT", [P, 2, 2, P], F32, c2)
        lg = sb("sl_lg", [P, 2, INNER], F32, c2)
        w = sb("sl_w", [P, 2, INNER], F32, c2)
        top = sb("sl_top", [P, 2, NH], F32, c2)
        tot = sb("sl_tot", [P, 2, NH], F32, c2)
        zero = sb("sl_zero", [P, D + 1], F32, c2)
        staged, turned, zt_ready, logits, exp_in, exp_out, weights, summed, wt_done, wt_taken, own, stage_own = (
            sem("sl_" + n) for n in ("staged", "turned", "zt_ready", "logits", "exp_in", "exp_out", "weights", "summed",
                                     "wt_done", "wt_taken", "own", "stage_own"))
        last = LASTT

        def vector(dve):
            ch = Chain(dve, own)
            dve.memset(zero[:, :], 0.0).then_inc(stage_own, 1)
            dve.memset(stage[:, :, D:D + 1], 1.0).then_inc(stage_own, 1)

            def stage_of(t, slot):
                wait_from(dve, summed, t - 3)
                dve.tensor_scalar(stage[:, slot, 0:D], row(X, t), mean[:, ds(t, 1)], rstd[:, ds(t, 1)], ALU.subtract,
                                  ALU.mult).then_inc(staged, 1)

            def body(t, slot):
                u = slot % 2
                if isinstance(t, int) and t > last:
                    return
                if not isinstance(t, int) or t < last:
                    stage_of(t + 1, (slot + 1) % 4)
                ch.enter(t * 3)
                heads = lg[:, u, :].rearrange("p (h g) -> p h g", h=NH)
                wait_from(dve, logits, t + 1)
                ch.link(dve.tensor_tensor(lg[:, u, :], ps[u][:, :], logit_b[:, :], ALU.add))
                ch.link(dve.tensor_reduce(top[:, u, :], heads, AX.X, ALU.max))
                dve.tensor_tensor(heads, heads, top[:, u, :].unsqueeze(2).broadcast_to([P, NH, NG]), ALU.subtract).then_inc(exp_in, 1)
                wait_from(dve, exp_out, t + 1)
                ch.link(dve.tensor_reduce(tot[:, u, :], heads, AX.X, ALU.add))
                dve.reciprocal(tot[:, u, :], tot[:, u, :]).then_inc(stage_own, 1)
                wait_from(dve, stage_own, t + 3)
                wait_from(dve, summed, t - 1)
                dve.tensor_tensor(w[:, u, :].rearrange("p (h g) -> p h g", h=NH), heads,
                                  tot[:, u, :].unsqueeze(2).broadcast_to([P, NH, NG]), ALU.mult).then_inc(weights, 1)

            stage_of(0, 0)
            four_slots(dve, body)

        def scalar(act):
            def take(t):
                wait_from(act, wt_done, t + 1)
                act.copy(wT[:, :, ds(t * P, P)], ps[6][:, :].rearrange("p (j n) -> p j n", j=PAIRS)).then_inc(wt_taken, 1)

            def zt(t, u):
                wait_from(act, turned, t + 1)
                act.copy(zT[:, u, :, :].rearrange("p k n -> p (k n)"), ps[7][:, 0:2 * P]).then_inc(zt_ready, 1)

            def body(t, slot):
                number = isinstance(t, int)
                if number and t > last:
                    return take(last)
                wait_from(act, exp_in, t + 1)
                act.activation(lg[:, slot % 2, :], lg[:, slot % 2, :], ACT.Exp).then_inc(exp_out, 1)
                if not number or t > 0:
                    take(t - 1)
                if not number or t < last:
                    zt(t + 1, (slot + 1) % 2)

            zt(0, 0)
            four_slots(act, body)

        def tensor(pe):
            pe.wait_ge(stage_own, 2)

            def turn(t, slot):
                wait_from(pe, staged, t + 1)
                wait_from(pe, zt_ready, t)
                for k in range(2):
                    mm = pe.transpose(ps[7][:, k * P:(k + 1) * P], stage[:, slot, k * P:(k + 1) * P], ident[:, :])
                mm.then_inc(turned, 1)

            def sums(t, slot):
                rows = NREST if isinstance(t, int) and t == last else P
                wait_from(pe, weights, t + 1)
                wait_from(pe, wt_taken, t)
                for j in range(PAIRS):
                    mm = pe.transpose(ps[6][:, j * P:(j + 1) * P], w[:, slot % 2, j * P:(j + 1) * P], ident[:, :])
                mm.then_inc(wt_done, 1)
                for j in range(PAIRS):
                    mm = pe.matmul(ps[2 + j][:, 0:D + 1], w[0:rows, slot % 2, j * P:(j + 1) * P], stage[0:rows, slot, :],
                                   start=False, stop=rows < P, skip_group_check=True)
                mm.then_inc(summed, 1)

            def body(t, slot):
                number = isinstance(t, int)
                if number and t > last:
                    return sums(last, last % 4)
                wait_from(pe, zt_ready, t + 1)
                wait_from(pe, exp_in, t - 1)
                for k in range(2):
                    mm = pe.matmul(ps[slot % 2][:, :], zT[:, slot % 2, k, :], logit_w[:, k, :], start=(k == 0), stop=(k == 1))
                mm.then_inc(logits, 1)
                if not number or t > 0:
                    sums(t - 1, (slot - 1) % 4)
                if not number or t < last:
                    turn(t + 1, (slot + 1) % 4)

            for j in range(PAIRS):
                pe.matmul(ps[2 + j][:, 0:D + 1], zero[:, 0:P], zero[:, :], start=True, stop=False, skip_group_check=True)
            turn(0, 0)
            four_slots(pe, body)

        run_block(nc, {"vector": vector, "scalar": scalar, "tensor": tensor})

    with ExitStack() as c2:
        names = ("turned", "copied", "tokens", "norms", "tok_ready", "tok_turned", "tokT_ready", "qkv", "qkv_ready", "scored",
                 "exp_in", "exp_out", "attn", "attn_turned", "attnT_ready", "mixed", "mixed_ready", "backed", "back_ready",
                 "loaded", "moved", "own")
        s = {n: sem("sa_" + n) for n in names}
        yT = sb("sa_yT", [P, 2, INNER], F32, c2)
        norm_row = sb("sa_norm_row", [1, INNER], F32, c2)
        bfx = sb("sa_bfx", [1, INNER], F32, c2)
        wfx = sb("sa_wfx", [P, 2, INNER], F32, c2)
        wq, wk, wv = (sb(n, [DH, DH], F32, c2) for n in ("sa_wq", "sa_wk", "sa_wv"))
        wo = sb("sa_wo", [DH, NH, D], F32, c2)
        den = sb("sa_den", [NG, NH], F32, c2)
        tok, tokT, qT, kT, v, at, atT, mixT = (sb("sa_" + n, [DH, INNER], F32, c2)
                                               for n in ("tok", "tokT", "qT", "kT", "v", "at", "atT", "mixT"))
        peak = sb("sa_peak", [NG, NH], F32, c2)
        odd = slices[0:NG, :, 0:D]
        scale = float(DH) ** -0.5

        def h_(a, h):
            return a[:, h * DH:(h + 1) * DH]

        def by_head(a):
            return a.rearrange("p (h g) -> p h g", h=NH)

        def sync(sp):
            for dst, src in ((wfx[:, :, :], g["L0_ffn_W_fx"].rearrange("(c p) n -> p c n", p=P)), (wq[:, :], g["L0_ffn_W_q"]),
                             (wk[:, :], g["L0_ffn_W_k"]), (wv[:, :], g["L0_ffn_W_v"]),
                             (wo[:, :, :], g["L0_ffn_W_out"].rearrange("(h d) n -> d h n", d=DH)),
                             (bfx[:, :], g["L0_ffn_b_fx"].rearrange("(a n) -> a n", a=1))):
                sp.dma_start(dst, src).then_inc(s["loaded"], 16)
            sp.wait_ge(s["back_ready"], 1)
            sp.dma_start(back[NG:P, :, :], odd).then_inc(s["moved"], 16)
            sp.wait_ge(s["moved"], 16)

        def tensor(pe):
            pe.wait_ge(s["copied"], 1)
            for j in range(PAIRS):
                for k in range(2):
                    pe.transpose(ps[k][:, j * P:(j + 1) * P], slices[:, j, k * P:(k + 1) * P], ident[:, :])
                mm = pe.transpose(ps[6][0:1, j * P:(j + 1) * P], slices[:, j, D:D + 1], ident[:, :])
            mm.then_inc(s["turned"], 1)
            pe.wait_ge(s["copied"], 4)
            pe.wait_ge(s["loaded"], 96)
            for h in range(NH):
                for k in range(2):
                    pe.matmul(h_(ps[3][0:NG, :], h), h_(yT[:, k, :], h), h_(wfx[:, k, :], h), start=(k == 0), stop=False)
                pe.matmul(h_(ps[3][0:NG, :], h), h_(norm_row, h), h_(bfx, h), start=False, stop=True)
            for h in range(NH):
                mm = pe.matmul(ps[4][0:NG, h:h + 1], h_(norm_row, h), ones[0:1, 0:1], start=True, stop=True)
            mm.then_inc(s["tokens"], 1)
            pe.wait_ge(s["tok_ready"], 1)
            for h in range(NH):
                mm = pe.transpose(h_(ps[5][0:DH, :], h), h_(tok, h), ident[0:DH, 0:DH])
            mm.then_inc(s["tok_turned"], 1)
            pe.wait_ge(s["tokT_ready"], 1)
            pe.matmul(ps[0][0:DH, :], wq[:, :], tokT[:, :], start=True, stop=True)
            pe.matmul(ps[1][0:DH, :], wk[:, :], tokT[:, :], start=True, stop=True)
            for h in range(NH):
                mm = pe.matmul(h_(ps[2][0:NG, :], h), h_(tokT, h), wv[:, :], start=True, stop=True)
            mm.then_inc(s["qkv"], 1)
            pe.wait_ge(s["qkv_ready"], 3)
            for h in range(NH):
                mm = pe.matmul(h_(ps[3][0:NG, :], h), h_(qT, h), h_(kT, h), start=True, stop=True)
            mm.then_inc(s["scored"], 1)
            pe.wait_ge(s["attn"], 1)
            for h in range(NH):
                mm = pe.transpose(h_(ps[4][0:NG, :], h), h_(at, h), ident[0:NG, 0:NG])
            mm.then_inc(s["attn_turned"], 1)
            pe.wait_ge(s["attnT_ready"], 1)
            for h in range(NH):
                mm = pe.matmul(h_(ps[5][0:DH, :], h), h_(v, h), h_(atT, h), start=True, stop=True)
            mm.then_inc(s["mixed"], 1)
            pe.wait_ge(s["mixed_ready"], 1)
            for h in range(NH):
                mm = pe.matmul(ps[h % 2 * 2 + h // 4][0:NG, (h // 2 % 2) * D:(h // 2 % 2 + 1) * D], h_(mixT, h), wo[:, h, :], start=True, stop=True)
            mm.then_inc(s["backed"], 1)

        def vector(dve):
            ch = Chain(dve, s["own"])
            for j in range(PAIRS):
                ins = dve.tensor_copy(slices[:, j, :], ps[2 + j][:, 0:D + 1])
            ins.then_inc(s["copied"], 1)
            dve.wait_ge(s["turned"], 1)
            for k in range(2):
                dve.tensor_copy(yT[:, k, :], ps[k][:, :]).then_inc(s["copied"], 1)
            dve.tensor_copy(norm_row[:, :], ps[6][0:1, :]).then_inc(s["copied"], 1)
            dve.wait_ge(s["tokens"], 1)
            ch.link(dve.tensor_scalar(den[:, :], ps[4][0:NG, 0:NH], 1e-5, None, ALU.add))
            ch.link(dve.reciprocal(den[:, :], den[:, :]))
            dve.tensor_tensor(by_head(tok), by_head(ps[3][0:NG, :]), den[:, :].unsqueeze(2).broadcast_to([NG, NH, DH]), ALU.mult).then_inc(s["tok_ready"], 1)
            dve.wait_ge(s["tok_turned"], 1)
            dve.tensor_copy(tokT[:, :], ps[5][0:DH, :]).then_inc(s["tokT_ready"], 1)
            dve.wait_ge(s["qkv"], 1)
            for k, a in enumerate((qT, kT, v)):
                dve.tensor_copy(a[:, :], ps[k][0:DH, :]).then_inc(s["qkv_ready"], 1)
            dve.wait_ge(s["scored"], 1)
            ch.link(dve.tensor_reduce(peak[:, :], by_head(ps[3][0:NG, :]), AX.X, ALU.max))
            dve.tensor_tensor(by_head(at), by_head(ps[3][0:NG, :]), peak[:, :].unsqueeze(2).broadcast_to([NG, NH, NG]), ALU.subtract).then_inc(s["exp_in"], 1)
            dve.wait_ge(s["exp_out"], 1)
            ch.link(dve.tensor_reduce(peak[:, :], by_head(at), AX.X, ALU.add))
            ch.link(dve.reciprocal(peak[:, :], peak[:, :]))
            dve.tensor_tensor(by_head(at), by_head(at), peak[:, :].unsqueeze(2).broadcast_to([NG, NH, NG]), ALU.mult).then_inc(s["attn"], 1)
            dve.wait_ge(s["attn_turned"], 1)
            dve.tensor_copy(atT[:, :], ps[4][0:NG, :]).then_inc(s["attnT_ready"], 1)
            dve.wait_ge(s["mixed"], 1)
            dve.tensor_copy(mixT[:, :], ps[5][0:DH, :]).then_inc(s["mixed_ready"], 1)
            dve.wait_ge(s["backed"], 1)
            for b in range(4):
                to = (back[0:NG, :, :], odd)[b // 2]
                ch.link(dve.tensor_copy(to[:, 2 * (b % 2):2 * (b % 2) + 2, :], ps[b][0:NG, :].rearrange("p (j d) -> p j d", j=2)))
            dve.sem_inc(s["back_ready"], 1)

        def scalar(act):
            act.wait_ge(s["exp_in"], 1)
            act.activation(at[:, :], at[:, :], ACT.Exp, scale=scale).then_inc(s["exp_out"], 1)

        run_block(nc, {"sync": sync, "tensor": tensor, "vector": vector, "scalar": scalar})

    with ExitStack() as c2:
        here = sb("sb_here", [P, 2, PAIRS * P], F32, c2)
        here_ready, products, added, own = (sem("sb_" + n) for n in ("here_ready", "products", "added", "own"))
        tiles = LASTT + 1

        def each(eng, body):
            for i in rounds_of(eng, tiles // 2):
                for u in range(2):
                    body(i * 2 + u, u)
            if tiles % 2:
                body(tiles - 1, 0)

        def scalar(act):
            def body(t, u):
                wait_from(act, products, t)
                act.copy(here[:, u, :].rearrange("p (j n) -> p j n", j=PAIRS), wT[:, :, ds(t * P, P)]).then_inc(here_ready, 1)
            each(act, body)

        def tensor(pe):
            pe.sem_inc(products, 1)

            def body(t, u):
                wait_from(pe, here_ready, t + 1)
                wait_from(pe, added, t)
                for j in range(PAIRS):
                    mm = pe.matmul(ps[u][:, 0:D], here[:, u, j * P:(j + 1) * P], back[:, j, :], start=(j == 0), stop=(j == PAIRS - 1))
                mm.then_inc(products, 1)
            each(pe, body)

        def vector(dve):
            dve.sem_inc(added, 1)
            ch = Chain(dve, own)

            def body(t, u):
                ch.enter(t)
                wait_from(dve, products, t + 2)
                ch.link(dve.tensor_tensor(row(X, t), ps[u][:, 0:D], row(X, t), ALU.add))
                dve.tensor_tensor(row(X, t), row(X, t), b_out[:, :], ALU.add).then_inc(added, 1)
            each(dve, body)

        run_block(nc, {"scalar": scalar, "tensor": tensor, "vector": vector})


H1, F1 = 8, 32
HB = F1 + 1
HW = H1 * HB
RW = HW + H1


def graph_attention(g, c):
    nc, sb, sem, ps, X, ident = (g[n] for n in ("nc", "sb", "sem", "ps", "X", "ident"))
    h_rows = nc.dram_tensor("h_rows", [NT * P, RW], F32)
    dst_scores = sb("dst_scores", [P, NT, H1], F32, c)
    local_key = sb("key1", [P, SG], F32, c)
    row_of = sb("row1", [P, SG], U32, c)
    last = sb("last1", [P, SG], F32, c)
    tile_of = sb("tile1", [1, SG], I32, c)
    acc = sb("acc", [P, NT, HW], F32, c)
    peak = sb("peak", [P, NT, H1], F32, c)

    with ExitStack() as c2:
        w = sb("ga_w", [P, 2, H1, F1], F32, c2)
        av = sb("ga_av", [P, 2, H1, F1], F32, c2)
        wa = sb("ga_wa", [P, 2, H1, F1], F32, c2)
        wall = sb("ga_wall", [P, 2, H1 * F1 + 2 * H1], F32, c2)
        stage = sb("ga_stage", [P, 2, D], F32, c2)
        zT = sb("ga_zT", [P, 2, 2, P], F32, c2)
        new = sb("ga_new", [P, 2, RW], F32, c2)
        loaded, folded, staged, turned, zt_ready, products, new_ready, taken, own = (
            sem("ga_" + n) for n in ("loaded", "folded", "staged", "turned", "zt_ready", "products", "new_ready", "taken", "own"))
        stored = [sem(f"ga_stored{u}") for u in range(2)]
        mean, rstd, norm_vector, norm_scalar = row_norm(g, c2, "ln2")

        def sync(sp):
            for k in range(2):
                sp.dma_start(w[:, k, :, :], g["L1_gnn_W"].rearrange("h (c p) f -> c p h f", p=P)[k]).then_inc(loaded, 16)
            for k, a in enumerate(("L1_gnn_a_src", "L1_gnn_a_dst")):
                sp.dma_start(av[:, k, :, :].rearrange("p h f -> p (h f)"), g[a].rearrange("(a h) f -> a (h f)", a=1).broadcast_to([P, H1 * F1])).then_inc(loaded, 16)
            sp.dma_start(local_key[:, :], g["key_by_dst"][:, :]).then_inc(loaded, 16)
            sp.dma_start(row_of[:, :], g["row_by_dst"][:, :]).then_inc(loaded, 16)
            sp.dma_start(last[:, :], g["last_by_dst"][:, :]).then_inc(loaded, 16)
            sp.dma_start(tile_of[:, :], g["tile_of_step_dram"][1:2, :]).then_inc(loaded, 16)
            with sp.Fori(0, NT // 2) as i:
                for u in range(2):
                    wait_from(sp, new_ready, (i * 2 + u + 1) * 2)
                    sp.dma_start(h_rows[ds((i * 2 + u) * P, P), :], new[:, u, :]).then_inc(stored[u], 16)
            for u in range(2):
                sp.wait_ge(stored[u], 16 * (NT // 2))

        def vector(dve):
            ch = Chain(dve, own)
            norm_vector(dve)
            dve.memset(acc[:, :, :], 0.0)
            dve.memset(peak[:, :, :], -FAR)
            for u in range(2):
                ch.link(dve.memset(new[:, u, :], 1.0))
            dve.sem_inc(taken, 1)
            dve.wait_ge(loaded, 128)
            for k in range(2):
                dve.tensor_copy(wall[:, k, 0:H1 * F1], w[:, k, :, :].rearrange("p h f -> p (h f)")).then_inc(folded, 1)
                for q in range(2):
                    ch.link(dve.tensor_tensor(wa[:, k, :, :], w[:, k, :, :], av[:, q, :, :], ALU.mult))
                    at = H1 * F1 + q * H1
                    ch.link(dve.tensor_reduce(wall[:, k, at:at + H1], wa[:, k, :, :], AX.X, ALU.add))
            ch.wait()
            dve.sem_inc(folded, 1)

            def ahead(t, u, pair):
                wait_from(dve, turned, t - 1)
                dve.tensor_scalar(stage[:, u, :], row(X, t), mean[:, ds(t, 1)], rstd[:, ds(t, 1)], ALU.subtract,
                                  ALU.mult).then_inc(staged, 1)

            def now(t, u, pair):
                wait_from(dve, products, t + 1)
                wait_from(dve, stored[u], pair * 16)
                dve.tensor_copy(new[:, u, 0:HW].rearrange("p (h b) -> p h b", b=HB)[:, :, 0:F1],
                                ps[u][:, 0:H1 * F1].rearrange("p (h f) -> p h f", f=F1)).then_inc(new_ready, 1)
                dve.tensor_copy(new[:, u, HW:RW], ps[u][:, H1 * F1:H1 * F1 + H1]).then_inc(new_ready, 1)
                dve.tensor_scalar(row(dst_scores, t), ps[u][:, H1 * F1 + H1:H1 * F1 + 2 * H1], 1.0, None, ALU.mult).then_inc(taken, 1)

            over_tiles(dve, ahead, now)

        def scalar(act):
            norm_scalar(act)

            def ahead(t, u, pair):
                wait_from(act, turned, t + 1)
                act.copy(zT[:, u, :, :].rearrange("p k n -> p (k n)"), ps[4 + u][:, 0:2 * P]).then_inc(zt_ready, 1)

            over_tiles(act, ahead, lambda t, u, pair: None)

        def tensor(pe):
            pe.wait_ge(folded, 3)

            def ahead(t, u, pair):
                wait_from(pe, staged, t + 1)
                for k in range(2):
                    mm = pe.transpose(ps[4 + u][:, k * P:(k + 1) * P], stage[:, u, k * P:(k + 1) * P], ident[:, :])
                mm.then_inc(turned, 1)

            def now(t, u, pair):
                wait_from(pe, zt_ready, t + 1)
                wait_from(pe, taken, t)
                for k in range(2):
                    mm = pe.matmul(ps[u][:, 0:H1 * F1 + 2 * H1], zT[:, u, k, :], wall[:, k, :], start=(k == 0), stop=(k == 1))
                mm.then_inc(products, 1)

            over_tiles(pe, ahead, now)

        run_block(nc, {"sync": sync, "vector": vector, "scalar": scalar, "tensor": tensor})

    pool_passed = sem("ge_pool_passed")
    with ExitStack() as c2:
        rows = sb("ge_rows", [P, 2, HALF, RW + 1], F32, c2)
        index = sb("ge_index", [P, 2, HALF], U32, c2)
        place = sb("ge_place", [P, 2, HALF, P], F32, c2)
        placeT = sb("ge_placeT", [P, 2, 4, P], F32, c2)
        cuts = sb("ge_cuts", [HALF * H1, 2, 2, P], F32, c2)
        run = sb("ge_run", [P, 2, P], F32, c2)
        sc = sb("ge_sc", [P, 3, HALF, H1], F32, c2)
        weight = sb("ge_weight", [P, HALF, H1], F32, c2)
        absent = sb("ge_absent", [P, HALF], F32, c2)
        big = sb("ge_big", [P, HALF, H1], F32, c2)
        tops = sb("ge_tops", [P, HALF, H1], F32, c2)
        scale = sb("ge_scale", [P, HALF, 2, H1], F32, c2)
        part = sb("ge_part", [P, 2, HW], F32, c2)
        src_scores = sb("ge_src_scores", [P, P], F32, c2)
        src_ready, cleared = sem("ge_src_ready"), sem("ge_cleared")
        names = ("indexed", "placed", "turned", "scanned", "maxed", "p_turned", "pT_ready", "scored", "taken", "exp_in",
                 "exp_out", "weighted", "tops_made", "summed", "scale_in", "scale_out", "scores_own", "tops_own",
                 "part_done", "add_own")
        (indexed, placed, turned, scanned, maxed, p_turned, pT_ready, scored, taken, exp_in, exp_out, weighted, tops_made,
         summed, scale_in, scale_out, scores_own, tops_own, part_done, add_own) = (sem("ge_" + n) for n in names)
        fetched = [sem(f"ge_fetched{h}") for h in range(2)]
        cut_loaded = [sem(f"ge_cut_loaded{h}") for h in range(2)]
        HH = HALF * H1

        def halves(eng, front, back=None):
            front(0, 0, 0)
            for i in rounds_of(eng, STEPS // (2 * HALF)):
                front(i * 2 + 1, 1, i)
                if back:
                    back(i * 2, 0)
                front(i * 2 + 2, 0, i + 1)
                if back:
                    back(i * 2 + 1, 1)

        def gpsimd(pool):
            def front(n, h, pair):
                wait_apart(pool, fetched[h], pair * (16 * HALF), pool_passed)
                pool.tensor_copy(index[:, h, :], row_of[:, ds(n * HALF, HALF)]).then_inc(indexed, 1)
                wait_apart(pool, indexed, n + 1, pool_passed)
                wait_apart(pool, summed, (n - 1) * HALF, pool_passed)
                for k in range(HALF):
                    pool.indirect_dma_start(out=rows[:, h, k, 0:RW], out_offset=None, in_=h_rows[:, :],
                                            in_offset=bass.IndirectOffsetOnAxis(ap=index[:, h, k:k + 1], axis=0)).then_inc(fetched[h], 16)
            halves(pool, front)

        def sync(sp):
            def front(n, h, pair):
                wait_from(sp, scanned, (n - 1) * 2)
                for k in range(HALF):
                    src = g["cuts_dram"][ds(n * HALF + k, 1), :].broadcast_to([H1, 2 * P])
                    sp.dma_start(cuts[k * H1:(k + 1) * H1, h, :, :].rearrange("q a e -> q (a e)"), src).then_inc(cut_loaded[h], 16)
            halves(sp, front)

        def tensor(pe):
            def front_a(n, h, pair):
                wait_from(pe, fetched[h], (pair + 1) * (16 * HALF))
                wait_from(pe, taken, n)
                wait_from(pe, src_ready, n + 1)
                pe.transpose(ps[0][:, 0:P], src_scores[:, :], ident[:, :]).then_inc(turned, 1)
                wait_from(pe, placed, n + 1)
                for q in range(2):
                    wait_from(pe, pT_ready, n * 2 + q)
                    for k in range(4):
                        mm = pe.transpose(ps[1][:, k * P:(k + 1) * P], place[:, h, q * 4 + k, :], ident[:, :])
                    mm.then_inc(p_turned, 1)
                    wait_from(pe, pT_ready, n * 2 + q + 1)
                    for k in range(4):
                        at = q * 4 + k
                        t = pe.value_load(tile_of[0:1, ds(n * HALF + at, 1)], min_val=0, max_val=NT - 1)
                        mm = pe.matmul(ps[2][:, at * H1:(at + 1) * H1], placeT[:, q, k, :], row(dst_scores, t), start=True, stop=True)
                    mm.then_inc(scored, 1)

            def front_b(n):
                wait_from(pe, scanned, n * 2 + 2)
                pe.transpose(ps[0][:, P:2 * P], run[:, 1, :], ident[:, :]).then_inc(maxed, 1)

            def front_c(n, h):
                wait_from(pe, weighted, n * 3 + 3)
                for k in range(HALF):
                    mm = pe.matmul(ps[3][:, k * 16:k * 16 + H1 + 1], place[:, h, k, :], rows[:, h, k, HW:RW + 1], start=True, stop=True)
                mm.then_inc(tops_made, 1)

            def back(n, h, some):
                for k in some:
                    wait_from(pe, part_done, n * HALF + k + 1)
                    pe.matmul(ps[4 + k % 4][:, 0:HW], place[:, h, k, :], rows[:, h, k, 0:HW], start=True, stop=True).then_inc(summed, 1)

            def both(n, h, pair):
                front_a(n + 1, 1 - h, pair)
                back(n, h, range(0, 4))
                front_b(n + 1)
                back(n, h, range(4, HALF))
                front_c(n + 1, 1 - h)

            front_a(0, 0, 0)
            front_b(0)
            front_c(0, 0)
            for i in rounds_of(pe, STEPS // (2 * HALF)):
                both(i * 2, 0, i)
                both(i * 2 + 1, 1, i + 1)

        def scalar(act):
            def front_a(n, h, pair):
                wait_from(act, fetched[h], (pair + 1) * (16 * HALF))
                wait_from(act, turned, n)
                act.copy(src_scores[:, 0:HH].rearrange("p (s h) -> p s h", h=H1), rows[:, h, :, HW:RW]).then_inc(src_ready, 1)
                for q in range(2):
                    wait_from(act, p_turned, n * 2 + q + 1)
                    wait_from(act, scored, n * 2 + q - 1)
                    act.copy(placeT[:, q, :, :].rearrange("p k n -> p (k n)"), ps[1][:, :]).then_inc(pT_ready, 1)

            def front_b(n):
                wait_from(act, exp_in, n + 1)
                act.activation(weight[:, :, :], sc[:, 1, :, :], ACT.Exp).then_inc(exp_out, 1)

            def both(n, h, pair):
                front_a(n + 1, 1 - h, pair)
                wait_from(act, scale_in, n + 1)
                act.activation(scale[:, :, :, :], scale[:, :, :, :], ACT.Exp).then_inc(scale_out, 1)
                front_b(n + 1)

            act.wait_ge(cleared, 2)
            front_a(0, 0, 0)
            front_b(0)
            for i in rounds_of(act, STEPS // (2 * HALF)):
                both(i * 2, 0, i)
                both(i * 2 + 1, 1, i + 1)

        def vector(dve):
            dve.memset(run[:, :, :], 0.0).then_inc(cleared, 1)
            dve.memset(src_scores[:, :], 0.0).then_inc(cleared, 1)
            dve.wait_ge(cleared, 2)
            dve.sem_inc(part_done, 4)

            def put_places(n, h):
                wait_from(dve, summed, (n - 1) * HALF)
                dve.tensor_tensor(place[:, h, :, :], g["iota_row"][:, :].unsqueeze(1).broadcast_to([P, HALF, P]),
                                  local_key[:, ds(n * HALF, HALF)].unsqueeze(2).broadcast_to([P, HALF, P]), ALU.is_equal).then_inc(placed, 1)

            def scan_runs(n, h, pair):
                wait_from(dve, turned, n + 1)
                wait_from(dve, cut_loaded[h], (pair + 1) * (16 * HALF))
                wait_from(dve, maxed, n)
                dve.tensor_tensor_scan(run[0:HH, 0, :], cuts[:, h, 0, :], ps[0][0:HH, 0:P], -FAR, ALU.add, ALU.max).then_inc(scanned, 1)
                wait_from(dve, scanned, n * 2 + 1)
                dve.tensor_tensor_scan(run[0:HH, 1, ::-1], cuts[:, h, 1, ::-1], run[0:HH, 0, ::-1], -FAR, ALU.add, ALU.max).then_inc(scanned, 1)

            def edge_scores(n, h):
                ch = Chain(dve, scores_own, n * 3)
                wait_from(dve, scored, n * 2 + 2)
                ch.link(dve.tensor_copy(sc[:, 0, :, :].rearrange("p s h -> p (s h)"), ps[2][:, 0:HH]))
                wait_from(dve, maxed, n + 1)
                dve.tensor_tensor(sc[:, 2, :, :].rearrange("p s h -> p (s h)"), ps[0][:, P:P + HH],
                                  sc[:, 0, :, :].rearrange("p s h -> p (s h)"), ALU.add).then_inc(taken, 1)
                ch.link(dve.tensor_tensor(sc[:, 1, :, :], rows[:, h, :, HW:RW], sc[:, 0, :, :], ALU.add))
                wait_from(dve, taken, n + 1)
                ch.link(dve.scalar_tensor_tensor(out=sc[:, 1:3, :, :].rearrange("p a s h -> p (a s h)"), scalar=0.2,
                                                 in0=sc[:, 1:3, :, :].rearrange("p a s h -> p (a s h)"),
                                                 in1=sc[:, 1:3, :, :].rearrange("p a s h -> p (a s h)"), op0=ALU.mult, op1=ALU.max))
                dve.tensor_tensor(sc[:, 1, :, :], sc[:, 1, :, :], sc[:, 2, :, :], ALU.subtract).then_inc(exp_in, 1)

            def weigh(n, h):
                flags = last[:, ds(n * HALF, HALF)]
                dve.tensor_tensor(rows[:, h, :, HW:RW], sc[:, 2, :, :], flags.unsqueeze(2).broadcast_to([P, HALF, H1]), ALU.mult).then_inc(weighted, 1)
                dve.tensor_scalar(rows[:, h, :, RW:RW + 1], flags.unsqueeze(2), 1.0, None, ALU.mult).then_inc(weighted, 1)
                wait_from(dve, exp_out, n + 1)
                blocks = rows[:, h, :, 0:HW].rearrange("p s (h b) -> p s h b", b=HB)
                dve.tensor_tensor(blocks, blocks, weight[:, :, :].unsqueeze(3).broadcast_to([P, HALF, H1, HB]), ALU.mult).then_inc(weighted, 1)

            def new_peaks(n):
                ch = Chain(dve, tops_own, n * (2 + 3 * HALF))
                made = ps[3][:, 0:16 * HALF].rearrange("p (s w) -> p s w", w=16)
                wait_from(dve, tops_made, n + 1)
                ch.link(dve.tensor_scalar(absent[:, :], made[:, :, H1], -1.0, FAR, ALU.add, ALU.mult))
                ch.link(dve.tensor_tensor(big[:, :, :], made[:, :, 0:H1], absent[:, :].unsqueeze(2).broadcast_to([P, HALF, H1]), ALU.add))
                tiles = []
                for k in range(HALF):
                    t = dve.value_load(tile_of[0:1, ds(n * HALF + k, 1)], min_val=0, max_val=NT - 1)
                    tiles.append(t)
                    ch.link(dve.tensor_tensor(tops[:, k, :], row(peak, t), big[:, k, :], ALU.max))
                    ch.link(dve.tensor_tensor(scale[:, k, 0, :], row(peak, t), tops[:, k, :], ALU.subtract))
                    ch.step(dve.tensor_scalar(row(peak, t), tops[:, k, :], 1.0, None, ALU.mult))
                    ch.wait()
                dve.tensor_tensor(scale[:, :, 1, :], big[:, :, :], tops[:, :, :], ALU.subtract).then_inc(scale_in, 1)
                return tiles

            def add_sums(n, tiles):
                ch = Chain(dve, add_own, n * (2 * HALF))
                wait_from(dve, scale_out, n + 1)
                for k in range(HALF):
                    here = row(acc, tiles[k])
                    blocks = here.rearrange("p (h b) -> p h b", b=HB)
                    wait_from(dve, summed, n * HALF + k + 1)
                    dve.tensor_tensor(part[:, k % 2, :].rearrange("p (h b) -> p h b", b=HB), ps[4 + k % 4][:, 0:HW].rearrange("p (h b) -> p h b", b=HB),
                                      scale[:, k, 1, :].unsqueeze(2).broadcast_to([P, H1, HB]), ALU.mult).then_inc(part_done, 1)
                    ch.link(dve.tensor_tensor(blocks, blocks, scale[:, k, 0, :].unsqueeze(2).broadcast_to([P, H1, HB]), ALU.mult))
                    wait_from(dve, part_done, n * HALF + k + 5)
                    ch.link(dve.tensor_tensor(here, here, part[:, k % 2, :], ALU.add))

            def both(n, h, pair):
                put_places(n + 1, 1 - h)
                scan_runs(n + 1, 1 - h, pair)
                tiles = new_peaks(n)
                edge_scores(n + 1, 1 - h)
                add_sums(n, tiles)
                weigh(n + 1, 1 - h)

            put_places(0, 0)
            scan_runs(0, 0, 0)
            edge_scores(0, 0)
            weigh(0, 0)
            for i in rounds_of(dve, STEPS // (2 * HALF)):
                both(i * 2, 0, i)
                both(i * 2 + 1, 1, i + 1)

        run_block(nc, {"gpsimd": gpsimd, "sync": sync, "tensor": tensor, "scalar": scalar, "vector": vector})

    with ExitStack() as c2:
        den = sb("gx_den", [P, NT, H1], F32, c2)
        many = 10
        out_rows = sb("gx_out", [P, many, D], F32, c2)
        own = sem("gx_own")

        def vector(dve):
            ch = Chain(dve, own)
            blocks = acc[:, :, :].rearrange("p t (h b) -> p t h b", b=HB)
            ch.link(dve.tensor_scalar(den[:, :, :], blocks[:, :, :, F1], 1e-8, None, ALU.add))
            ch.link(dve.reciprocal(den[:, :, :], den[:, :, :]))
            start = ch.n
            with dve.Fori(0, NT // many) as i:
                ch.enter(i * 2 + start)
                tiles = ds(i * many, many)
                ch.link(dve.tensor_tensor(out_rows[:, :, :].rearrange("p t (h f) -> p t h f", f=F1), blocks[:, tiles, :, 0:F1],
                                          den[:, tiles, :].unsqueeze(3).broadcast_to([P, many, H1, F1]), ALU.mult))
                ch.link(dve.tensor_tensor(X[:, tiles, :], X[:, tiles, :], out_rows[:, :, :], ALU.add))

        run_block(nc, {"vector": vector})


HID, NE = 1024, 8
HC = HID // P
XW = D + 5
ESTEPS = LASTT + 1 + NE - 1


def laps(eng, body, count):
    whole = (count - 1) // 4
    for t in range(4):
        body(t, t, 0)
    with eng.Fori(1, whole) as i:
        for v in range(4):
            body(i * 4 + v, v, i)
    for t in range(4 * whole, count):
        body(t, t % 4, t // 4)


def hidden(g, c, pre, count, stage, product, consume):
    nc, sb, sem, ps, ident, w1, b1 = (g[n] for n in ("nc", "sb", "sem", "ps", "ident", "w1", "b1"))
    rows = sb(pre + "rows", [P, 2, D], F32, c)
    zT = sb(pre + "zT", [P, 2, 2, P], F32, c)
    hT = sb(pre + "hT", [P, 2, HC, P], F32, c)
    staged, turned, zt_ready, h_done, gelu_done, produced, taken = (
        sem(pre + n) for n in ("staged", "turned", "zt_ready", "h_done", "gelu_done", "produced", "taken"))

    def after(slot, lap):
        return (slot + 1) % 4, lap + (slot == 3)

    def vector(dve):
        def stage_of(t, slot, lap):
            wait_from(dve, turned, t - 1)
            stage(dve, t, slot, lap, rows[:, slot % 2, :]).then_inc(staged, 1)

        def consume_of(t, slot, lap):
            wait_from(dve, produced, t + 1)
            consume(dve, t, slot, lap, lambda ins: ins.then_inc(taken, 1))

        def body(t, slot, lap):
            if not isinstance(t, int) or t + 1 < count:
                stage_of(t + 1, *after(slot, lap))
            if not isinstance(t, int) or t > 0:
                consume_of(t - 1, (slot - 1) % 4, lap - (slot == 0))

        stage_of(0, 0, 0)
        laps(dve, body, count)
        consume_of(count - 1, (count - 1) % 4, (count - 1) // 4)

    def scalar(act):
        def turn_copy(t, u):
            wait_from(act, turned, t + 1)
            wait_from(act, h_done, (t - 1) * 2)
            act.copy(zT[:, u, :, :].rearrange("p k n -> p (k n)"), ps[4 + u][:, 0:2 * P]).then_inc(zt_ready, 1)

        def body(t, slot, lap):
            u = slot % 2
            if not isinstance(t, int) or t + 1 < count:
                turn_copy(t + 1, 1 - u)
            wait_from(act, produced, t - 1)
            for m in range(HC):
                if m % 4 == 0:
                    wait_from(act, h_done, t * 2 + m // 4 + 1)
                act.activation(hT[:, u, m, :], ps[2 * u + m // 4][:, (m % 4) * P:(m % 4 + 1) * P], ACT.Gelu,
                               bias=b1[:, m:m + 1]).then_inc(gelu_done, 1)

        turn_copy(0, 0)
        laps(act, body, count)

    def tensor(pe):
        pe.wait_ge(g["w_loaded"], g["w_count"])

        def turn(t, u):
            wait_from(pe, staged, t + 1)
            wait_from(pe, zt_ready, t - 1)
            for k in range(2):
                mm = pe.transpose(ps[4 + u][:, k * P:(k + 1) * P], rows[:, u, k * P:(k + 1) * P], ident[:, :])
            mm.then_inc(turned, 1)

        def produce(t, u):
            wait_from(pe, gelu_done, (t + 1) * HC)
            wait_from(pe, taken, t - 1)
            product(pe, t, u, hT[:, u, :, :]).then_inc(produced, 1)

        def body(t, slot, lap):
            u = slot % 2
            if not isinstance(t, int) or t + 1 < count:
                turn(t + 1, 1 - u)
            wait_from(pe, zt_ready, t + 1)
            wait_from(pe, gelu_done, (t - 1) * HC)
            for m in range(HC):
                for k in range(2):
                    mm = pe.matmul(ps[2 * u + m // 4][:, (m % 4) * P:(m % 4 + 1) * P], w1[:, k, m * P:(m + 1) * P], zT[:, u, k, :],
                                   start=(k == 0), stop=(k == 1))
                if m % 4 == 3:
                    mm.then_inc(h_done, 1)
            if not isinstance(t, int) or t > 0:
                produce(t - 1, 1 - u)

        turn(0, 0)
        laps(pe, body, count)
        produce(count - 1, (count - 1) % 2)

    return {"vector": vector, "scalar": scalar, "tensor": tensor, "taken": taken}


def routed_network(g, c, out):
    nc, sb, sem, ps, X, ident = (g[n] for n in ("nc", "sb", "sem", "ps", "X", "ident"))
    routed_rows = nc.dram_tensor("routed_rows", [NT * P, XW], F32)
    tile_of_estep = nc.dram_tensor("tile_of_estep", [2, 64], I32)
    w1 = g["w1"] = sb("w1", [P, 2, HID], F32, c)
    b1 = g["b1"] = sb("b1", [P, HC], F32, c)
    wg = sb("wg", [P, HC, NE], F32, c)
    bg = sb("bg", [P, NE], F32, c)
    wd = sb("wd", [P, NE, HC, D], F32, c)
    bd = sb("bd", [P, NE, D], F32, c)
    gates = sb("gates", [P, NT, NE], F32, c)
    w_loaded = g["w_loaded"] = sem("ffn_w_loaded")
    g["w_count"] = 64
    expert_of = sb("expert_of", [P, 64], F32, c)
    step_tables = sb("step_tables", [1, 2, 64], I32, c)
    mean, rstd, norm_vector, norm_scalar = row_norm(g, c, "ln3")

    with ExitStack() as c2:
        def stage(dve, t, slot, lap, to):
            return dve.tensor_scalar(to, row(X, t), mean[:, ds(t, 1)], rstd[:, ds(t, 1)], ALU.subtract, ALU.mult)

        def product(pe, t, u, hT):
            for m in range(HC):
                mm = pe.matmul(ps[6 + u][:, 0:NE], hT[:, m, :], wg[:, m, :], start=(m == 0), stop=(m == HC - 1))
            return mm

        def consume(dve, t, slot, lap, signal):
            signal(dve.tensor_tensor(row(gates, t), ps[6 + slot % 2][:, 0:NE], bg[:, :], ALU.add))

        programs = hidden(g, c2, "fa_", NT, stage, product, consume)

        def vector(dve):
            norm_vector(dve)
            dve.wait_ge(w_loaded, 64)
            programs["vector"](dve)

        def scalar(act):
            norm_scalar(act)
            act.wait_ge(w_loaded, 64)
            programs["scalar"](act)

        def sync(sp):
            sp.dma_start(w1[:, :, :], g["L1_ffn_W1"].rearrange("(k p) n -> p k n", p=P)).then_inc(w_loaded, 16)
            with nc.allow_non_contiguous_dma(reason="1024 numbers"):
                sp.dma_start(b1[:, :], g["L1_ffn_b1"].rearrange("(m p) -> p m", p=P)).then_inc(w_loaded, 16)
            sp.dma_start(wg[:, :, :], g["L1_ffn_Wg"].rearrange("(m p) e -> p m e", p=P)).then_inc(w_loaded, 16)
            sp.dma_start(bg[:, :], g["L1_ffn_bg"].rearrange("(a e) -> a e", a=1).broadcast_to([P, NE])).then_inc(w_loaded, 16)
            sp.wait_ge(w_loaded, 64)
            for e in range(NE):
                sp.dma_start(wd[:, e, :, :], g["L1_ffn_Wd"][e].rearrange("(m p) d -> p m d", p=P)).then_inc(w_loaded, 16)
            sp.dma_start(bd[:, :, :].rearrange("p e d -> p (e d)"), g["L1_ffn_bd"].rearrange("(a e) d -> a (e d)", a=1).broadcast_to([P, NE * D])).then_inc(w_loaded, 16)
            sp.wait_ge(w_loaded, 64 + 16 * (NE + 1))

        run_block(nc, {"sync": sync, "vector": vector, "scalar": scalar, "tensor": programs["tensor"]})

    with ExitStack() as c2:
        NB = NE + 1
        top = sb("rt_top", [P, NT], F32, c2)
        tot = sb("rt_tot", [P, NT], F32, c2)
        cand = sb("rt_cand", [P, NT, NE], F32, c2)
        extra = sb("rt_extra", [P, NT, 5], F32, c2)
        pad = sb("rt_pad", [P, NT], F32, c2)
        mask = sb("rt_mask", [P, NT], F32, c2)
        mask_u = sb("rt_mask_u", [P, NT], U32, c2)
        count = sb("rt_count", [P, NB], F32, c2)
        total = sb("rt_total", [P, NB], F32, c2)
        upto_b = sb("rt_upto", [P, NB], F32, c2)
        base = sb("rt_base", [P, NB], F32, c2)
        border_i = sb("rt_border_i", [P, NB], I32, c2)
        border = sb("rt_border", [P, NB], F32, c2)
        rank = sb("rt_rank", [P, NT], F32, c2)
        pos = sb("rt_pos", [P, NT], F32, c2)
        pos_u = sb("rt_pos_u", [P, NT], U32, c2)
        steps_i = sb("rt_steps_i", [P, 2, 64], I32, c2)
        steps_f = sb("rt_steps_f", [P, 64], F32, c2)
        hit = sb("rt_hit", [P, 64], F32, c2)
        ring = sb("rt_ring", [P, 2, XW], F32, c2)
        ring_pos = sb("rt_ring_pos", [P, 2, 1], U32, c2)
        own, exp_in, exp_out, counted, totals, pos_ready, ring_ready, ring_at, steps_ready, tables_in = (
            sem("rt_" + n) for n in ("own", "exp_in", "exp_out", "counted", "totals", "pos_ready", "ring_ready", "ring_at",
                                     "steps_ready", "tables_in"))
        scattered = [sem(f"rt_scattered{u}") for u in range(2)]
        pool_passed = sem("rt_pool_passed")

        def vector(dve):
            ch = Chain(dve, own)
            ch.link(dve.tensor_reduce(top[:, :], gates[:, :, :], AX.X, ALU.max))
            dve.tensor_tensor(gates[:, :, :], gates[:, :, :], top[:, :].unsqueeze(2).broadcast_to([P, NT, NE]), ALU.subtract).then_inc(exp_in, 1)
            dve.wait_ge(exp_out, 1)
            ch.link(dve.tensor_reduce(tot[:, :], gates[:, :, :], AX.X, ALU.add))
            ch.link(dve.reciprocal(extra[:, :, 0], tot[:, :]))
            ch.link(dve.tensor_scalar(cand[:, :, :], gates[:, :, :], 1.0, float(NB), ALU.is_lt, ALU.mult))
            ch.link(dve.tensor_tensor(cand[:, :, :], cand[:, :, :], g["iota_row"][:, 0:NE].unsqueeze(1).broadcast_to([P, NT, NE]), ALU.add))
            ch.link(dve.tensor_reduce(extra[:, :, 1], cand[:, :, :], AX.X, ALU.min))
            ch.link(dve.tensor_scalar(extra[:, :, 2], g["iota_row"][:, 0:NT], float(P), None, ALU.mult))
            ch.link(dve.tensor_scalar(extra[:, :, 2], extra[:, :, 2], g["iota_part"][:, 0:1], None, ALU.add))
            ch.link(dve.tensor_scalar(pad[:, :], extra[:, :, 2], float(N), float(NE), ALU.is_ge, ALU.mult))
            ch.link(dve.tensor_tensor(extra[:, :, 1], extra[:, :, 1], pad[:, :], ALU.max))
            ch.step(dve.tensor_copy(extra[:, :, 3], mean[:, :]))
            ch.step(dve.tensor_copy(extra[:, :, 4], rstd[:, :]))
            for b in range(NB):
                ch.link(dve.tensor_scalar(mask[:, :], extra[:, :, 1], float(b), 0.0, ALU.is_equal, ALU.add, accum_out=count[:, b:b + 1]))
            dve.sem_inc(counted, 1)
            dve.wait_ge(totals, 1)
            ch.link(dve.tensor_copy(total[:, :], ps[0][:, 0:NB]))
            ch.link(dve.tensor_tensor_scan(upto_b[:, :], total[:, :], total[:, :], 0.0, ALU.add, ALU.bypass))
            ch.link(dve.tensor_tensor(upto_b[:, :], upto_b[:, :], total[:, :], ALU.subtract))
            ch.link(dve.scalar_tensor_tensor(out=base[:, :], in0=ps[1][:, 0:NB], scalar=-1.0, in1=upto_b[:, :], op0=ALU.add, op1=ALU.add))
            ch.link(dve.memset(pos[:, :], 0.0))
            for b in range(NB):
                ch.link(dve.tensor_scalar(mask_u[:, :], extra[:, :, 1], float(b), None, ALU.is_equal))
                ch.link(dve.tensor_tensor_scan(rank[:, :], mask_u[:, :], mask_u[:, :], base[:, b:b + 1], ALU.add, ALU.bypass))
                ch.link(dve.copy_predicated(pos[:, :], mask_u[:, :], rank[:, :]))
            dve.tensor_copy(pos_u[:, :], pos[:, :]).then_inc(pos_ready, 1)
            ch.link(dve.tensor_copy(border_i[:, :], upto_b[:, :]))
            ch.link(dve.tensor_scalar(border_i[:, :], border_i[:, :], 7, None, ALU.logical_shift_right))
            ch.link(dve.tensor_copy(border[:, :], border_i[:, :]))
            ch.link(dve.tensor_tensor(border[:, :], border[:, :], g["iota_row"][:, 0:NB], ALU.add))
            ch.link(dve.memset(expert_of[:, :], 0.0))
            for b in range(1, NE):
                ch.link(dve.tensor_scalar(hit[:, :], g["iota_row"][:, 0:64], border[:, b:b + 1], None, ALU.is_ge))
                ch.link(dve.tensor_tensor(expert_of[:, :], expert_of[:, :], hit[:, :], ALU.add))
            ch.link(dve.tensor_tensor(steps_f[:, :], g["iota_row"][:, 0:64], expert_of[:, :], ALU.subtract))
            ch.link(dve.tensor_copy(steps_i[:, 0, :], steps_f[:, :]))
            ch.link(dve.tensor_copy(steps_i[:, 1, :], expert_of[:, :]))
            ch.link(dve.tensor_scalar(steps_i[:, 0, :], steps_i[:, 0, :], P, None, ALU.mult))
            ch.link(dve.tensor_copy(step_tables[:, :, :], steps_i[0:1, :, :]))
            dve.sem_inc(steps_ready, 1)
            start = ch.n
            for i in rounds_of(dve, NT // 2):
                for u in range(2):
                    t = i * 2 + u
                    wait_from(dve, scattered[u], i * 16)
                    dve.tensor_copy(ring[:, u, 0:D], row(X, t)).then_inc(ring_ready, 1)
                    dve.tensor_copy(ring[:, u, D:XW], row(extra, t)).then_inc(ring_ready, 1)

        def scalar(act):
            act.wait_ge(exp_in, 1)
            act.activation(gates[:, :, :], gates[:, :, :], ACT.Exp).then_inc(exp_out, 1)

        def tensor(pe):
            pe.wait_ge(counted, 1)
            pe.matmul(ps[0][:, 0:NB], g["ones"][:, :], count[:, :], start=True, stop=True)
            pe.matmul(ps[1][:, 0:NB], g["before"][:, :], count[:, :], start=True, stop=True).then_inc(totals, 1)

        def gpsimd(pool):
            pool.wait_ge(pos_ready, 1)
            for i in rounds_of(pool, NT // 2):
                for u in range(2):
                    t = i * 2 + u
                    wait_apart(pool, scattered[u], i * 16, pool_passed)
                    pool.tensor_copy(ring_pos[:, u, :], pos_u[:, ds(t, 1)]).then_inc(ring_at, 1)
                    wait_apart(pool, ring_at, t + 1, pool_passed)
                    wait_apart(pool, ring_ready, t * 2 + 2, pool_passed)
                    pool.indirect_dma_start(out=routed_rows[:, :], out_offset=bass.IndirectOffsetOnAxis(ap=ring_pos[:, u, :], axis=0),
                                            in_=ring[:, u, :], in_offset=None).then_inc(scattered[u], 16)
            for u in range(2):
                pool.wait_ge(scattered[u], 16 * (NT // 2))

        run_block(nc, {"vector": vector, "scalar": scalar, "tensor": tensor, "gpsimd": gpsimd})

    with ExitStack() as c2:
        xr = sb("ex_rows", [P, 4, XW], F32, c2)
        result = sb("ex_result", [P, 2, D], F32, c2)
        target = sb("ex_target", [P, 2, 1], F32, c2)
        target_u = sb("ex_target_u", [P, 4, 1], U32, c2)
        own, result_ready, target_ready = (sem("ex_" + n) for n in ("own", "result_ready", "target_ready"))
        loaded = [sem(f"ex_loaded{k}") for k in range(4)]
        scattered = [sem(f"ex_scattered{u}") for u in range(2)]
        pool_passed = sem("ex_pool_passed")

        def pair_of(slot, lap):
            return lap * 2 + slot // 2

        def stage(dve, t, slot, lap, to):
            wait_from(dve, loaded[slot], (lap + 1) * 16)
            return dve.tensor_scalar(to, xr[:, slot, 0:D], xr[:, slot, D + 3:D + 4], xr[:, slot, D + 4:D + 5], ALU.subtract, ALU.mult)

        def product(pe, t, u, hT):
            e = pe.value_load(step_tables[0:1, 1, ds(t, 1)], min_val=0, max_val=NE - 1)
            for m in range(HC):
                w = wd[:, ds(e, 1), m, :].rearrange("p a d -> p (a d)")
                mm = pe.matmul(ps[6 + u][:, 0:D], hT[:, m, :], w, start=(m == 0), stop=(m == HC - 1))
            return mm

        def consume(dve, t, slot, lap, signal):
            u = slot % 2
            ch = Chain(dve, own, t * 3)
            e = dve.value_load(step_tables[0:1, 1, ds(t, 1)], min_val=0, max_val=NE - 1)
            ch.link(dve.tensor_scalar(target[:, u, :], xr[:, slot, D + 1:D + 2], expert_of[:, ds(t, 1)], float(NT * P), ALU.not_equal, ALU.mult))
            ch.link(dve.tensor_tensor(target[:, u, :], target[:, u, :], xr[:, slot, D + 2:D + 3], ALU.add))
            ch.link(dve.tensor_copy(target_u[:, slot, :], target[:, u, :]))
            wait_from(dve, scattered[u], pair_of(slot, lap) * 16)
            signal(dve.tensor_tensor(result[:, u, :], ps[6 + u][:, 0:D], bd[:, ds(e, 1), :].rearrange("p a d -> p (a d)"), ALU.add))
            wait_from(dve, programs["taken"], t + 1)
            dve.scalar_tensor_tensor(out=result[:, u, :], in0=result[:, u, :], scalar=xr[:, slot, D:D + 1], in1=xr[:, slot, 0:D],
                                     op0=ALU.mult, op1=ALU.add).then_inc(result_ready, 1)

        programs = hidden(g, c2, "fb_", ESTEPS, stage, product, consume)

        def sync(sp):
            def body(t, slot, lap):
                wait_from(sp, result_ready, t - 2)
                first = sp.value_load(step_tables[0:1, 0, ds(t, 1)], min_val=0, max_val=(NT - 1) * P)
                sp.dma_start(xr[:, slot, :], routed_rows[ds(first, P), :]).then_inc(loaded[slot], 16)
            laps(sp, body, ESTEPS)

        def gpsimd(pool):
            def body(t, slot, lap):
                wait_apart(pool, result_ready, t + 2, pool_passed)
                pool.indirect_dma_start(out=out[:, :], out_offset=bass.IndirectOffsetOnAxis(ap=target_u[:, slot, :], axis=0),
                                        in_=result[:, slot % 2, :], in_offset=None, bounds_check=N - 1, oob_is_err=False).then_inc(scattered[slot % 2], 16)
            laps(pool, body, ESTEPS)
            for u in range(2):
                pool.wait_ge(scattered[u], 16 * (ESTEPS // 2))

        def vector(dve):
            dve.sem_inc(result_ready, 1)
            hidden_vector(dve)

        hidden_vector = programs["vector"]
        programs = {**programs, "vector": vector, "sync": sync, "gpsimd": gpsimd}
        run_block(nc, programs)


INPUTS = ["x", "src", "dst", "L0_gnn_W", "L0_gnn_envW", "L0_gnn_envb", "L0_ffn_W_fx", "L0_ffn_b_fx", "L0_ffn_W_x", "L0_ffn_b_x",
          "L0_ffn_W_slice", "L0_ffn_b_slice", "L0_ffn_W_q", "L0_ffn_W_k", "L0_ffn_W_v", "L0_ffn_W_out", "L0_ffn_b_out",
          "L0_ffn_temperature", "L1_gnn_W", "L1_gnn_a_src", "L1_gnn_a_dst", "L1_ffn_W1", "L1_ffn_b1", "L1_ffn_Wg", "L1_ffn_bg",
          "L1_ffn_Wd", "L1_ffn_bd"]


def kernel(**inputs):
    import numpy as np
    import concourse.bacc as bacc
    from concourse.bass_utils import run_bass_kernel_spmd

    nc = bacc.Bacc("TRN2", target_bir_lowering=False, num_devices=1)
    arrays, args = {}, {}
    for name in INPUTS:
        arrays[f"in_{name}"] = a = np.ascontiguousarray(inputs[name])
        args[name] = nc.dram_tensor(f"in_{name}", a.shape, mybir.dt.from_np(a.dtype), kind="ExternalInput").ap()
    out = nc.dram_tensor("out", (N, D), F32, kind="ExternalOutput").ap()
    build(nc, out, **args)
    result = run_bass_kernel_spmd(nc, [arrays], core_ids=[0])
    return result.results[0]["out"]
```

```python
import concourse.bass as bass
from concourse import mybir
from concourse.alu_op_type import AluOpType as ALU
from contextlib import ExitStack

ACT = mybir.ActivationFunctionType
AX = mybir.AxisListType
F32 = mybir.dt.float32
BF16 = mybir.dt.bfloat16
U16 = mybir.dt.uint16
I32 = mybir.dt.int32
U32 = mybir.dt.uint32

P = 128
N = 6250
D = 256
E = 100000
NT = 50
NFULL = N // P
NREST = N - NFULL * P
LASTT = NFULL
COLS = 784
EPAD = P * COLS
EREST = E - (P - 1) * COLS
PADKEY = 49 * P
STEPS = 832
GROUPS = 7
SG = GROUPS * P
K0 = 4
HALF = 8
FAR = 1e30
ds = bass.ds


class Chain:

    def __init__(self, eng, sem, at=0):
        self.eng, self.sem, self.at, self.n = eng, sem, at, 0

    def step(self, ins):
        ins.then_inc(self.sem, 1)
        self.n += 1
        return ins

    def wait(self):
        self.eng.wait_ge(self.sem, self.at + self.n)

    def link(self, ins):
        self.step(ins)
        self.wait()
        return ins

    def enter(self, at):
        self.at, self.n = at, 0


def build(nc, out, *, x, src, dst, L0_gnn_W, L0_gnn_envW, L0_gnn_envb, L0_ffn_W_fx, L0_ffn_b_fx, L0_ffn_W_x,
          L0_ffn_b_x, L0_ffn_W_slice, L0_ffn_b_slice, L0_ffn_W_q, L0_ffn_W_k, L0_ffn_W_v, L0_ffn_W_out,
          L0_ffn_b_out, L0_ffn_temperature, L1_gnn_W, L1_gnn_a_src, L1_gnn_a_dst, L1_ffn_W1, L1_ffn_b1,
          L1_ffn_Wg, L1_ffn_bg, L1_ffn_Wd, L1_ffn_bd):
    with ExitStack() as top:
        stage_sems = []

        def sem(name):
            stage_sems.append(nc.alloc_semaphore(name=name))
            return stage_sems[-1]

        def stage_ends():
            nc.clear_and_free_semaphores(stage_sems)
            stage_sems.clear()
            nc.all_engine_barrier()

        def sb(name, shape, dt=F32, ctx=top):
            return ctx.enter_context(nc.sbuf_tensor(name, shape, dt))

        z_rows = [nc.dram_tensor(f"z_rows{l}", [NT * P, D], F32) for l in range(2)]
        pairs = [nc.dram_tensor(f"pairs_{q}", [EPAD, 2], I32) for q in ("src", "dst")]
        tile_of_step_dram = nc.dram_tensor("tile_of_step_dram", [2, SG], I32)

        key_by_dst = nc.dram_tensor("key_by_dst", [P, SG], F32)
        row_by_dst = nc.dram_tensor("row_by_dst", [P, SG], U32)

        cuts_dram = nc.dram_tensor("cuts_dram", [2, SG * P], F32)
        ends_dram = nc.dram_tensor("ends_dram", [2, SG + 2], F32)

        X = sb("X", [P, NT, D])
        iota_row = sb("iota_row", [P, P])
        iota_part = sb("iota_part", [P, 1])
        step_index = sb("step_index", [P, GROUPS])
        ident = sb("ident", [P, P])
        before = sb("before", [P, P])
        ones = sb("ones", [P, P])
        eps_ln = sb("eps_ln", [P, 1])
        banks01 = top.enter_context(nc.psum_tensor("banks01", [P, 1024], F32))
        ps = [banks01[:, 0:512], banks01[:, 512:1024]] + [
            top.enter_context(nc.psum_tensor(f"bank{b}", [P, 512], F32)) for b in range(2, 8)]

        g = dict(locals())
        constants(g)
        graph_mixture(g)
        stage_ends()
        with ExitStack() as c:
            slice_attention(g, c)
        stage_ends()
        with ExitStack() as c:
            graph_attention(g, c)
        stage_ends()
        with ExitStack() as c:
            routed_network(g, c, out)


def graph_mixture(g):
    nc, sb = g["nc"], g["sb"]
    with ExitStack() as c1:
        g["local_key"] = sb("local_key", [P, SG], ctx=c1)
        g["row_of"] = sb("row_of", [P, SG], U32, c1)
        g["tile_of"] = sb("tile_of", [1, SG], I32, c1)
        g["Z"] = sb("Z", [P, NT, D], ctx=c1)
        g["mix"] = sb("mix", [P, NT, K0], ctx=c1)
        with ExitStack() as c2:
            edge_tables(g, c2)
        with ExitStack() as c3:
            g["A"] = sb("A", [P, NT, D + 1], ctx=c3)
            for layer in range(2):
                if layer == 1:
                    with ExitStack() as c4:
                        run_block(nc, mixture(g, c4, layer, "own"))
                with ExitStack() as c4:
                    run_block(nc, gather_sum(g, c4, layer))
                with ExitStack() as c4:
                    run_block(nc, mixture(g, c4, layer, "agg"))


def constants(g):
    nc, X, sem, sb = g["nc"], g["X"], g["sem"], g["sb"]
    x_loaded, const_made, iota_made, own = (sem(n) for n in ("x_loaded", "const_made", "iota_made", "const_own"))
    with ExitStack() as c:
        irow = sb("irow", [P, P], I32, c)
        ipart = sb("ipart", [P, 1], I32, c)
        istep = sb("istep", [P, GROUPS], I32, c)
        block = c.enter_context(nc.Block())

        @block.gpsimd
        def _(pool):
            nc.gpsimd.iota(irow[:, :], [[1, P]], base=0, channel_multiplier=0).then_inc(iota_made, 1)
            nc.gpsimd.iota(ipart[:, :], [[0, 1]], base=0, channel_multiplier=1).then_inc(iota_made, 1)
            nc.gpsimd.iota(istep[:, :], [[P, GROUPS]], base=0, channel_multiplier=1).then_inc(iota_made, 1)

        @block.vector
        def _(dve):
            ch = Chain(dve, own)
            dve.memset(X[:, LASTT:NT, :], 0.0).then_inc(const_made, 1)
            dve.memset(g["ones"][:, :], 1.0)
            dve.memset(g["eps_ln"][:, :], 1e-5)
            dve.wait_ge(iota_made, 3)
            ch.step(dve.tensor_copy(g["iota_row"][:, :], irow[:, :]))
            ch.step(dve.tensor_copy(g["iota_part"][:, :], ipart[:, :]))
            dve.tensor_copy(g["step_index"][:, :], istep[:, :])
            ch.wait()
            dve.tensor_scalar(g["ident"][:, :], g["iota_row"][:, :], g["iota_part"][:, 0:1], None, ALU.is_equal)
            dve.tensor_scalar(g["before"][:, :], g["iota_row"][:, :], g["iota_part"][:, 0:1], None, ALU.is_gt)

        @block.sync
        def _(sp):
            sp.dma_start(X[:, 0:NFULL, :], g["x"][0:NFULL * P, :].rearrange("(t p) d -> p t d", p=P)).then_inc(x_loaded, 16)
            sp.wait_ge(const_made, 1)
            sp.dma_start(X[0:NREST, LASTT, :], g["x"][NFULL * P:N, :]).then_inc(x_loaded, 16)
            sp.wait_ge(x_loaded, 32)


def edge_tables(g, c):
    nc, sb, sem, ps, X = g["nc"], g["sb"], g["sem"], g["ps"], g["X"]
    ones, before, ident, iota_row = g["ones"], g["before"], g["ident"], g["iota_row"]
    keys = [sb(f"keys{q}", [P, COLS], I32, c) for q in range(2)]
    bucket_i = sb("bucket_i", [P, COLS], I32, c)
    bucket = [sb(f"bucket{q}", [P, COLS], BF16, c) for q in range(2)]
    mask = sb("mask", [P, 2, COLS], U16, c)
    rank = sb("rank", [P, 2, COLS], F32, c)
    pos = sb("pos", [P, COLS], F32, c)
    pos_u = sb("pos_u", [P, COLS], U32, c)
    pay = [sb(f"pay{q}", [P, COLS, 2], I32, c) for q in range(2)]
    count = sb("count", [P, 2, NT], F32, c)
    total = sb("total", [P, 2, NT], F32, c)
    upto_b = sb("upto_b", [P, 2, NT], F32, c)
    first = sb("first", [P, 2, NT], F32, c)
    base = sb("base", [P, NT], F32, c)
    first_i = sb("first_i", [P, 2, NT], I32, c)
    border = sb("border", [P, 2, NT], F32, c)
    ring_pos = sb("ring_pos", [P, 2, HALF], U32, c)
    ring_pay = sb("ring_pay", [P, 2, HALF, 2], I32, c)
    stats = sb("stats", [P, NT, 6], F32, c)
    edges_loaded, cleared, counted, totals_ready, pos_ready, pay_ready, own, pool_own = (
        sem(n) for n in ("edges_loaded", "cleared", "counted", "totals_ready", "pos_ready", "pay_ready", "tab_own",
                         "tab_pool_own"))
    scattered = [sem(f"scattered{h}") for h in range(2)]
    pool_passed = sem("tab_pool_passed")
    dst_stored = sem("dst_stored")
    per_half = COLS // (2 * HALF)

    mix0 = mixture(g, c, 0, "own")
    with nc.Block() as block:
        @block.scalar
        def _(act):
            mix0["scalar"](act)

        @block.sync
        def _(sp):
            sp.wait_ge(cleared, 2)
            for q, a in enumerate((g["src"], g["dst"])):
                sp.dma_start(keys[q][0:P - 1, :], a[0:(P - 1) * COLS].rearrange("(p j) -> p j", j=COLS)).then_inc(edges_loaded, 16)
                sp.dma_start(keys[q][P - 1:P, 0:EREST], a[(P - 1) * COLS:E].rearrange("(p j) -> p j", p=1)).then_inc(edges_loaded, 16)
            sp.wait_ge(pay_ready, 4)
            sp.dma_start(g["pairs"][1][:, :].rearrange("(p j) w -> p (j w)", p=P), pay[1][:, :, :].rearrange("p j w -> p (j w)")).then_inc(dst_stored, 16)
            mix0["sync"](sp)
            sp.wait_ge(dst_stored, 16)

        @block.vector
        def _(dve):
            ch = Chain(dve, own)
            for q in range(2):
                dve.memset(keys[q][:, :], PADKEY).then_inc(cleared, 1)
            dve.memset(pos[:, :], 0.0)
            dve.wait_ge(edges_loaded, 64)
            for q in range(2):
                ch.link(dve.tensor_scalar(bucket_i[:, :], keys[q][:, :], 7, None, ALU.logical_shift_right))
                ch.link(dve.tensor_copy(bucket[q][:, :], bucket_i[:, :]))
            for b in rounds_of(dve, NT):
                for q in range(2):
                    wait_from(dve, counted, b * 2 + q)
                    dve.tensor_scalar(mask[:, q, :], bucket[q][:, :], iota_row[:, ds(b, 1)], 0.0, ALU.is_equal, ALU.add,
                                      accum_out=count[:, q, ds(b, 1)]).then_inc(counted, 1)
            dve.wait_ge(totals_ready, 1)
            for q in range(2):
                ch.step(dve.tensor_copy(total[:, q, :], ps[0][:, q * NT:(q + 1) * NT]))
            ch.wait()
            for q in range(2):
                ch.step(dve.tensor_tensor_scan(upto_b[:, q, :], total[:, q, :], total[:, q, :], 0.0, ALU.add, ALU.bypass))
            ch.wait()
            ch.link(dve.tensor_tensor(first[:, :, :], upto_b[:, :, :], total[:, :, :], ALU.subtract))
            ch.link(dve.scalar_tensor_tensor(out=base[:, :], in0=ps[1][:, 0:NT], scalar=-1.0, in1=first[:, 0, :], op0=ALU.add, op1=ALU.add))
            per_b, start = 4, ch.n
            with dve.Fori(0, NT) as b:
                ch.enter(b * per_b + start)
                ch.link(dve.tensor_scalar(mask[:, 0, :], bucket[0][:, :], iota_row[:, ds(b, 1)], None, ALU.is_equal))
                ch.link(dve.tensor_tensor_scan(rank[:, 0, :], mask[:, 0, :], mask[:, 0, :], base[:, ds(b, 1)], ALU.add, ALU.bypass))
                ch.link(dve.tensor_tensor(rank[:, 0, :], rank[:, 0, :], mask[:, 0, :], ALU.mult))
                ch.link(dve.tensor_tensor(pos[:, :], pos[:, :], rank[:, 0, :], ALU.add))
            ch.enter(NT * per_b + start)
            for q in range(2):
                for w in range(2):
                    dve.tensor_copy(pay[q][:, :, w], keys[(q + w) % 2][:, :]).then_inc(pay_ready, 1)
            dve.tensor_copy(pos_u[:, :], pos[:, :]).then_inc(pos_ready, 1)
            ch.link(dve.tensor_copy(first_i[:, :, :], first[:, :, :]))
            ch.link(dve.tensor_scalar(first_i[:, :, :], first_i[:, :, :], 7, None, ALU.logical_shift_right))
            ch.link(dve.tensor_copy(border[:, :, :], first_i[:, :, :]))
            for q in range(2):
                ch.link(dve.tensor_tensor(border[:, q, :], border[:, q, :], iota_row[:, 0:NT], ALU.add))
            mix0["vector"](dve)

        @block.tensor
        def _(pe):
            pe.wait_ge(counted, 2 * NT)
            pe.matmul(ps[0][:, 0:2 * NT], ones[:, :], count[:, :, :].rearrange("p q b -> p (q b)"), start=True, stop=True)
            pe.matmul(ps[1][:, 0:NT], before[:, :], count[:, 0, :], start=True, stop=True).then_inc(totals_ready, 1)
            mix0["tensor"](pe)

        @block.gpsimd
        def _(pool):
            pool.wait_ge(pos_ready, 1)
            pool.wait_ge(pay_ready, 2)
            for i in rounds_of(pool, per_half):
                for h in range(2):
                    j = i * (2 * HALF) + h * HALF
                    wait_apart(pool, scattered[h], i * (16 * HALF), pool_passed)
                    pool.tensor_copy(ring_pos[:, h, :], pos_u[:, ds(j, HALF)]).then_inc(pool_own, 1)
                    pool.tensor_copy(ring_pay[:, h, :, :], pay[0][:, ds(j, HALF), :]).then_inc(pool_own, 1)
                    wait_apart(pool, pool_own, i * 4 + 2 * h + 2, pool_passed)
                    for k in range(HALF):
                        pool.indirect_dma_start(
                            out=g["pairs"][0][:, :], out_offset=bass.IndirectOffsetOnAxis(ap=ring_pos[:, h, k:k + 1], axis=0),
                            in_=ring_pay[:, h, k, :], in_offset=None).then_inc(scattered[h], 16)
            for h in range(2):
                pool.wait_ge(scattered[h], per_half * 16 * HALF)

    local_key = [g["local_key"], sb("local_key1", [P, SG], F32, c)]
    row_of = [g["row_of"], sb("row_of1", [P, SG], U32, c)]
    tile_f = sb("tile_f", [P, 2, GROUPS], F32, c)
    tile_i = sb("tile_i", [2 * GROUPS, P], I32, c)
    tile_key = sb("tile_key", [P, 2, GROUPS], F32, c)
    chunk_f = sb("chunk_f", [P, 2, GROUPS], F32, c)
    chunk_u = sb("chunk_u", [P, 2 * GROUPS], U32, c)
    scratch = sb("scratch", [P, NT], F32, c)
    rows = sb("rows", [P, 4, P, 2], I32, c)
    rows_f = sb("rows_f", [P, 2, 2, P], F32, c)
    ends = sb("ends", [P, GROUPS, 2], F32, c)
    beside = sb("beside", [P, GROUPS, 2], F32, c)
    outside = sb("outside", [1, 2], F32, c)
    cuts = sb("cuts", [P, GROUPS, 2, P], F32, c)
    cuts_made, ends_made, ends_out, beside_in, cuts_ready = (
        sem(n) for n in ("cuts_made", "ends_made", "ends_out", "beside_in", "cuts_ready"))
    chunk_ready, rows_loaded, rows_used, rows_made, turned, taken, own2, tiles_out, tiles_in = (
        sem(n) for n in ("chunk_ready", "rows_loaded", "rows_used", "rows_made", "turned", "taken", "tab_own2",
                         "tiles_out", "tiles_in"))
    tiles_turned = sem("tiles_turned")
    rows_at = [sem(f"rows_at{k}") for k in range(4)]
    n2 = 2 * GROUPS
    with nc.Block() as block:
        @block.gpsimd
        def _(pool):
            pool.wait_ge(chunk_ready, 1)
            for k in range(n2):
                q = k // GROUPS
                if k >= 4:
                    pool.wait_ge(rows_used, k - 3)
                pool.indirect_dma_start(
                    out=rows[:, k % 4, :, :].rearrange("p e w -> p (e w)"), out_offset=None,
                    in_=g["pairs"][q][:, :].rearrange("(c e) w -> c (e w)", e=P),
                    in_offset=bass.IndirectOffsetOnAxis(ap=chunk_u[:, k:k + 1], axis=0)).then_inc(rows_at[k % 4], 16)

        @block.vector
        def _(dve):
            ch = Chain(dve, own2)
            dve.memset(outside[:, :], -1.0).then_inc(ends_made, 1)
            for q in range(2):
                for s in range(GROUPS):
                    ch.link(dve.tensor_scalar(scratch[:, 0:48], border[:, q, 1:49], g["step_index"][:, s:s + 1], 0.0, ALU.is_le,
                                              ALU.add, accum_out=tile_f[:, q, s:s + 1]))
            for q in range(2):
                ch.link(dve.tensor_tensor(chunk_f[:, q, :], g["step_index"][:, :], tile_f[:, q, :], ALU.subtract))
            ch.link(dve.tensor_scalar_min(chunk_f[:, :, :], chunk_f[:, :, :], float(COLS - 1)))
            dve.tensor_copy(chunk_u[:, :], chunk_f[:, :, :].rearrange("p q s -> p (q s)")).then_inc(chunk_ready, 1)
            dve.wait_ge(tiles_turned, 1)
            dve.tensor_copy(tile_i[:, :], ps[4][0:n2, 0:P]).then_inc(chunk_ready, 1)
            ch.link(dve.tensor_scalar(tile_key[:, :, :], tile_f[:, :, :], float(P), None, ALU.mult))
            for k in range(n2):
                q, s = k // GROUPS, k % GROUPS
                dve.wait_ge(rows_at[k % 4], 16 * (k // 4 + 1))
                if k >= 2:
                    dve.wait_ge(turned, k - 1)
                dve.tensor_scalar(rows_f[:, k % 2, 0, :], rows[:, k % 4, :, 0], tile_key[:, q, s:s + 1], None,
                                  ALU.subtract).then_inc(rows_made, 1)
                dve.tensor_copy(rows_f[:, k % 2, 1, :], rows[:, k % 4, :, 1]).then_inc(rows_made, 1)
                if q == 1:
                    dve.tensor_copy(ends[:, s, :], rows[:, k % 4, 0:P:P - 1, 0]).then_inc(ends_made, 1)
                    dve.wait_ge(ends_made, s + 2)
                dve.wait_ge(rows_made, 2 * k + 2)
                dve.sem_inc(rows_used, 1)
                if q == 1:
                    here, before_ = rows_f[:, k % 2, 0, 1:P], rows_f[:, k % 2, 0, 0:P - 1]
                    dve.tensor_tensor(cuts[:, s, 0, 1:P], here, before_, ALU.not_equal).then_inc(cuts_made, 1)
                    dve.tensor_tensor(cuts[:, s, 1, 0:P - 1], here, before_, ALU.not_equal).then_inc(cuts_made, 1)
                dve.wait_ge(turned, k + 1)
                dve.tensor_copy(local_key[q][:, s * P:(s + 1) * P], ps[2 * (k % 2)][:, 0:P])
                dve.tensor_copy(row_of[q][:, s * P:(s + 1) * P], ps[2 * (k % 2) + 1][:, 0:P]).then_inc(taken, 1)
            ch.wait()
            dve.wait_ge(beside_in, 32)
            dve.tensor_tensor(cuts[:, :, 0, 0], ends[:, :, 0], beside[:, :, 0], ALU.not_equal).then_inc(cuts_made, 1)
            dve.tensor_tensor(cuts[:, :, 1, P - 1], ends[:, :, 1], beside[:, :, 1], ALU.not_equal).then_inc(cuts_made, 1)
            dve.wait_ge(cuts_made, 2 * GROUPS + 2)
            dve.tensor_scalar(cuts[:, :, :, :], cuts[:, :, :, :], -FAR, None, ALU.mult).then_inc(cuts_ready, 1)

        @block.tensor
        def _(pe):
            pe.wait_ge(chunk_ready, 1)
            pe.transpose(ps[4][0:n2, 0:P], tile_f[:, :, :].rearrange("p q s -> p (q s)"), ident[:, :]).then_inc(tiles_turned, 1)
            for k in range(n2):
                pe.wait_ge(rows_made, 2 * k + 2)
                if k >= 2:
                    pe.wait_ge(taken, k - 1)
                pe.transpose(ps[2 * (k % 2)][:, 0:P], rows_f[:, k % 2, 0, :], ident[:, :])
                pe.transpose(ps[2 * (k % 2) + 1][:, 0:P], rows_f[:, k % 2, 1, :], ident[:, :]).then_inc(turned, 1)

        @block.sync
        def _(sp):
            sp.wait_ge(chunk_ready, 2)
            sp.dma_start(g["tile_of_step_dram"][:, :].rearrange("q (s p) -> (q s) p", p=P), tile_i[:, :]).then_inc(tiles_out, 16)
            sp.wait_ge(tiles_out, 16)
            sp.dma_start(g["tile_of"][:, :], g["tile_of_step_dram"][0:1, :]).then_inc(tiles_in, 16)
            sp.wait_ge(taken, n2)
            sp.dma_start(g["key_by_dst"][:, :], local_key[1][:, :]).then_inc(tiles_in, 16)
            sp.dma_start(g["row_by_dst"][:, :], row_of[1][:, :]).then_inc(tiles_in, 16)
            sp.wait_ge(ends_made, GROUPS + 1)
            for a in range(2):
                sp.dma_start(g["ends_dram"][a:a + 1, 1:SG + 1].rearrange("a (s p) -> p (a s)", p=P), ends[:, :, a], allow_slow_non_contiguous=True).then_inc(ends_out, 16)
                sp.dma_start(g["ends_dram"][1 - a:2 - a, a * (SG + 1):a * (SG + 1) + 1], outside[:, a:a + 1]).then_inc(ends_out, 16)
            sp.wait_ge(ends_out, 64)
            for a in range(2):
                sp.dma_start(beside[:, :, a], g["ends_dram"][1 - a:2 - a, 2 * a:2 * a + SG].rearrange("a (s p) -> p (a s)", p=P), allow_slow_non_contiguous=True).then_inc(beside_in, 16)
            sp.wait_ge(cuts_ready, 1)
            for a in range(2):
                sp.dma_start(g["cuts_dram"][a:a + 1, :].rearrange("a (s p e) -> p (a s) e", p=P, e=P), cuts[:, :, a, :]).then_inc(tiles_in, 16)
            sp.wait_ge(tiles_in, 80)


def row_norm(g, c, name):
    nc, sb, sem, X = g["nc"], g["sb"], g["sem"], g["X"]
    stats = sb(name + "_stats", [P, NT, 6], F32, c)
    mean = sb(name + "_mean", [P, NT], F32, c)
    var = sb(name + "_var", [P, NT], F32, c)
    apart = sb(name + "_apart", [P, NT], F32, c)
    rstd = sb(name + "_rstd", [P, NT], F32, c)
    own, var_ready, std_ready = (sem(name + n) for n in ("_own", "_var_ready", "_std_ready"))

    def vector(dve):
        ch = Chain(dve, own)
        with dve.Fori(0, NT // 2) as i:
            for u in range(2):
                t = i * 2 + u
                dve.bn_stats(row(stats, t), row(X, t)).then_inc(own, 1)
        ch.enter(NT)
        ch.wait()
        ch.step(dve.tensor_tensor(mean[:, :], stats[:, :, 1], stats[:, :, 4], ALU.add))
        ch.step(dve.tensor_tensor(apart[:, :], stats[:, :, 1], stats[:, :, 4], ALU.subtract))
        ch.link(dve.tensor_tensor(var[:, :], stats[:, :, 2], stats[:, :, 5], ALU.add))
        ch.link(dve.tensor_scalar(mean[:, :], mean[:, :], 0.5, None, ALU.mult))
        ch.link(dve.tensor_tensor(apart[:, :], apart[:, :], apart[:, :], ALU.mult))
        ch.link(dve.tensor_scalar(apart[:, :], apart[:, :], 0.25, None, ALU.mult))
        dve.scalar_tensor_tensor(out=var[:, :], in0=var[:, :], scalar=1.0 / D, in1=apart[:, :], op0=ALU.mult, op1=ALU.add).then_inc(var_ready, 1)
        dve.wait_ge(std_ready, 1)
        ch.link(dve.reciprocal(rstd[:, :], rstd[:, :]))

    def scalar(act):
        act.wait_ge(var_ready, 1)
        act.activation(rstd[:, :], var[:, :], ACT.Sqrt, bias=g["eps_ln"][:, 0:1]).then_inc(std_ready, 1)

    return mean, rstd, vector, scalar


def rounds_of(eng, count):
    yield 0
    with eng.Fori(1, count) as i:
        yield i


def over_tiles(eng, ahead, now):
    ahead(0, 0, 0)
    for i in rounds_of(eng, NT // 2 - 1):
        ahead(i * 2 + 1, 1, i)
        now(i * 2, 0, i)
        ahead(i * 2 + 2, 0, i + 1)
        now(i * 2 + 1, 1, i)
    ahead(NT - 1, 1, NT // 2 - 1)
    now(NT - 2, 0, NT // 2 - 1)
    now(NT - 1, 1, NT // 2 - 1)


def wait_from(eng, sem, value):
    if not isinstance(value, int) or value > 0:
        eng.wait_ge(sem, value)


def wait_apart(eng, sem, value, passed):
    if isinstance(value, int) and value <= 0:
        return
    eng.wait_ge(sem, value)
    eng.sem_inc(passed, 1)


def row(a, t):
    return a[:, ds(t, 1), :].rearrange("p a d -> p (a d)")


def mixture(g, c, layer, part):
    nc, sb, sem, ps, X, Z, mix = (g[n] for n in ("nc", "sb", "sem", "ps", "X", "Z", "mix"))
    ident = g["ident"]
    own_part = part == "own"
    pre = f"{part}{layer}_"
    W0 = sb(pre + "W", [P, 2, K0, D], F32, c)
    stage = sb(pre + "stage", [P, 2, D], F32, c)
    zT = sb(pre + "zT", [P, 2, 2, P], F32, c)
    names = ("dve_ahead", "dve_now", "staged", "turned", "zt_ready", "products", "exp_in", "exp_out", "mixed", "w_loaded",
             "act_own")
    dve_ahead, dve_now, staged, turned, zt_ready, products, exp_in, exp_out, mixed, w_loaded, act_own = (
        sem(pre + n) for n in names)
    stored = [sem(pre + f"stored{u}") for u in range(2)]
    store_stage = own_part and layer == 0
    store_new = not own_part and layer == 0
    z_new = sb(pre + "z_new", [P, 2, D], F32, c) if not own_part else None
    new_ready = sem(pre + "new_ready")
    if own_part:
        envw = sb(pre + "envw", [P, 2, K0], F32, c)
        envb = sb(pre + "envb", [P, K0], F32, c)
        lg = sb(pre + "lg", [P, 2, K0], F32, c)
        ex = sb(pre + "ex", [P, 2, K0], F32, c)
        col = sb(pre + "col", [P, 2, 4], F32, c)
    if store_stage:
        mean, rstd, norm_vector, norm_scalar = row_norm(g, c, "ln0")
    if not own_part:
        per_count = sb(pre + "per_count", [P, NT], F32, c)
    first_chunk = 2 if own_part else 0

    def sync(sp):
        for k in range(K0):
            sp.dma_start(W0[:, :, k, :], g["L0_gnn_W"][layer, k].rearrange("(c p) d -> p c d", p=P)[:, first_chunk:first_chunk + 2, :]).then_inc(w_loaded, 16)
        if own_part:
            sp.dma_start(envw[:, :, :], g["L0_gnn_envW"][layer].rearrange("(c p) k -> p c k", p=P)).then_inc(w_loaded, 16)
            sp.dma_start(envb[:, :], g["L0_gnn_envb"][layer:layer + 1, :].broadcast_to([P, K0])).then_inc(w_loaded, 16)
        if store_stage or store_new:
            ready, what = (staged, stage) if store_stage else (new_ready, z_new)
            with sp.Fori(0, NT // 2) as i:
                for u in range(2):
                    wait_from(sp, ready, i * 2 + u + 1)
                    sp.dma_start(g["z_rows"][layer if store_stage else 1][ds((i * 2 + u) * P, P), :], what[:, u, :]).then_inc(stored[u], 16)
            for u in range(2):
                sp.wait_ge(stored[u], 16 * (NT // 2))

    def vector(dve):
        cha, chn = Chain(dve, dve_ahead), Chain(dve, dve_now)
        if store_stage:
            norm_vector(dve)
        if not own_part:
            cha.link(dve.tensor_scalar_max(per_count[:, :], g["A"][:, :, D], 1.0))
            cha.link(dve.reciprocal(per_count[:, :], per_count[:, :]))
        if own_part:
            dve.wait_ge(w_loaded, 16 * (K0 + 2))

        dve.sem_inc(mixed, 1)

        def ahead(t, u, pair):
            wait_from(dve, turned, t - 1)
            if store_stage:
                wait_from(dve, stored[u], pair * 16)
                dve.tensor_scalar(stage[:, u, :], row(X, t), mean[:, ds(t, 1)], rstd[:, ds(t, 1)], ALU.subtract,
                                  ALU.mult).then_inc(staged, 1)
            elif own_part:
                dve.tensor_scalar(stage[:, u, :], row(Z, t), 1.0, None, ALU.mult).then_inc(staged, 1)
            else:
                dve.tensor_scalar(stage[:, u, :], g["A"][:, ds(t, 1), 0:D].rearrange("p a d -> p (a d)"),
                                  per_count[:, ds(t, 1)], None, ALU.mult).then_inc(staged, 1)

        def now(t, u, pair):
            z = row(Z, t)
            wait_from(dve, products, t + 1)
            if own_part:
                chn.enter(t * 9)
                chn.link(dve.tensor_tensor(lg[:, u, :], ps[6 + u][:, 0:K0], envb[:, :], ALU.add))
                dve.tensor_reduce(col[:, u, 0:1], lg[:, u, :], AX.X, ALU.max, negate=True).then_inc(exp_in, 1)
                wait_from(dve, exp_out, t + 1)
                chn.link(dve.reciprocal(col[:, u, 2:3], col[:, u, 1:2]))
                chn.link(dve.tensor_scalar(ex[:, u, :], ex[:, u, :], col[:, u, 2:3], None, ALU.mult))
                chn.step(dve.tensor_scalar(row(mix, t), ex[:, u, :], 1.0, None, ALU.mult))
                chn.link(dve.tensor_reduce(col[:, u, 3:4], ex[:, u, :], AX.X, ALU.add))
                chn.link(dve.tensor_scalar(z, stage[:, u, :], col[:, u, 3:4], None, ALU.mult))
            else:
                chn.enter(t * 5)
            for k in range(K0):
                ins = dve.scalar_tensor_tensor(out=z, in0=ps[2 * u + k // 2][:, (k % 2) * D:(k % 2 + 1) * D],
                                               scalar=mix[:, ds(t, 1), k:k + 1].rearrange("p a k -> p (a k)"), in1=z,
                                               op0=ALU.mult, op1=ALU.add)
                if k == K0 - 1 and own_part:
                    ins.then_inc(mixed, 1)
                else:
                    chn.link(ins)
            if not own_part:
                if layer == 0:
                    wait_from(dve, stored[u], pair * 16)
                    dve.tensor_scalar_max(z_new[:, u, :], z, 0.0).then_inc(new_ready, 1)
                    chn.link(dve.tensor_scalar_max(z, z, 0.0))
                else:
                    chn.link(dve.scalar_tensor_tensor(out=row(X, t), in0=z, scalar=0.0, in1=row(X, t), op0=ALU.max, op1=ALU.add))
                dve.sem_inc(mixed, 1)

        over_tiles(dve, ahead, now)

    def scalar(act):
        if store_stage:
            norm_scalar(act)

        def ahead(t, u, pair):
            wait_from(act, turned, t + 1)
            act.copy(zT[:, u, :, :].rearrange("p k n -> p (k n)"), ps[4 + u][:, 0:2 * P]).then_inc(zt_ready, 1)

        def now(t, u, pair):
            if own_part:
                wait_from(act, exp_in, t + 1)
                act.activation(ex[:, u, :], lg[:, u, :], ACT.Exp, bias=col[:, u, 0:1], accum_out=col[:, u, 1:2]).then_inc(exp_out, 1)

        over_tiles(act, ahead, now)

    def tensor(pe):
        pe.wait_ge(w_loaded, 16 * (K0 + 2 * own_part))

        def ahead(t, u, pair):
            wait_from(pe, staged, t + 1)
            for k in range(2):
                mm = pe.transpose(ps[4 + u][:, k * P:(k + 1) * P], stage[:, u, k * P:(k + 1) * P], ident[:, :])
            mm.then_inc(turned, 1)

        def now(t, u, pair):
            wait_from(pe, zt_ready, t + 1)
            wait_from(pe, mixed, t)
            for k in range(2):
                for h in range(2):
                    mm = pe.matmul(ps[2 * u + h][:, :], zT[:, u, k, :],
                                   W0[:, k, 2 * h:2 * h + 2, :].rearrange("p k d -> p (k d)"),
                                   start=(k == 0), stop=(k == 1))
            if own_part:
                for k in range(2):
                    mm = pe.matmul(ps[6 + u][:, 0:K0], zT[:, u, k, :], envw[:, k, :], start=(k == 0), stop=(k == 1))
            mm.then_inc(products, 1)

        over_tiles(pe, ahead, now)

    return {"sync": sync, "vector": vector, "scalar": scalar, "tensor": tensor}


def run_block(nc, programs):
    with nc.Block() as block:
        if "sync" in programs:
            @block.sync
            def _(sp):
                programs["sync"](sp)

        if "vector" in programs:
            @block.vector
            def _(dve):
                programs["vector"](dve)

        if "scalar" in programs:
            @block.scalar
            def _(act):
                programs["scalar"](act)

        if "tensor" in programs:
            @block.tensor
            def _(pe):
                programs["tensor"](pe)

        if "gpsimd" in programs:
            @block.gpsimd
            def _(pool):
                programs["gpsimd"](pool)


def gather_sum(g, c, layer):
    nc, sb, sem, ps, A = g["nc"], g["sb"], g["sem"], g["ps"], g["A"]
    pre = f"sum{layer}_"
    ring_rows = sb(pre + "rows", [P, 2 * HALF, D + 1], F32, c)
    ring_index = sb(pre + "index", [P, 2, HALF], U32, c)
    place = sb(pre + "place", [P, 2, HALF, P], F32, c)
    indexed, placed, summed, cleared, dve_own = (
        sem(pre + n) for n in ("indexed", "placed", "summed", "cleared", "dve_own"))
    fetched = [sem(pre + f"fetched{h}") for h in range(2)]
    rounds = STEPS // (2 * HALF)
    pool_passed = sem(pre + "pool_passed")

    def gpsimd(pool):
        pool.wait_ge(cleared, 1)
        for i in rounds_of(pool, rounds):
            for h in range(2):
                wait_apart(pool, fetched[h], i * (16 * HALF), pool_passed)
                pool.tensor_copy(ring_index[:, h, :], g["row_of"][:, ds((i * 2 + h) * HALF, HALF)]).then_inc(indexed, 1)
                wait_apart(pool, indexed, i * 2 + h + 1, pool_passed)
                for k in range(HALF):
                    wait_apart(pool, summed, (i * 2 + h) * HALF + k + 1, pool_passed)
                    pool.indirect_dma_start(
                        out=ring_rows[:, h * HALF + k, 0:D], out_offset=None, in_=g["z_rows"][layer][:, :],
                        in_offset=bass.IndirectOffsetOnAxis(ap=ring_index[:, h, k:k + 1], axis=0)).then_inc(fetched[h], 16)

    def vector(dve):
        ch = Chain(dve, dve_own)
        dve.memset(ring_rows[:, :, D:D + 1], 1.0)
        dve.memset(A[:, :, :], 0.0).then_inc(cleared, 1)
        dve.wait_ge(cleared, 1)

        def places(half, h):
            wait_from(dve, summed, half * HALF + HALF)
            key = g["local_key"][:, ds(half * HALF, HALF)]
            dve.tensor_tensor(place[:, h, :, :], g["iota_row"][:, :].unsqueeze(1).broadcast_to([P, HALF, P]),
                              key.unsqueeze(2).broadcast_to([P, HALF, P]), ALU.is_equal).then_inc(placed, 1)

        dve.sem_inc(dve_own, HALF)
        places(0, 0)
        for i in rounds_of(dve, rounds):
            for h in range(2):
                places(i * 2 + h + 1, 1 - h)
                ch.enter((i * 2 + h) * HALF + HALF)
                for k in range(HALF):
                    s = (i * 2 + h) * HALF + k
                    t = dve.value_load(g["tile_of"][0:1, ds(s, 1)], min_val=0, max_val=NT - 1)
                    here = row(A, t)
                    wait_from(dve, summed, s + 1 + 2 * HALF)
                    ch.wait()
                    ch.step(dve.tensor_tensor(here, ps[k][:, 0:D + 1], here, ALU.add))

    def tensor(pe):
        pe.sem_inc(summed, 2 * HALF)
        for i in rounds_of(pe, rounds):
            for h in range(2):
                wait_from(pe, fetched[h], (i + 1) * (16 * HALF))
                wait_from(pe, placed, i * 2 + h + 1)
                for k in range(HALF):
                    s = (i * 2 + h) * HALF + k
                    wait_from(pe, dve_own, s + 1)
                    pe.matmul(ps[k][:, 0:D + 1], place[:, h, k, :], ring_rows[:, h * HALF + k, :],
                              start=True, stop=True).then_inc(summed, 1)

    return {"gpsimd": gpsimd, "vector": vector, "tensor": tensor}


NH, DH, NG = 8, 64, 64
INNER = NH * DH
PAIRS = NH // 2


def four_slots(eng, body):
    for t in range(4):
        body(t, t)
    with eng.Fori(1, NT // 4 - 1) as i:
        for v in range(4):
            body(i * 4 + v, v)
    for t in range(4 * (NT // 4 - 1), NT):
        body(t, t % 4)


def slice_attention(g, c):
    nc, sb, sem, ps, X, ident, ones = (g[n] for n in ("nc", "sb", "sem", "ps", "X", "ident", "ones"))
    logit_w = sb("logit_w", [P, 2, INNER], F32, c)
    logit_b = sb("logit_b", [P, INNER], F32, c)
    slices = sb("slices", [P, PAIRS, D + 1], F32, c)
    back = sb("back", [P, PAIRS, D], F32, c)
    b_out = sb("b_out", [P, D], F32, c)
    wT = sb("wT", [P, PAIRS, (LASTT + 1) * P], F32, c)

    mean, rstd, norm_vector, norm_scalar = row_norm(g, c, "ln1")

    with ExitStack() as c2:
        wx = sb("wx", [P, 2, INNER], F32, c2)
        wxT = sb("wxT", [DH, 2, NH, P], F32, c2)
        ws = sb("ws", [DH, NG], F32, c2)
        bx = sb("bx", [DH, NH], F32, c2)
        bxb = sb("bxb", [DH, NH, P], F32, c2)
        bs = sb("bs", [P, NG], F32, c2)
        tb = sb("tb", [P, NH], F32, c2)
        loaded, turned, copied, multiplied, widened, own = (
            sem("slw_" + n) for n in ("loaded", "turned", "copied", "multiplied", "widened", "own"))
        with nc.Block() as block:
            @block.sync
            def _(sp):
                sp.dma_start(wx[:, :, :], g["L0_ffn_W_x"].rearrange("(c p) n -> p c n", p=P)).then_inc(loaded, 16)
                sp.dma_start(ws[:, :], g["L0_ffn_W_slice"]).then_inc(loaded, 16)
                with nc.allow_non_contiguous_dma(reason="512 numbers"):
                    sp.dma_start(bx[:, :], g["L0_ffn_b_x"].rearrange("(h d) -> d h", h=NH)).then_inc(loaded, 16)
                sp.dma_start(bs[:, :], g["L0_ffn_b_slice"].rearrange("(a n) -> a n", a=1).broadcast_to([P, NG])).then_inc(loaded, 16)
                sp.dma_start(tb[:, :], g["L0_ffn_temperature"].rearrange("a h b c -> a (h b c)").broadcast_to([P, NH])).then_inc(loaded, 16)
                sp.dma_start(b_out[:, :], g["L0_ffn_b_out"].rearrange("(a n) -> a n", a=1).broadcast_to([P, D])).then_inc(loaded, 16)
                sp.wait_ge(loaded, 96)

            @block.tensor
            def _(pe):
                pe.wait_ge(loaded, 96)
                for k in range(2):
                    for h in range(NH):
                        mm = pe.transpose(ps[2 * k + h // 4][0:DH, (h % 4) * P:(h % 4 + 1) * P], wx[:, k, h * DH:(h + 1) * DH], ident[:, :])
                mm.then_inc(turned, 1)
                pe.wait_ge(copied, 4)
                for k in range(2):
                    for h in range(NH):
                        pe.matmul(ps[4 + k][:, h * NG:(h + 1) * NG], wxT[:, k, h, :], ws[:, :], start=True, stop=True)
                pe.wait_ge(widened, 1)
                for h in range(NH):
                    mm = pe.matmul(ps[6][:, h * NG:(h + 1) * NG], bxb[:, h, :], ws[:, :], start=True, stop=True)
                mm.then_inc(multiplied, 1)

            @block.vector
            def _(dve):
                ch = Chain(dve, own)
                dve.wait_ge(loaded, 96)
                dve.tensor_copy(bxb[:, :, :], bx[:, :].unsqueeze(2).broadcast_to([DH, NH, P])).then_inc(widened, 1)
                ch.link(dve.tensor_scalar(tb[:, :], tb[:, :], 0.1, 5.0, ALU.max, ALU.min))
                ch.link(dve.reciprocal(tb[:, :], tb[:, :]))
                dve.wait_ge(turned, 1)
                for k in range(4):
                    dve.tensor_copy(wxT[:, k // 2, (k % 2) * 4:(k % 2) * 4 + 4, :].rearrange("d h p -> d (h p)"), ps[k][0:DH, :]).then_inc(copied, 1)
                dve.wait_ge(multiplied, 1)
                per_head = tb[:, :].unsqueeze(2).broadcast_to([P, NH, NG])
                for k in range(2):
                    dve.tensor_tensor(logit_w[:, k, :].rearrange("p (h g) -> p h g", h=NH),
                                      ps[4 + k][:, :].rearrange("p (h g) -> p h g", h=NH), per_head, ALU.mult)
                bias = logit_b[:, :].rearrange("p (h g) -> p h g", h=NH)
                ch.link(dve.tensor_tensor(bias, ps[6][:, :].rearrange("p (h g) -> p h g", h=NH),
                                          bs[:, :].unsqueeze(1).broadcast_to([P, NH, NG]), ALU.add))
                ch.link(dve.tensor_tensor(bias, bias, per_head, ALU.mult))
                norm_vector(dve)

            @block.scalar
            def _(act):
                norm_scalar(act)

    with ExitStack() as c2:
        stage = sb("sl_stage", [P, 4, D + 1], F32, c2)
        zT = sb("sl_zT", [P, 2, 2, P], F32, c2)
        lg = sb("sl_lg", [P, 2, INNER], F32, c2)
        w = sb("sl_w", [P, 2, INNER], F32, c2)
        top = sb("sl_top", [P, 2, NH], F32, c2)
        tot = sb("sl_tot", [P, 2, NH], F32, c2)
        zero = sb("sl_zero", [P, D + 1], F32, c2)
        staged, turned, zt_ready, logits, exp_in, exp_out, weights, summed, wt_done, wt_taken, own, stage_own = (
            sem("sl_" + n) for n in ("staged", "turned", "zt_ready", "logits", "exp_in", "exp_out", "weights", "summed",
                                     "wt_done", "wt_taken", "own", "stage_own"))
        last = LASTT

        def vector(dve):
            ch = Chain(dve, own)
            dve.memset(zero[:, :], 0.0).then_inc(stage_own, 1)
            dve.memset(stage[:, :, D:D + 1], 1.0).then_inc(stage_own, 1)

            def stage_of(t, slot):
                wait_from(dve, summed, t - 3)
                dve.tensor_scalar(stage[:, slot, 0:D], row(X, t), mean[:, ds(t, 1)], rstd[:, ds(t, 1)], ALU.subtract,
                                  ALU.mult).then_inc(staged, 1)

            def body(t, slot):
                u = slot % 2
                if isinstance(t, int) and t > last:
                    return
                if not isinstance(t, int) or t < last:
                    stage_of(t + 1, (slot + 1) % 4)
                ch.enter(t * 3)
                heads = lg[:, u, :].rearrange("p (h g) -> p h g", h=NH)
                wait_from(dve, logits, t + 1)
                ch.link(dve.tensor_tensor(lg[:, u, :], ps[u][:, :], logit_b[:, :], ALU.add))
                ch.link(dve.tensor_reduce(top[:, u, :], heads, AX.X, ALU.max))
                dve.tensor_tensor(heads, heads, top[:, u, :].unsqueeze(2).broadcast_to([P, NH, NG]), ALU.subtract).then_inc(exp_in, 1)
                wait_from(dve, exp_out, t + 1)
                ch.link(dve.tensor_reduce(tot[:, u, :], heads, AX.X, ALU.add))
                dve.reciprocal(tot[:, u, :], tot[:, u, :]).then_inc(stage_own, 1)
                wait_from(dve, stage_own, t + 3)
                wait_from(dve, summed, t - 1)
                dve.tensor_tensor(w[:, u, :].rearrange("p (h g) -> p h g", h=NH), heads,
                                  tot[:, u, :].unsqueeze(2).broadcast_to([P, NH, NG]), ALU.mult).then_inc(weights, 1)

            stage_of(0, 0)
            four_slots(dve, body)

        def scalar(act):
            def take(t):
                wait_from(act, wt_done, t + 1)
                act.copy(wT[:, :, ds(t * P, P)], ps[6][:, :].rearrange("p (j n) -> p j n", j=PAIRS)).then_inc(wt_taken, 1)

            def zt(t, u):
                wait_from(act, turned, t + 1)
                act.copy(zT[:, u, :, :].rearrange("p k n -> p (k n)"), ps[7][:, 0:2 * P]).then_inc(zt_ready, 1)

            def body(t, slot):
                number = isinstance(t, int)
                if number and t > last:
                    return take(last)
                wait_from(act, exp_in, t + 1)
                act.activation(lg[:, slot % 2, :], lg[:, slot % 2, :], ACT.Exp).then_inc(exp_out, 1)
                if not number or t > 0:
                    take(t - 1)
                if not number or t < last:
                    zt(t + 1, (slot + 1) % 2)

            zt(0, 0)
            four_slots(act, body)

        def tensor(pe):
            pe.wait_ge(stage_own, 2)

            def turn(t, slot):
                wait_from(pe, staged, t + 1)
                wait_from(pe, zt_ready, t)
                for k in range(2):
                    mm = pe.transpose(ps[7][:, k * P:(k + 1) * P], stage[:, slot, k * P:(k + 1) * P], ident[:, :])
                mm.then_inc(turned, 1)

            def sums(t, slot):
                rows = NREST if isinstance(t, int) and t == last else P
                wait_from(pe, weights, t + 1)
                wait_from(pe, wt_taken, t)
                for j in range(PAIRS):
                    mm = pe.transpose(ps[6][:, j * P:(j + 1) * P], w[:, slot % 2, j * P:(j + 1) * P], ident[:, :])
                mm.then_inc(wt_done, 1)
                for j in range(PAIRS):
                    mm = pe.matmul(ps[2 + j][:, 0:D + 1], w[0:rows, slot % 2, j * P:(j + 1) * P], stage[0:rows, slot, :],
                                   start=False, stop=rows < P, skip_group_check=True)
                mm.then_inc(summed, 1)

            def body(t, slot):
                number = isinstance(t, int)
                if number and t > last:
                    return sums(last, last % 4)
                wait_from(pe, zt_ready, t + 1)
                wait_from(pe, exp_in, t - 1)
                for k in range(2):
                    mm = pe.matmul(ps[slot % 2][:, :], zT[:, slot % 2, k, :], logit_w[:, k, :], start=(k == 0), stop=(k == 1))
                mm.then_inc(logits, 1)
                if not number or t > 0:
                    sums(t - 1, (slot - 1) % 4)
                if not number or t < last:
                    turn(t + 1, (slot + 1) % 4)

            for j in range(PAIRS):
                pe.matmul(ps[2 + j][:, 0:D + 1], zero[:, 0:P], zero[:, :], start=True, stop=False, skip_group_check=True)
            turn(0, 0)
            four_slots(pe, body)

        run_block(nc, {"vector": vector, "scalar": scalar, "tensor": tensor})

    with ExitStack() as c2:
        names = ("turned", "copied", "tokens", "norms", "tok_ready", "tok_turned", "tokT_ready", "qkv", "qkv_ready", "scored",
                 "exp_in", "exp_out", "attn", "attn_turned", "attnT_ready", "mixed", "mixed_ready", "backed", "back_ready",
                 "loaded", "moved", "own")
        s = {n: sem("sa_" + n) for n in names}
        yT = sb("sa_yT", [P, 2, INNER], F32, c2)
        norm_row = sb("sa_norm_row", [1, INNER], F32, c2)
        bfx = sb("sa_bfx", [1, INNER], F32, c2)
        wfx = sb("sa_wfx", [P, 2, INNER], F32, c2)
        wq, wk, wv = (sb(n, [DH, DH], F32, c2) for n in ("sa_wq", "sa_wk", "sa_wv"))
        wo = sb("sa_wo", [DH, NH, D], F32, c2)
        den = sb("sa_den", [NG, NH], F32, c2)
        tok, tokT, qT, kT, v, at, atT, mixT = (sb("sa_" + n, [DH, INNER], F32, c2)
                                               for n in ("tok", "tokT", "qT", "kT", "v", "at", "atT", "mixT"))
        peak = sb("sa_peak", [NG, NH], F32, c2)
        odd = slices[0:NG, :, 0:D]
        scale = float(DH) ** -0.5

        def h_(a, h):
            return a[:, h * DH:(h + 1) * DH]

        def by_head(a):
            return a.rearrange("p (h g) -> p h g", h=NH)

        def sync(sp):
            for dst, src in ((wfx[:, :, :], g["L0_ffn_W_fx"].rearrange("(c p) n -> p c n", p=P)), (wq[:, :], g["L0_ffn_W_q"]),
                             (wk[:, :], g["L0_ffn_W_k"]), (wv[:, :], g["L0_ffn_W_v"]),
                             (wo[:, :, :], g["L0_ffn_W_out"].rearrange("(h d) n -> d h n", d=DH)),
                             (bfx[:, :], g["L0_ffn_b_fx"].rearrange("(a n) -> a n", a=1))):
                sp.dma_start(dst, src).then_inc(s["loaded"], 16)
            sp.wait_ge(s["back_ready"], 1)
            sp.dma_start(back[NG:P, :, :], odd).then_inc(s["moved"], 16)
            sp.wait_ge(s["moved"], 16)

        def tensor(pe):
            pe.wait_ge(s["copied"], 1)
            for j in range(PAIRS):
                for k in range(2):
                    pe.transpose(ps[k][:, j * P:(j + 1) * P], slices[:, j, k * P:(k + 1) * P], ident[:, :])
                mm = pe.transpose(ps[6][0:1, j * P:(j + 1) * P], slices[:, j, D:D + 1], ident[:, :])
            mm.then_inc(s["turned"], 1)
            pe.wait_ge(s["copied"], 4)
            pe.wait_ge(s["loaded"], 96)
            for h in range(NH):
                for k in range(2):
                    pe.matmul(h_(ps[3][0:NG, :], h), h_(yT[:, k, :], h), h_(wfx[:, k, :], h), start=(k == 0), stop=False)
                pe.matmul(h_(ps[3][0:NG, :], h), h_(norm_row, h), h_(bfx, h), start=False, stop=True)
            for h in range(NH):
                mm = pe.matmul(ps[4][0:NG, h:h + 1], h_(norm_row, h), ones[0:1, 0:1], start=True, stop=True)
            mm.then_inc(s["tokens"], 1)
            pe.wait_ge(s["tok_ready"], 1)
            for h in range(NH):
                mm = pe.transpose(h_(ps[5][0:DH, :], h), h_(tok, h), ident[0:DH, 0:DH])
            mm.then_inc(s["tok_turned"], 1)
            pe.wait_ge(s["tokT_ready"], 1)
            pe.matmul(ps[0][0:DH, :], wq[:, :], tokT[:, :], start=True, stop=True)
            pe.matmul(ps[1][0:DH, :], wk[:, :], tokT[:, :], start=True, stop=True)
            for h in range(NH):
                mm = pe.matmul(h_(ps[2][0:NG, :], h), h_(tokT, h), wv[:, :], start=True, stop=True)
            mm.then_inc(s["qkv"], 1)
            pe.wait_ge(s["qkv_ready"], 3)
            for h in range(NH):
                mm = pe.matmul(h_(ps[3][0:NG, :], h), h_(qT, h), h_(kT, h), start=True, stop=True)
            mm.then_inc(s["scored"], 1)
            pe.wait_ge(s["attn"], 1)
            for h in range(NH):
                mm = pe.transpose(h_(ps[4][0:NG, :], h), h_(at, h), ident[0:NG, 0:NG])
            mm.then_inc(s["attn_turned"], 1)
            pe.wait_ge(s["attnT_ready"], 1)
            for h in range(NH):
                mm = pe.matmul(h_(ps[5][0:DH, :], h), h_(v, h), h_(atT, h), start=True, stop=True)
            mm.then_inc(s["mixed"], 1)
            pe.wait_ge(s["mixed_ready"], 1)
            for h in range(NH):
                mm = pe.matmul(ps[h % 2 * 2 + h // 4][0:NG, (h // 2 % 2) * D:(h // 2 % 2 + 1) * D], h_(mixT, h), wo[:, h, :], start=True, stop=True)
            mm.then_inc(s["backed"], 1)

        def vector(dve):
            ch = Chain(dve, s["own"])
            for j in range(PAIRS):
                ins = dve.tensor_copy(slices[:, j, :], ps[2 + j][:, 0:D + 1])
            ins.then_inc(s["copied"], 1)
            dve.wait_ge(s["turned"], 1)
            for k in range(2):
                dve.tensor_copy(yT[:, k, :], ps[k][:, :]).then_inc(s["copied"], 1)
            dve.tensor_copy(norm_row[:, :], ps[6][0:1, :]).then_inc(s["copied"], 1)
            dve.wait_ge(s["tokens"], 1)
            ch.link(dve.tensor_scalar(den[:, :], ps[4][0:NG, 0:NH], 1e-5, None, ALU.add))
            ch.link(dve.reciprocal(den[:, :], den[:, :]))
            dve.tensor_tensor(by_head(tok), by_head(ps[3][0:NG, :]), den[:, :].unsqueeze(2).broadcast_to([NG, NH, DH]), ALU.mult).then_inc(s["tok_ready"], 1)
            dve.wait_ge(s["tok_turned"], 1)
            dve.tensor_copy(tokT[:, :], ps[5][0:DH, :]).then_inc(s["tokT_ready"], 1)
            dve.wait_ge(s["qkv"], 1)
            for k, a in enumerate((qT, kT, v)):
                dve.tensor_copy(a[:, :], ps[k][0:DH, :]).then_inc(s["qkv_ready"], 1)
            dve.wait_ge(s["scored"], 1)
            ch.link(dve.tensor_reduce(peak[:, :], by_head(ps[3][0:NG, :]), AX.X, ALU.max))
            dve.tensor_tensor(by_head(at), by_head(ps[3][0:NG, :]), peak[:, :].unsqueeze(2).broadcast_to([NG, NH, NG]), ALU.subtract).then_inc(s["exp_in"], 1)
            dve.wait_ge(s["exp_out"], 1)
            ch.link(dve.tensor_reduce(peak[:, :], by_head(at), AX.X, ALU.add))
            ch.link(dve.reciprocal(peak[:, :], peak[:, :]))
            dve.tensor_tensor(by_head(at), by_head(at), peak[:, :].unsqueeze(2).broadcast_to([NG, NH, NG]), ALU.mult).then_inc(s["attn"], 1)
            dve.wait_ge(s["attn_turned"], 1)
            dve.tensor_copy(atT[:, :], ps[4][0:NG, :]).then_inc(s["attnT_ready"], 1)
            dve.wait_ge(s["mixed"], 1)
            dve.tensor_copy(mixT[:, :], ps[5][0:DH, :]).then_inc(s["mixed_ready"], 1)
            dve.wait_ge(s["backed"], 1)
            for b in range(4):
                to = (back[0:NG, :, :], odd)[b // 2]
                ch.link(dve.tensor_copy(to[:, 2 * (b % 2):2 * (b % 2) + 2, :], ps[b][0:NG, :].rearrange("p (j d) -> p j d", j=2)))
            dve.sem_inc(s["back_ready"], 1)

        def scalar(act):
            act.wait_ge(s["exp_in"], 1)
            act.activation(at[:, :], at[:, :], ACT.Exp, scale=scale).then_inc(s["exp_out"], 1)

        run_block(nc, {"sync": sync, "tensor": tensor, "vector": vector, "scalar": scalar})

    with ExitStack() as c2:
        here = sb("sb_here", [P, 2, PAIRS * P], F32, c2)
        here_ready, products, added, own = (sem("sb_" + n) for n in ("here_ready", "products", "added", "own"))
        tiles = LASTT + 1

        def each(eng, body):
            for i in rounds_of(eng, tiles // 2):
                for u in range(2):
                    body(i * 2 + u, u)
            if tiles % 2:
                body(tiles - 1, 0)

        def scalar(act):
            def body(t, u):
                wait_from(act, products, t)
                act.copy(here[:, u, :].rearrange("p (j n) -> p j n", j=PAIRS), wT[:, :, ds(t * P, P)]).then_inc(here_ready, 1)
            each(act, body)

        def tensor(pe):
            pe.sem_inc(products, 1)

            def body(t, u):
                wait_from(pe, here_ready, t + 1)
                wait_from(pe, added, t)
                for j in range(PAIRS):
                    mm = pe.matmul(ps[u][:, 0:D], here[:, u, j * P:(j + 1) * P], back[:, j, :], start=(j == 0), stop=(j == PAIRS - 1))
                mm.then_inc(products, 1)
            each(pe, body)

        def vector(dve):
            dve.sem_inc(added, 1)
            ch = Chain(dve, own)

            def body(t, u):
                ch.enter(t)
                wait_from(dve, products, t + 2)
                ch.link(dve.tensor_tensor(row(X, t), ps[u][:, 0:D], row(X, t), ALU.add))
                dve.tensor_tensor(row(X, t), row(X, t), b_out[:, :], ALU.add).then_inc(added, 1)
            each(dve, body)

        run_block(nc, {"scalar": scalar, "tensor": tensor, "vector": vector})


H1, F1 = 8, 32
HB = F1 + 1
HW = H1 * HB
RW = HW + H1


def graph_attention(g, c):
    nc, sb, sem, ps, X, ident = (g[n] for n in ("nc", "sb", "sem", "ps", "X", "ident"))
    banks01 = g["banks01"]
    h_rows = nc.dram_tensor("h_rows", [NT * P, RW], F32)
    dst_scores = sb("dst_scores", [P, NT, H1], F32, c)
    local_key = sb("key1", [P, SG], F32, c)
    row_of = sb("row1", [P, SG], U32, c)
    tile_of = sb("tile1", [1, SG], I32, c)
    acc = sb("acc", [P, NT, HW], F32, c)

    with ExitStack() as c2:
        w = sb("ga_w", [P, 2, H1, F1], F32, c2)
        av = sb("ga_av", [P, 2, H1, F1], F32, c2)
        wa = sb("ga_wa", [P, 2, H1, F1], F32, c2)
        wall = sb("ga_wall", [P, 2, H1 * F1 + 2 * H1], F32, c2)
        stage = sb("ga_stage", [P, 2, D], F32, c2)
        zT = sb("ga_zT", [P, 2, 2, P], F32, c2)
        new = sb("ga_new", [P, 2, RW], F32, c2)
        loaded, folded, staged, turned, zt_ready, products, new_ready, taken, own = (
            sem("ga_" + n) for n in ("loaded", "folded", "staged", "turned", "zt_ready", "products", "new_ready", "taken", "own"))
        stored = [sem(f"ga_stored{u}") for u in range(2)]
        mean, rstd, norm_vector, norm_scalar = row_norm(g, c2, "ln2")

        def sync(sp):
            for k in range(2):
                sp.dma_start(w[:, k, :, :], g["L1_gnn_W"].rearrange("h (c p) f -> c p h f", p=P)[k]).then_inc(loaded, 16)
            for k, a in enumerate(("L1_gnn_a_src", "L1_gnn_a_dst")):
                sp.dma_start(av[:, k, :, :].rearrange("p h f -> p (h f)"), g[a].rearrange("(a h) f -> a (h f)", a=1).broadcast_to([P, H1 * F1])).then_inc(loaded, 16)
            sp.dma_start(local_key[:, :], g["key_by_dst"][:, :]).then_inc(loaded, 16)
            sp.dma_start(row_of[:, :], g["row_by_dst"][:, :]).then_inc(loaded, 16)
            sp.dma_start(tile_of[:, :], g["tile_of_step_dram"][1:2, :]).then_inc(loaded, 16)
            with sp.Fori(0, NT // 2) as i:
                for u in range(2):
                    wait_from(sp, new_ready, (i * 2 + u + 1) * 2)
                    sp.dma_start(h_rows[ds((i * 2 + u) * P, P), :], new[:, u, :]).then_inc(stored[u], 16)
            for u in range(2):
                sp.wait_ge(stored[u], 16 * (NT // 2))

        def vector(dve):
            ch = Chain(dve, own)
            norm_vector(dve)
            dve.memset(acc[:, :, :], 0.0)
            for u in range(2):
                ch.link(dve.memset(new[:, u, :], 1.0))
            dve.sem_inc(taken, 1)
            dve.wait_ge(loaded, 112)
            for k in range(2):
                dve.tensor_copy(wall[:, k, 0:H1 * F1], w[:, k, :, :].rearrange("p h f -> p (h f)")).then_inc(folded, 1)
                for q in range(2):
                    ch.link(dve.tensor_tensor(wa[:, k, :, :], w[:, k, :, :], av[:, q, :, :], ALU.mult))
                    at = H1 * F1 + q * H1
                    ch.link(dve.tensor_reduce(wall[:, k, at:at + H1], wa[:, k, :, :], AX.X, ALU.add))
            ch.wait()
            dve.sem_inc(folded, 1)

            def ahead(t, u, pair):
                wait_from(dve, turned, t - 1)
                dve.tensor_scalar(stage[:, u, :], row(X, t), mean[:, ds(t, 1)], rstd[:, ds(t, 1)], ALU.subtract,
                                  ALU.mult).then_inc(staged, 1)

            def now(t, u, pair):
                wait_from(dve, products, t + 1)
                wait_from(dve, stored[u], pair * 16)
                dve.tensor_copy(new[:, u, 0:HW].rearrange("p (h b) -> p h b", b=HB)[:, :, 0:F1],
                                ps[u][:, 0:H1 * F1].rearrange("p (h f) -> p h f", f=F1)).then_inc(new_ready, 1)
                dve.tensor_copy(new[:, u, HW:RW], ps[u][:, H1 * F1:H1 * F1 + H1]).then_inc(new_ready, 1)
                dve.tensor_scalar(row(dst_scores, t), ps[u][:, H1 * F1 + H1:H1 * F1 + 2 * H1], 1.0, None, ALU.mult).then_inc(taken, 1)

            over_tiles(dve, ahead, now)

        def scalar(act):
            norm_scalar(act)

            def ahead(t, u, pair):
                wait_from(act, turned, t + 1)
                act.copy(zT[:, u, :, :].rearrange("p k n -> p (k n)"), ps[4 + u][:, 0:2 * P]).then_inc(zt_ready, 1)

            over_tiles(act, ahead, lambda t, u, pair: None)

        def tensor(pe):
            pe.wait_ge(folded, 3)

            def ahead(t, u, pair):
                wait_from(pe, staged, t + 1)
                for k in range(2):
                    mm = pe.transpose(ps[4 + u][:, k * P:(k + 1) * P], stage[:, u, k * P:(k + 1) * P], ident[:, :])
                mm.then_inc(turned, 1)

            def now(t, u, pair):
                wait_from(pe, zt_ready, t + 1)
                wait_from(pe, taken, t)
                for k in range(2):
                    mm = pe.matmul(ps[u][:, 0:H1 * F1 + 2 * H1], zT[:, u, k, :], wall[:, k, :], start=(k == 0), stop=(k == 1))
                mm.then_inc(products, 1)

            over_tiles(pe, ahead, now)

        run_block(nc, {"sync": sync, "vector": vector, "scalar": scalar, "tensor": tensor})

    pool_passed = sem("ge_pool_passed")
    with ExitStack() as c2:
        halves_count = STEPS // HALF
        HE = HALF * P
        BLOCKS = HALF + 1
        rows = sb("ge_rows", [P, 2, HALF, RW], F32, c2)
        index = sb("ge_index", [P, 2, HALF], U32, c2)
        place = sb("ge_place", [P, 2, HALF, P], F32, c2)
        placeT = sb("ge_placeT", [P, 2, 4, P], F32, c2)
        cuts = sb("ge_cuts", [H1, 2, 2, HE], F32, c2)
        goes_on = sb("ge_goes_on", [H1, halves_count + 1], F32, c2)
        upto_edge = sb("ge_upto_edge", [H1, 2, HE], F32, c2)
        run_peak = sb("ge_run_peak", [H1, BLOCKS * P], F32, c2)
        fresh = sb("ge_fresh", [H1, 1], F32, c2)
        sc = sb("ge_sc", [P, 3, BLOCKS, H1], F32, c2)
        weight = sb("ge_weight", [P, HALF, H1], F32, c2)
        drop = sb("ge_drop", [P, H1], F32, c2)
        scale = sb("ge_scale", [P, H1], F32, c2)
        names = ("ready", "indexed", "placed", "src_turned", "places_turned", "placesT_ready", "runs_made", "dst_scored",
                 "dst_taken", "peaks_turned", "exp_in", "exp_out", "weighted", "summed", "drop_ready", "drop_placed",
                 "scale_ready", "scan_own", "scores_own", "adds", "scaled")
        (ready, indexed, placed, src_turned, places_turned, placesT_ready, runs_made, dst_scored, dst_taken, peaks_turned,
         exp_in, exp_out, weighted, summed, drop_ready, drop_placed, scale_ready, scan_own, scores_own, adds, scaled) = (
            sem("ge_" + n) for n in names)
        fetched = [sem(f"ge_fetched{h}") for h in range(2)]
        cut_loaded = [sem(f"ge_cut_loaded{h}") for h in range(2)]
        goes_on_loaded = sem("ge_goes_on_loaded")
        small, sums = ps[4], ps[5:8]
        PEAKS = BLOCKS * H1
        DROPS = 2 * BLOCKS * H1
        AHEAD = 2 * HALF
        ADDS_AHEAD = 2

        def halves(eng, front):
            front(0, 0, 0)
            for i in rounds_of(eng, halves_count // 2):
                front(i * 2 + 1, 1, i)
                front(i * 2 + 2, 0, i + 1)

        def gpsimd(pool):
            def front(n, h, pair):
                wait_apart(pool, fetched[h], pair * (16 * HALF), pool_passed)
                pool.tensor_copy(index[:, h, :], row_of[:, ds(n * HALF, HALF)]).then_inc(indexed, 1)
                wait_apart(pool, indexed, n + 1, pool_passed)
                for k in range(HALF):
                    wait_apart(pool, summed, n * HALF + k + 1, pool_passed)
                    pool.indirect_dma_start(out=rows[:, h, k, :], out_offset=None, in_=h_rows[:, :],
                                            in_offset=bass.IndirectOffsetOnAxis(ap=index[:, h, k:k + 1], axis=0)).then_inc(fetched[h], 16)
            halves(pool, front)

        def sync(sp):
            starts = g["cuts_dram"][0:1, 0:(halves_count + 1) * HE].rearrange("a (n e) -> a n e", e=HE)[:, :, 0]
            sp.dma_start(goes_on[:, :], starts.broadcast_to([H1, halves_count + 1]), allow_slow_non_contiguous=True).then_inc(goes_on_loaded, 16)

            def front(n, h, pair):
                wait_from(sp, runs_made, n - 1)
                for a in range(2):
                    sp.dma_start(cuts[:, h, a, :], g["cuts_dram"][a:a + 1, ds(n * HE, HE)].broadcast_to([H1, HE])).then_inc(cut_loaded[h], 16)
            halves(sp, front)

        def tensor(pe):
            def turn(n, h, pair):
                wait_from(pe, fetched[h], (pair + 1) * (16 * HALF))
                wait_from(pe, runs_made, n)
                for k in range(HALF):
                    mm = pe.matmul(banks01[0:H1, k * P:(k + 1) * P], rows[:, h, k, HW:RW], ident[:, :], start=True, stop=True)
                mm.then_inc(src_turned, 1)
                wait_from(pe, placed, n + 1)
                for q in range(2):
                    wait_from(pe, placesT_ready, n * 2 + q - 1)
                    for k in range(4):
                        mm = pe.transpose(ps[2 + q][:, k * P:(k + 1) * P], place[:, h, q * 4 + k, :], ident[:, :])
                    mm.then_inc(places_turned, 1)
                tiles = [pe.value_load(tile_of[0:1, ds(n * HALF + k, 1)], min_val=0, max_val=NT - 1) for k in range(HALF)]
                wait_from(pe, scale_ready, n)
                for k in range(HALF):
                    if k % 4 == 0:
                        wait_from(pe, placesT_ready, n * 2 + k // 4 + 1)
                    at = k * H1
                    pe.matmul(small[:, at:at + H1], placeT[:, k // 4, k % 4, :], row(dst_scores, tiles[k]), start=True, stop=True)
                pe.matmul(small[:, HALF * H1:BLOCKS * H1], placeT[:, 0, 0, :], row(dst_scores, tiles[0]), start=True, stop=True).then_inc(dst_scored, 1)

            def turn_peaks(n):
                wait_from(pe, runs_made, n + 1)
                wait_from(pe, dst_taken, n + 1)
                for k in range(BLOCKS):
                    at = PEAKS + k * H1
                    mm = pe.matmul(small[:, at:at + H1], run_peak[:, k * P:(k + 1) * P], ident[0:H1, 0:H1], start=True, stop=True)
                mm.then_inc(peaks_turned, 1)

            def place_drop(n, h):
                wait_from(pe, drop_ready, n + 1)
                pe.matmul(small[:, DROPS:DROPS + H1], place[0:1, h, 0, :], drop[0:1, :], start=True, stop=True).then_inc(drop_placed, 1)

            def sum_rows(n, h, some):
                for k in some:
                    behind = k + (k < 2)
                    wait_from(pe, adds, n * HALF + behind)
                    pe.matmul(sums[k % 3][:, 0:HW], place[:, h, k, :], rows[:, h, k, 0:HW], start=True, stop=True).then_inc(summed, 1)

            def both(n, h, pair):
                turn(n + 1, 1 - h, pair)
                wait_from(pe, weighted, n + 1)
                sum_rows(n, h, range(0, 4))
                turn_peaks(n + 1)
                sum_rows(n, h, range(4, HALF))
                place_drop(n + 1, 1 - h)

            pe.sem_inc(summed, AHEAD)
            turn(0, 0, 0)
            turn_peaks(0)
            place_drop(0, 0)
            for i in rounds_of(pe, halves_count // 2):
                both(i * 2, 0, i)
                both(i * 2 + 1, 1, i + 1)

        def scalar(act):
            def front(n):
                for q in range(2):
                    wait_from(act, places_turned, n * 2 + q + 1)
                    wait_from(act, dst_scored, n)
                    act.copy(placeT[:, q, :, :].rearrange("p k n -> p (k n)"), ps[2 + q][:, :]).then_inc(placesT_ready, 1)
                wait_from(act, exp_in, n + 1)
                act.activation(weight[:, :, :], sc[:, 1, 0:HALF, :], ACT.Exp).then_inc(exp_out, 1)
                wait_from(act, drop_placed, n + 1)
                act.activation(scale[:, :], small[:, DROPS:DROPS + H1], ACT.Exp).then_inc(scale_ready, 1)

            front(0)
            with act.Fori(1, halves_count + 1) as n:
                front(n)

        def vector(dve):
            def put_places(n, h):
                wait_from(dve, summed, n * HALF + HALF)
                dve.tensor_tensor(place[:, h, :, :], g["iota_row"][:, :].unsqueeze(1).broadcast_to([P, HALF, P]),
                                  local_key[:, ds(n * HALF, HALF)].unsqueeze(2).broadcast_to([P, HALF, P]), ALU.is_equal).then_inc(placed, 1)

            def scan_runs(n, h, pair):
                ch = Chain(dve, scan_own, n * 3)
                wait_from(dve, src_turned, n + 1)
                wait_from(dve, cut_loaded[h], (pair + 1) * 32)
                wait_from(dve, peaks_turned, n)
                carried = upto_edge[:, 1 - h, HE - 1:HE]
                ch.link(dve.tensor_tensor_scan(upto_edge[:, h, :], cuts[:, h, 0, :], banks01[0:H1, :], carried, ALU.add, ALU.max))
                ch.link(dve.tensor_tensor_scan(run_peak[:, HE - 1::-1], cuts[:, h, 1, ::-1], upto_edge[:, h, ::-1], -FAR, ALU.add, ALU.max))
                ch.link(dve.tensor_scalar(fresh[:, :], run_peak[:, 0:1], goes_on[:, ds(n, 1)], None, ALU.add))
                dve.scalar_tensor_tensor(out=run_peak[:, HE:HE + 1], in0=carried, scalar=cuts[:, h, 0, 0:1], in1=fresh[:, :],
                                         op0=ALU.add, op1=ALU.max).then_inc(runs_made, 1)

            def take_dst_scores(n):
                wait_from(dve, dst_scored, n + 1)
                dve.tensor_copy(sc[:, 0, :, :].rearrange("p s h -> p (s h)"), small[:, 0:PEAKS]).then_inc(dst_taken, 1)

            def edge_scores(n, h):
                ch = Chain(dve, scores_own, n * 3)
                wait_from(dve, dst_taken, n + 1)
                wait_from(dve, peaks_turned, n + 1)
                ch.step(dve.tensor_tensor(sc[:, 1, 0:HALF, :], rows[:, h, :, HW:RW], sc[:, 0, 0:HALF, :], ALU.add))
                ch.link(dve.tensor_tensor(sc[:, 2, :, :].rearrange("p s h -> p (s h)"), small[:, PEAKS:DROPS],
                                          sc[:, 0, :, :].rearrange("p s h -> p (s h)"), ALU.add))
                both_sc = sc[:, 1:3, :, :].rearrange("p a s h -> p (a s h)")
                ch.link(dve.scalar_tensor_tensor(out=both_sc, in0=both_sc, scalar=0.2, in1=both_sc, op0=ALU.mult, op1=ALU.max))
                dve.tensor_tensor(sc[:, 1, 0:HALF, :], sc[:, 1, 0:HALF, :], sc[:, 2, 0:HALF, :], ALU.subtract).then_inc(exp_in, 1)
                dve.tensor_tensor(drop[:, :], sc[:, 2, HALF, :], sc[:, 2, 0, :], ALU.subtract).then_inc(drop_ready, 1)

            def weigh(n, h):
                wait_from(dve, exp_out, n + 1)
                blocks = rows[:, h, :, 0:HW].rearrange("p s (h b) -> p s h b", b=HB)
                dve.tensor_tensor(blocks, blocks, weight[:, :, :].unsqueeze(3).broadcast_to([P, HALF, H1, HB]), ALU.mult).then_inc(weighted, 1)

            def load_tiles(n):
                return [dve.value_load(tile_of[0:1, ds(n * HALF + k, 1)], min_val=0, max_val=NT - 1) for k in range(HALF)]

            def rescale(n, tiles):
                blocks = row(acc, tiles[0]).rearrange("p (h b) -> p h b", b=HB)
                wait_from(dve, scale_ready, n + 1)
                wait_from(dve, adds, n * HALF + ADDS_AHEAD)
                dve.tensor_tensor(blocks, blocks, scale[:, :].unsqueeze(2).broadcast_to([P, H1, HB]), ALU.mult).then_inc(scaled, 1)
                wait_from(dve, scaled, n + 1)

            def add_sums(n, tiles, some):
                for k in some:
                    here = row(acc, tiles[k])
                    wait_from(dve, summed, n * HALF + k + 1 + AHEAD)
                    wait_from(dve, adds, n * HALF + k + ADDS_AHEAD)
                    dve.tensor_tensor(here, sums[k % 3][:, 0:HW], here, ALU.add).then_inc(adds, 1)

            def both(n, h, pair):
                scan_runs(n + 1, 1 - h, pair)
                tiles = load_tiles(n)
                take_dst_scores(n + 1)
                rescale(n, tiles)
                add_sums(n, tiles, range(0, 4))
                edge_scores(n + 1, 1 - h)
                add_sums(n, tiles, range(4, HALF))
                weigh(n + 1, 1 - h)
                put_places(n + 2, h)

            dve.memset(upto_edge[:, 1, HE - 1:HE], -FAR).then_inc(ready, 1)
            dve.memset(run_peak[:, :], 0.0).then_inc(ready, 1)
            dve.memset(sc[:, :, :, :], 0.0).then_inc(ready, 1)
            dve.wait_ge(goes_on_loaded, 16)
            dve.tensor_scalar(goes_on[:, :], goes_on[:, :], -1.0, -FAR, ALU.mult, ALU.add).then_inc(ready, 1)
            dve.sem_inc(adds, ADDS_AHEAD)
            dve.wait_ge(ready, 4)
            put_places(0, 0)
            put_places(1, 1)
            scan_runs(0, 0, 0)
            take_dst_scores(0)
            edge_scores(0, 0)
            weigh(0, 0)
            for i in rounds_of(dve, halves_count // 2):
                both(i * 2, 0, i)
                both(i * 2 + 1, 1, i + 1)

        run_block(nc, {"gpsimd": gpsimd, "sync": sync, "tensor": tensor, "scalar": scalar, "vector": vector})

    with ExitStack() as c2:
        den = sb("gx_den", [P, NT, H1], F32, c2)
        many = 10
        out_rows = sb("gx_out", [P, many, D], F32, c2)
        own = sem("gx_own")

        def vector(dve):
            ch = Chain(dve, own)
            blocks = acc[:, :, :].rearrange("p t (h b) -> p t h b", b=HB)
            ch.link(dve.tensor_scalar(den[:, :, :], blocks[:, :, :, F1], 1e-8, None, ALU.add))
            ch.link(dve.reciprocal(den[:, :, :], den[:, :, :]))
            start = ch.n
            with dve.Fori(0, NT // many) as i:
                ch.enter(i * 2 + start)
                tiles = ds(i * many, many)
                ch.link(dve.tensor_tensor(out_rows[:, :, :].rearrange("p t (h f) -> p t h f", f=F1), blocks[:, tiles, :, 0:F1],
                                          den[:, tiles, :].unsqueeze(3).broadcast_to([P, many, H1, F1]), ALU.mult))
                ch.link(dve.tensor_tensor(X[:, tiles, :], X[:, tiles, :], out_rows[:, :, :], ALU.add))

        run_block(nc, {"vector": vector})


HID, NE = 1024, 8
HC = HID // P
XW = D + 5
ESTEPS = LASTT + 1 + NE - 1


def laps(eng, body, count):
    whole = (count - 1) // 4
    for t in range(4):
        body(t, t, 0)
    with eng.Fori(1, whole) as i:
        for v in range(4):
            body(i * 4 + v, v, i)
    for t in range(4 * whole, count):
        body(t, t % 4, t // 4)


def hidden(g, c, pre, count, stage, product, consume):
    nc, sb, sem, ps, ident, w1, b1 = (g[n] for n in ("nc", "sb", "sem", "ps", "ident", "w1", "b1"))
    rows = sb(pre + "rows", [P, 2, D], F32, c)
    zT = sb(pre + "zT", [P, 2, 2, P], F32, c)
    hT = sb(pre + "hT", [P, 2, HC, P], F32, c)
    staged, turned, zt_ready, h_done, gelu_done, produced, taken = (
        sem(pre + n) for n in ("staged", "turned", "zt_ready", "h_done", "gelu_done", "produced", "taken"))

    def after(slot, lap):
        return (slot + 1) % 4, lap + (slot == 3)

    def vector(dve):
        def stage_of(t, slot, lap):
            wait_from(dve, turned, t - 1)
            stage(dve, t, slot, lap, rows[:, slot % 2, :]).then_inc(staged, 1)

        def consume_of(t, slot, lap):
            wait_from(dve, produced, t + 1)
            consume(dve, t, slot, lap, lambda ins: ins.then_inc(taken, 1))

        def body(t, slot, lap):
            if not isinstance(t, int) or t + 1 < count:
                stage_of(t + 1, *after(slot, lap))
            if not isinstance(t, int) or t > 0:
                consume_of(t - 1, (slot - 1) % 4, lap - (slot == 0))

        stage_of(0, 0, 0)
        laps(dve, body, count)
        consume_of(count - 1, (count - 1) % 4, (count - 1) // 4)

    def scalar(act):
        def turn_copy(t, u):
            wait_from(act, turned, t + 1)
            wait_from(act, h_done, (t - 1) * 2)
            act.copy(zT[:, u, :, :].rearrange("p k n -> p (k n)"), ps[4 + u][:, 0:2 * P]).then_inc(zt_ready, 1)

        def body(t, slot, lap):
            u = slot % 2
            if not isinstance(t, int) or t + 1 < count:
                turn_copy(t + 1, 1 - u)
            wait_from(act, produced, t - 1)
            for m in range(HC):
                if m % 4 == 0:
                    wait_from(act, h_done, t * 2 + m // 4 + 1)
                act.activation(hT[:, u, m, :], ps[2 * u + m // 4][:, (m % 4) * P:(m % 4 + 1) * P], ACT.Gelu,
                               bias=b1[:, m:m + 1]).then_inc(gelu_done, 1)

        turn_copy(0, 0)
        laps(act, body, count)

    def tensor(pe):
        pe.wait_ge(g["w_loaded"], g["w_count"])

        def turn(t, u):
            wait_from(pe, staged, t + 1)
            wait_from(pe, zt_ready, t - 1)
            for k in range(2):
                mm = pe.transpose(ps[4 + u][:, k * P:(k + 1) * P], rows[:, u, k * P:(k + 1) * P], ident[:, :])
            mm.then_inc(turned, 1)

        def produce(t, u):
            wait_from(pe, gelu_done, (t + 1) * HC)
            wait_from(pe, taken, t - 1)
            product(pe, t, u, hT[:, u, :, :]).then_inc(produced, 1)

        def body(t, slot, lap):
            u = slot % 2
            if not isinstance(t, int) or t + 1 < count:
                turn(t + 1, 1 - u)
            wait_from(pe, zt_ready, t + 1)
            wait_from(pe, gelu_done, (t - 1) * HC)
            for m in range(HC):
                for k in range(2):
                    mm = pe.matmul(ps[2 * u + m // 4][:, (m % 4) * P:(m % 4 + 1) * P], w1[:, k, m * P:(m + 1) * P], zT[:, u, k, :],
                                   start=(k == 0), stop=(k == 1))
                if m % 4 == 3:
                    mm.then_inc(h_done, 1)
            if not isinstance(t, int) or t > 0:
                produce(t - 1, 1 - u)

        turn(0, 0)
        laps(pe, body, count)
        produce(count - 1, (count - 1) % 2)

    return {"vector": vector, "scalar": scalar, "tensor": tensor, "taken": taken}


def routed_network(g, c, out):
    nc, sb, sem, ps, X, ident = (g[n] for n in ("nc", "sb", "sem", "ps", "X", "ident"))
    routed_rows = nc.dram_tensor("routed_rows", [NT * P, XW], F32)
    tile_of_estep = nc.dram_tensor("tile_of_estep", [2, 64], I32)
    w1 = g["w1"] = sb("w1", [P, 2, HID], F32, c)
    b1 = g["b1"] = sb("b1", [P, HC], F32, c)
    wg = sb("wg", [P, HC, NE], F32, c)
    bg = sb("bg", [P, NE], F32, c)
    wd = sb("wd", [P, NE, HC, D], F32, c)
    bd = sb("bd", [P, NE, D], F32, c)
    gates = sb("gates", [P, NT, NE], F32, c)
    w_loaded = g["w_loaded"] = sem("ffn_w_loaded")
    g["w_count"] = 64
    expert_of = sb("expert_of", [P, 64], F32, c)
    step_tables = sb("step_tables", [1, 2, 64], I32, c)
    mean, rstd, norm_vector, norm_scalar = row_norm(g, c, "ln3")

    with ExitStack() as c2:
        def stage(dve, t, slot, lap, to):
            return dve.tensor_scalar(to, row(X, t), mean[:, ds(t, 1)], rstd[:, ds(t, 1)], ALU.subtract, ALU.mult)

        def product(pe, t, u, hT):
            for m in range(HC):
                mm = pe.matmul(ps[6 + u][:, 0:NE], hT[:, m, :], wg[:, m, :], start=(m == 0), stop=(m == HC - 1))
            return mm

        def consume(dve, t, slot, lap, signal):
            signal(dve.tensor_tensor(row(gates, t), ps[6 + slot % 2][:, 0:NE], bg[:, :], ALU.add))

        programs = hidden(g, c2, "fa_", NT, stage, product, consume)

        def vector(dve):
            norm_vector(dve)
            dve.wait_ge(w_loaded, 64)
            programs["vector"](dve)

        def scalar(act):
            norm_scalar(act)
            act.wait_ge(w_loaded, 64)
            programs["scalar"](act)

        def sync(sp):
            sp.dma_start(w1[:, :, :], g["L1_ffn_W1"].rearrange("(k p) n -> p k n", p=P)).then_inc(w_loaded, 16)
            with nc.allow_non_contiguous_dma(reason="1024 numbers"):
                sp.dma_start(b1[:, :], g["L1_ffn_b1"].rearrange("(m p) -> p m", p=P)).then_inc(w_loaded, 16)
            sp.dma_start(wg[:, :, :], g["L1_ffn_Wg"].rearrange("(m p) e -> p m e", p=P)).then_inc(w_loaded, 16)
            sp.dma_start(bg[:, :], g["L1_ffn_bg"].rearrange("(a e) -> a e", a=1).broadcast_to([P, NE])).then_inc(w_loaded, 16)
            sp.wait_ge(w_loaded, 64)
            for e in range(NE):
                sp.dma_start(wd[:, e, :, :], g["L1_ffn_Wd"][e].rearrange("(m p) d -> p m d", p=P)).then_inc(w_loaded, 16)
            sp.dma_start(bd[:, :, :].rearrange("p e d -> p (e d)"), g["L1_ffn_bd"].rearrange("(a e) d -> a (e d)", a=1).broadcast_to([P, NE * D])).then_inc(w_loaded, 16)
            sp.wait_ge(w_loaded, 64 + 16 * (NE + 1))

        run_block(nc, {"sync": sync, "vector": vector, "scalar": scalar, "tensor": programs["tensor"]})

    with ExitStack() as c2:
        NB = NE + 1
        top = sb("rt_top", [P, NT], F32, c2)
        tot = sb("rt_tot", [P, NT], F32, c2)
        cand = sb("rt_cand", [P, NT, NE], F32, c2)
        extra = sb("rt_extra", [P, NT, 5], F32, c2)
        pad = sb("rt_pad", [P, NT], F32, c2)
        mask = sb("rt_mask", [P, NT], F32, c2)
        mask_u = sb("rt_mask_u", [P, NT], U32, c2)
        count = sb("rt_count", [P, NB], F32, c2)
        total = sb("rt_total", [P, NB], F32, c2)
        upto_b = sb("rt_upto", [P, NB], F32, c2)
        base = sb("rt_base", [P, NB], F32, c2)
        border_i = sb("rt_border_i", [P, NB], I32, c2)
        border = sb("rt_border", [P, NB], F32, c2)
        rank = sb("rt_rank", [P, NT], F32, c2)
        pos = sb("rt_pos", [P, NT], F32, c2)
        pos_u = sb("rt_pos_u", [P, NT], U32, c2)
        steps_i = sb("rt_steps_i", [P, 2, 64], I32, c2)
        steps_f = sb("rt_steps_f", [P, 64], F32, c2)
        hit = sb("rt_hit", [P, 64], F32, c2)
        ring = sb("rt_ring", [P, 2, XW], F32, c2)
        ring_pos = sb("rt_ring_pos", [P, 2, 1], U32, c2)
        own, exp_in, exp_out, counted, totals, pos_ready, ring_ready, ring_at, steps_ready, tables_in = (
            sem("rt_" + n) for n in ("own", "exp_in", "exp_out", "counted", "totals", "pos_ready", "ring_ready", "ring_at",
                                     "steps_ready", "tables_in"))
        scattered = [sem(f"rt_scattered{u}") for u in range(2)]
        pool_passed = sem("rt_pool_passed")

        def vector(dve):
            ch = Chain(dve, own)
            ch.link(dve.tensor_reduce(top[:, :], gates[:, :, :], AX.X, ALU.max))
            dve.tensor_tensor(gates[:, :, :], gates[:, :, :], top[:, :].unsqueeze(2).broadcast_to([P, NT, NE]), ALU.subtract).then_inc(exp_in, 1)
            dve.wait_ge(exp_out, 1)
            ch.link(dve.tensor_reduce(tot[:, :], gates[:, :, :], AX.X, ALU.add))
            ch.link(dve.reciprocal(extra[:, :, 0], tot[:, :]))
            ch.link(dve.tensor_scalar(cand[:, :, :], gates[:, :, :], 1.0, float(NB), ALU.is_lt, ALU.mult))
            ch.link(dve.tensor_tensor(cand[:, :, :], cand[:, :, :], g["iota_row"][:, 0:NE].unsqueeze(1).broadcast_to([P, NT, NE]), ALU.add))
            ch.link(dve.tensor_reduce(extra[:, :, 1], cand[:, :, :], AX.X, ALU.min))
            ch.link(dve.tensor_scalar(extra[:, :, 2], g["iota_row"][:, 0:NT], float(P), None, ALU.mult))
            ch.link(dve.tensor_scalar(extra[:, :, 2], extra[:, :, 2], g["iota_part"][:, 0:1], None, ALU.add))
            ch.link(dve.tensor_scalar(pad[:, :], extra[:, :, 2], float(N), float(NE), ALU.is_ge, ALU.mult))
            ch.link(dve.tensor_tensor(extra[:, :, 1], extra[:, :, 1], pad[:, :], ALU.max))
            ch.step(dve.tensor_copy(extra[:, :, 3], mean[:, :]))
            ch.step(dve.tensor_copy(extra[:, :, 4], rstd[:, :]))
            for b in range(NB):
                ch.link(dve.tensor_scalar(mask[:, :], extra[:, :, 1], float(b), 0.0, ALU.is_equal, ALU.add, accum_out=count[:, b:b + 1]))
            dve.sem_inc(counted, 1)
            dve.wait_ge(totals, 1)
            ch.link(dve.tensor_copy(total[:, :], ps[0][:, 0:NB]))
            ch.link(dve.tensor_tensor_scan(upto_b[:, :], total[:, :], total[:, :], 0.0, ALU.add, ALU.bypass))
            ch.link(dve.tensor_tensor(upto_b[:, :], upto_b[:, :], total[:, :], ALU.subtract))
            ch.link(dve.scalar_tensor_tensor(out=base[:, :], in0=ps[1][:, 0:NB], scalar=-1.0, in1=upto_b[:, :], op0=ALU.add, op1=ALU.add))
            ch.link(dve.memset(pos[:, :], 0.0))
            for b in range(NB):
                ch.link(dve.tensor_scalar(mask_u[:, :], extra[:, :, 1], float(b), None, ALU.is_equal))
                ch.link(dve.tensor_tensor_scan(rank[:, :], mask_u[:, :], mask_u[:, :], base[:, b:b + 1], ALU.add, ALU.bypass))
                ch.link(dve.copy_predicated(pos[:, :], mask_u[:, :], rank[:, :]))
            dve.tensor_copy(pos_u[:, :], pos[:, :]).then_inc(pos_ready, 1)
            ch.link(dve.tensor_copy(border_i[:, :], upto_b[:, :]))
            ch.link(dve.tensor_scalar(border_i[:, :], border_i[:, :], 7, None, ALU.logical_shift_right))
            ch.link(dve.tensor_copy(border[:, :], border_i[:, :]))
            ch.link(dve.tensor_tensor(border[:, :], border[:, :], g["iota_row"][:, 0:NB], ALU.add))
            ch.link(dve.memset(expert_of[:, :], 0.0))
            for b in range(1, NE):
                ch.link(dve.tensor_scalar(hit[:, :], g["iota_row"][:, 0:64], border[:, b:b + 1], None, ALU.is_ge))
                ch.link(dve.tensor_tensor(expert_of[:, :], expert_of[:, :], hit[:, :], ALU.add))
            ch.link(dve.tensor_tensor(steps_f[:, :], g["iota_row"][:, 0:64], expert_of[:, :], ALU.subtract))
            ch.link(dve.tensor_copy(steps_i[:, 0, :], steps_f[:, :]))
            ch.link(dve.tensor_copy(steps_i[:, 1, :], expert_of[:, :]))
            ch.link(dve.tensor_scalar(steps_i[:, 0, :], steps_i[:, 0, :], P, None, ALU.mult))
            ch.link(dve.tensor_copy(step_tables[:, :, :], steps_i[0:1, :, :]))
            dve.sem_inc(steps_ready, 1)
            start = ch.n
            for i in rounds_of(dve, NT // 2):
                for u in range(2):
                    t = i * 2 + u
                    wait_from(dve, scattered[u], i * 16)
                    dve.tensor_copy(ring[:, u, 0:D], row(X, t)).then_inc(ring_ready, 1)
                    dve.tensor_copy(ring[:, u, D:XW], row(extra, t)).then_inc(ring_ready, 1)

        def scalar(act):
            act.wait_ge(exp_in, 1)
            act.activation(gates[:, :, :], gates[:, :, :], ACT.Exp).then_inc(exp_out, 1)

        def tensor(pe):
            pe.wait_ge(counted, 1)
            pe.matmul(ps[0][:, 0:NB], g["ones"][:, :], count[:, :], start=True, stop=True)
            pe.matmul(ps[1][:, 0:NB], g["before"][:, :], count[:, :], start=True, stop=True).then_inc(totals, 1)

        def gpsimd(pool):
            pool.wait_ge(pos_ready, 1)
            for i in rounds_of(pool, NT // 2):
                for u in range(2):
                    t = i * 2 + u
                    wait_apart(pool, scattered[u], i * 16, pool_passed)
                    pool.tensor_copy(ring_pos[:, u, :], pos_u[:, ds(t, 1)]).then_inc(ring_at, 1)
                    wait_apart(pool, ring_at, t + 1, pool_passed)
                    wait_apart(pool, ring_ready, t * 2 + 2, pool_passed)
                    pool.indirect_dma_start(out=routed_rows[:, :], out_offset=bass.IndirectOffsetOnAxis(ap=ring_pos[:, u, :], axis=0),
                                            in_=ring[:, u, :], in_offset=None).then_inc(scattered[u], 16)
            for u in range(2):
                pool.wait_ge(scattered[u], 16 * (NT // 2))

        run_block(nc, {"vector": vector, "scalar": scalar, "tensor": tensor, "gpsimd": gpsimd})

    with ExitStack() as c2:
        xr = sb("ex_rows", [P, 4, XW], F32, c2)
        result = sb("ex_result", [P, 2, D], F32, c2)
        target = sb("ex_target", [P, 2, 1], F32, c2)
        target_u = sb("ex_target_u", [P, 4, 1], U32, c2)
        own, result_ready, target_ready = (sem("ex_" + n) for n in ("own", "result_ready", "target_ready"))
        loaded = [sem(f"ex_loaded{k}") for k in range(4)]
        scattered = [sem(f"ex_scattered{u}") for u in range(2)]
        pool_passed = sem("ex_pool_passed")

        def pair_of(slot, lap):
            return lap * 2 + slot // 2

        def stage(dve, t, slot, lap, to):
            wait_from(dve, loaded[slot], (lap + 1) * 16)
            return dve.tensor_scalar(to, xr[:, slot, 0:D], xr[:, slot, D + 3:D + 4], xr[:, slot, D + 4:D + 5], ALU.subtract, ALU.mult)

        def product(pe, t, u, hT):
            e = pe.value_load(step_tables[0:1, 1, ds(t, 1)], min_val=0, max_val=NE - 1)
            for m in range(HC):
                w = wd[:, ds(e, 1), m, :].rearrange("p a d -> p (a d)")
                mm = pe.matmul(ps[6 + u][:, 0:D], hT[:, m, :], w, start=(m == 0), stop=(m == HC - 1))
            return mm

        def consume(dve, t, slot, lap, signal):
            u = slot % 2
            ch = Chain(dve, own, t * 3)
            e = dve.value_load(step_tables[0:1, 1, ds(t, 1)], min_val=0, max_val=NE - 1)
            ch.link(dve.tensor_scalar(target[:, u, :], xr[:, slot, D + 1:D + 2], expert_of[:, ds(t, 1)], float(NT * P), ALU.not_equal, ALU.mult))
            ch.link(dve.tensor_tensor(target[:, u, :], target[:, u, :], xr[:, slot, D + 2:D + 3], ALU.add))
            ch.link(dve.tensor_copy(target_u[:, slot, :], target[:, u, :]))
            wait_from(dve, scattered[u], pair_of(slot, lap) * 16)
            signal(dve.tensor_tensor(result[:, u, :], ps[6 + u][:, 0:D], bd[:, ds(e, 1), :].rearrange("p a d -> p (a d)"), ALU.add))
            wait_from(dve, programs["taken"], t + 1)
            dve.scalar_tensor_tensor(out=result[:, u, :], in0=result[:, u, :], scalar=xr[:, slot, D:D + 1], in1=xr[:, slot, 0:D],
                                     op0=ALU.mult, op1=ALU.add).then_inc(result_ready, 1)

        programs = hidden(g, c2, "fb_", ESTEPS, stage, product, consume)

        def sync(sp):
            def body(t, slot, lap):
                wait_from(sp, result_ready, t - 2)
                first = sp.value_load(step_tables[0:1, 0, ds(t, 1)], min_val=0, max_val=(NT - 1) * P)
                sp.dma_start(xr[:, slot, :], routed_rows[ds(first, P), :]).then_inc(loaded[slot], 16)
            laps(sp, body, ESTEPS)

        def gpsimd(pool):
            def body(t, slot, lap):
                wait_apart(pool, result_ready, t + 2, pool_passed)
                pool.indirect_dma_start(out=out[:, :], out_offset=bass.IndirectOffsetOnAxis(ap=target_u[:, slot, :], axis=0),
                                        in_=result[:, slot % 2, :], in_offset=None, bounds_check=N - 1, oob_is_err=False).then_inc(scattered[slot % 2], 16)
            laps(pool, body, ESTEPS)
            for u in range(2):
                pool.wait_ge(scattered[u], 16 * (ESTEPS // 2))

        def vector(dve):
            dve.sem_inc(result_ready, 1)
            hidden_vector(dve)

        hidden_vector = programs["vector"]
        programs = {**programs, "vector": vector, "sync": sync, "gpsimd": gpsimd}
        run_block(nc, programs)


INPUTS = ["x", "src", "dst", "L0_gnn_W", "L0_gnn_envW", "L0_gnn_envb", "L0_ffn_W_fx", "L0_ffn_b_fx", "L0_ffn_W_x", "L0_ffn_b_x",
          "L0_ffn_W_slice", "L0_ffn_b_slice", "L0_ffn_W_q", "L0_ffn_W_k", "L0_ffn_W_v", "L0_ffn_W_out", "L0_ffn_b_out",
          "L0_ffn_temperature", "L1_gnn_W", "L1_gnn_a_src", "L1_gnn_a_dst", "L1_ffn_W1", "L1_ffn_b1", "L1_ffn_Wg", "L1_ffn_bg",
          "L1_ffn_Wd", "L1_ffn_bd"]


def kernel(**inputs):
    import numpy as np
    import concourse.bacc as bacc
    from concourse.bass_utils import run_bass_kernel_spmd

    nc = bacc.Bacc("TRN2", target_bir_lowering=False, num_devices=1)
    arrays, args = {}, {}
    for name in INPUTS:
        arrays[f"in_{name}"] = a = np.ascontiguousarray(inputs[name])
        args[name] = nc.dram_tensor(f"in_{name}", a.shape, mybir.dt.from_np(a.dtype), kind="ExternalInput").ap()
    out = nc.dram_tensor("out", (N, D), F32, kind="ExternalOutput").ap()
    build(nc, out, **args)
    result = run_bass_kernel_spmd(nc, [arrays], core_ids=[0])
    return result.results[0]["out"]
```

```python
import concourse.bass as bass
from concourse import mybir
from concourse.alu_op_type import AluOpType as ALU
from contextlib import ExitStack

ACT = mybir.ActivationFunctionType
AX = mybir.AxisListType
F32 = mybir.dt.float32
BF16 = mybir.dt.bfloat16
U16 = mybir.dt.uint16
I32 = mybir.dt.int32
U32 = mybir.dt.uint32

P = 128
N = 6250
D = 256
E = 100000
NT = 50
NFULL = N // P
NREST = N - NFULL * P
LASTT = NFULL
COLS = 784
EPAD = P * COLS
EREST = E - (P - 1) * COLS
PADKEY = 49 * P
STEPS = 832
GROUPS = 7
SG = GROUPS * P
K0 = 4
HALF = 8
FAR = 1e30
ds = bass.ds


class Chain:

    def __init__(self, eng, sem, at=0):
        self.eng, self.sem, self.at, self.n = eng, sem, at, 0

    def step(self, ins):
        ins.then_inc(self.sem, 1)
        self.n += 1
        return ins

    def wait(self):
        self.eng.wait_ge(self.sem, self.at + self.n)

    def link(self, ins):
        self.step(ins)
        self.wait()
        return ins

    def enter(self, at):
        self.at, self.n = at, 0


def build(nc, out, *, x, src, dst, L0_gnn_W, L0_gnn_envW, L0_gnn_envb, L0_ffn_W_fx, L0_ffn_b_fx, L0_ffn_W_x,
          L0_ffn_b_x, L0_ffn_W_slice, L0_ffn_b_slice, L0_ffn_W_q, L0_ffn_W_k, L0_ffn_W_v, L0_ffn_W_out,
          L0_ffn_b_out, L0_ffn_temperature, L1_gnn_W, L1_gnn_a_src, L1_gnn_a_dst, L1_ffn_W1, L1_ffn_b1,
          L1_ffn_Wg, L1_ffn_bg, L1_ffn_Wd, L1_ffn_bd):
    with ExitStack() as top:
        stage_sems = []

        def sem(name):
            stage_sems.append(nc.alloc_semaphore(name=name))
            return stage_sems[-1]

        def stage_ends():
            nc.clear_and_free_semaphores(stage_sems)
            stage_sems.clear()
            nc.all_engine_barrier()

        def sb(name, shape, dt=F32, ctx=top):
            return ctx.enter_context(nc.sbuf_tensor(name, shape, dt))

        z_rows = [nc.dram_tensor(f"z_rows{l}", [NT * P, D], F32) for l in range(2)]
        pairs = [nc.dram_tensor(f"pairs_{q}", [EPAD // P, 2 * P], I32) for q in ("src", "dst")]
        four_tiles_dram = nc.dram_tensor("four_tiles_dram", [2, SG // 4], I32)

        key_by_dst = nc.dram_tensor("key_by_dst", [P, SG], F32)
        row_by_dst = nc.dram_tensor("row_by_dst", [P, SG], U32)

        cuts_dram = nc.dram_tensor("cuts_dram", [2, SG * P], F32)
        ends_dram = nc.dram_tensor("ends_dram", [2, SG + 2], F32)

        X = sb("X", [P, NT, D])
        iota_row = sb("iota_row", [P, P])
        iota_part = sb("iota_part", [P, 1])
        step_index = sb("step_index", [P, GROUPS])
        ident = sb("ident", [P, P])
        before = sb("before", [P, P])
        ones = sb("ones", [P, P])
        eps_ln = sb("eps_ln", [P, 1])
        banks01 = top.enter_context(nc.psum_tensor("banks01", [P, 1024], F32))
        ps = [banks01[:, 0:512], banks01[:, 512:1024]] + [
            top.enter_context(nc.psum_tensor(f"bank{b}", [P, 512], F32)) for b in range(2, 8)]

        g = dict(locals())
        constants(g)
        graph_mixture(g)
        stage_ends()
        with ExitStack() as c:
            slice_attention(g, c)
        stage_ends()
        with ExitStack() as c:
            graph_attention(g, c)
        stage_ends()
        with ExitStack() as c:
            routed_network(g, c, out)


def graph_mixture(g):
    nc, sb = g["nc"], g["sb"]
    with ExitStack() as c1:
        g["local_key"] = sb("local_key", [P, SG], ctx=c1)
        g["row_of"] = sb("row_of", [P, SG], U32, c1)
        g["four_tiles"] = sb("four_tiles", [1, SG // 4], I32, c1)
        g["Z"] = sb("Z", [P, NT, D], ctx=c1)
        g["mix"] = sb("mix", [P, NT, K0], ctx=c1)
        with ExitStack() as c2:
            edge_tables(g, c2)
        with ExitStack() as c3:
            g["A"] = sb("A", [P, NT, D + 1], ctx=c3)
            for layer in range(2):
                if layer == 1:
                    with ExitStack() as c4:
                        run_block(nc, mixture(g, c4, layer, "own"))
                with ExitStack() as c4:
                    run_block(nc, gather_sum(g, c4, layer))
                with ExitStack() as c4:
                    run_block(nc, mixture(g, c4, layer, "agg"))


def constants(g):
    nc, X, sem, sb = g["nc"], g["X"], g["sem"], g["sb"]
    x_loaded, const_made, iota_made, own = (sem(n) for n in ("x_loaded", "const_made", "iota_made", "const_own"))
    with ExitStack() as c:
        irow = sb("irow", [P, P], I32, c)
        ipart = sb("ipart", [P, 1], I32, c)
        istep = sb("istep", [P, GROUPS], I32, c)
        block = c.enter_context(nc.Block())

        @block.gpsimd
        def _(pool):
            nc.gpsimd.iota(irow[:, :], [[1, P]], base=0, channel_multiplier=0).then_inc(iota_made, 1)
            nc.gpsimd.iota(ipart[:, :], [[0, 1]], base=0, channel_multiplier=1).then_inc(iota_made, 1)
            nc.gpsimd.iota(istep[:, :], [[P, GROUPS]], base=0, channel_multiplier=1).then_inc(iota_made, 1)

        @block.vector
        def _(dve):
            ch = Chain(dve, own)
            dve.memset(X[:, LASTT:NT, :], 0.0).then_inc(const_made, 1)
            dve.memset(g["ones"][:, :], 1.0)
            dve.memset(g["eps_ln"][:, :], 1e-5)
            dve.wait_ge(iota_made, 3)
            ch.step(dve.tensor_copy(g["iota_row"][:, :], irow[:, :]))
            ch.step(dve.tensor_copy(g["iota_part"][:, :], ipart[:, :]))
            dve.tensor_copy(g["step_index"][:, :], istep[:, :])
            ch.wait()
            dve.tensor_scalar(g["ident"][:, :], g["iota_row"][:, :], g["iota_part"][:, 0:1], None, ALU.is_equal)
            dve.tensor_scalar(g["before"][:, :], g["iota_row"][:, :], g["iota_part"][:, 0:1], None, ALU.is_gt)

        @block.sync
        def _(sp):
            sp.dma_start(X[:, 0:NFULL, :], g["x"][0:NFULL * P, :].rearrange("(t p) d -> p t d", p=P)).then_inc(x_loaded, 16)
            sp.wait_ge(const_made, 1)
            sp.dma_start(X[0:NREST, LASTT, :], g["x"][NFULL * P:N, :]).then_inc(x_loaded, 16)
            sp.wait_ge(x_loaded, 32)


def edge_tables(g, c):
    nc, sb, sem, ps, X = g["nc"], g["sb"], g["sem"], g["ps"], g["X"]
    ones, before, ident, iota_row = g["ones"], g["before"], g["ident"], g["iota_row"]
    keys = [sb(f"keys{q}", [P, COLS], I32, c) for q in range(2)]
    bucket_i = sb("bucket_i", [P, COLS], I32, c)
    bucket = [sb(f"bucket{q}", [P, COLS], BF16, c) for q in range(2)]
    mask = sb("mask", [P, 2, COLS], U16, c)
    rank = sb("rank", [P, 2, COLS], F32, c)
    pos = sb("pos", [P, COLS], F32, c)
    pos_u = sb("pos_u", [P, COLS], U32, c)
    pay = [sb(f"pay{q}", [P, COLS, 2], I32, c) for q in range(2)]
    count = sb("count", [P, 2, NT], F32, c)
    total = sb("total", [P, 2, NT], F32, c)
    upto_b = sb("upto_b", [P, 2, NT], F32, c)
    first = sb("first", [P, 2, NT], F32, c)
    base = sb("base", [P, NT], F32, c)
    first_i = sb("first_i", [P, 2, NT], I32, c)
    border = sb("border", [P, 2, NT], F32, c)
    ring_pos = sb("ring_pos", [P, 2, HALF], U32, c)
    ring_pay = sb("ring_pay", [P, 2, HALF, 2], I32, c)
    edges_loaded, cleared, ranked, added, totals_ready, pos_ready, pay_ready, own, pool_own = (
        sem(n) for n in ("edges_loaded", "cleared", "ranked", "added", "totals_ready", "pos_ready", "pay_ready", "tab_own",
                         "tab_pool_own"))
    counted = [sem(f"counted{q}") for q in range(2)]
    scattered = [sem(f"scattered{h}") for h in range(2)]
    pool_passed = sem("tab_pool_passed")
    dst_stored = sem("dst_stored")
    per_half = COLS // (2 * HALF)

    mix0 = mixture(g, c, 0, "own")
    with nc.Block() as block:
        @block.scalar
        def _(act):
            mix0["scalar"](act)

        @block.sync
        def _(sp):
            sp.wait_ge(cleared, 2)
            for q, a in enumerate((g["src"], g["dst"])):
                sp.dma_start(keys[q][0:P - 1, :], a[0:(P - 1) * COLS].rearrange("(p j) -> p j", j=COLS)).then_inc(edges_loaded, 16)
                sp.dma_start(keys[q][P - 1:P, 0:EREST], a[(P - 1) * COLS:E].rearrange("(p j) -> p j", p=1)).then_inc(edges_loaded, 16)
            sp.wait_ge(pay_ready, 4)
            sp.dma_start(g["pairs"][1][:, :].rearrange("c (e w) -> (c e) w", w=2).rearrange("(p j) w -> p (j w)", p=P), pay[1][:, :, :].rearrange("p j w -> p (j w)")).then_inc(dst_stored, 16)
            mix0["sync"](sp)
            sp.wait_ge(dst_stored, 16)

        @block.vector
        def _(dve):
            ch = Chain(dve, own)
            for q in range(2):
                dve.memset(keys[q][:, :], PADKEY).then_inc(cleared, 1)
            dve.memset(pos[:, :], 0.0).then_inc(cleared, 1)
            dve.wait_ge(edges_loaded, 64)
            for q in range(2):
                ch.link(dve.tensor_scalar(bucket_i[:, :], keys[q][:, :], 7, None, ALU.logical_shift_right))
                ch.link(dve.tensor_copy(bucket[q][:, :], bucket_i[:, :]))

            def count_edges(q):
                for i in rounds_of(dve, NT // 2):
                    for u in range(2):
                        b = i * 2 + u
                        wait_from(dve, counted[q], b - 1)
                        dve.tensor_scalar(mask[:, u, :], bucket[q][:, :], iota_row[:, ds(b, 1)], 0.0, ALU.is_equal, ALU.add,
                                          accum_out=count[:, q, ds(b, 1)]).then_inc(counted[q], 1)
                dve.wait_ge(counted[q], NT)

            def first_positions(q):
                dve.wait_ge(totals_ready, q + 1)
                ch.link(dve.tensor_copy(total[:, q, :], ps[0][:, 0:NT]))
                ch.link(dve.tensor_tensor_scan(upto_b[:, q, :], total[:, q, :], total[:, q, :], 0.0, ALU.add, ALU.bypass))
                ch.link(dve.tensor_tensor(first[:, q, :], upto_b[:, q, :], total[:, q, :], ALU.subtract))

            count_edges(0)
            first_positions(0)
            ch.link(dve.scalar_tensor_tensor(out=base[:, :], in0=ps[1][:, 0:NT], scalar=-1.0, in1=first[:, 0, :], op0=ALU.add, op1=ALU.add))
            per_pair, start = 4, ch.n
            for i in rounds_of(dve, NT // 2):
                ch.enter(i * per_pair + start)
                wait_from(dve, ranked, i * 2)
                for u in range(2):
                    ch.step(dve.tensor_scalar(mask[:, u, :], bucket[0][:, :], iota_row[:, ds(i * 2 + u, 1)], None, ALU.is_equal))
                ch.wait()
                for u in range(2):
                    wait_from(dve, added, i * 2 + u - 1)
                    ch.step(dve.tensor_tensor_scan(rank[:, u, :], mask[:, u, :], mask[:, u, :], base[:, ds(i * 2 + u, 1)], ALU.add, ALU.bypass))
                ch.wait()
                for u in range(2):
                    dve.tensor_tensor(rank[:, u, :], rank[:, u, :], mask[:, u, :], ALU.mult).then_inc(ranked, 1)
            ch.enter((NT // 2) * per_pair + start)
            for w in range(2):
                dve.tensor_copy(pay[0][:, :, w], keys[w][:, :]).then_inc(pay_ready, 1)
            dve.wait_ge(added, NT)
            dve.tensor_copy(pos_u[:, :], pos[:, :]).then_inc(pos_ready, 1)
            for w in range(2):
                dve.tensor_copy(pay[1][:, :, w], keys[1 - w][:, :]).then_inc(pay_ready, 1)
            dve.wait_ge(ranked, NT)
            count_edges(1)
            first_positions(1)
            ch.link(dve.tensor_copy(first_i[:, :, :], first[:, :, :]))
            ch.link(dve.tensor_scalar(first_i[:, :, :], first_i[:, :, :], 7, None, ALU.logical_shift_right))
            ch.link(dve.tensor_copy(border[:, :, :], first_i[:, :, :]))
            for q in range(2):
                ch.link(dve.tensor_tensor(border[:, q, :], border[:, q, :], iota_row[:, 0:NT], ALU.add))
            mix0["vector"](dve)

        @block.tensor
        def _(pe):
            pe.wait_ge(counted[0], NT)
            pe.matmul(ps[0][:, 0:NT], ones[:, :], count[:, 0, :], start=True, stop=True)
            pe.matmul(ps[1][:, 0:NT], before[:, :], count[:, 0, :], start=True, stop=True).then_inc(totals_ready, 1)
            pe.wait_ge(counted[1], NT)
            pe.matmul(ps[0][:, 0:NT], ones[:, :], count[:, 1, :], start=True, stop=True).then_inc(totals_ready, 1)
            mix0["tensor"](pe)

        @block.gpsimd
        def _(pool):
            pool.wait_ge(cleared, 3)
            for i in rounds_of(pool, NT // 2):
                for u in range(2):
                    wait_apart(pool, ranked, i * 2 + u + 1, pool_passed)
                    wait_apart(pool, added, i * 2 + u, pool_passed)
                    pool.tensor_tensor(pos[:, :], pos[:, :], rank[:, u, :], ALU.add).then_inc(added, 1)
            pool.wait_ge(pos_ready, 1)
            pool.wait_ge(pay_ready, 2)
            for i in rounds_of(pool, per_half):
                for h in range(2):
                    j = i * (2 * HALF) + h * HALF
                    wait_apart(pool, scattered[h], i * (16 * HALF), pool_passed)
                    pool.tensor_copy(ring_pos[:, h, :], pos_u[:, ds(j, HALF)]).then_inc(pool_own, 1)
                    pool.tensor_copy(ring_pay[:, h, :, :], pay[0][:, ds(j, HALF), :]).then_inc(pool_own, 1)
                    wait_apart(pool, pool_own, i * 4 + 2 * h + 2, pool_passed)
                    for k in range(HALF):
                        pool.indirect_dma_start(
                            out=g["pairs"][0][:, :].rearrange("c (e w) -> (c e) w", w=2), out_offset=bass.IndirectOffsetOnAxis(ap=ring_pos[:, h, k:k + 1], axis=0),
                            in_=ring_pay[:, h, k, :], in_offset=None).then_inc(scattered[h], 16)
            for h in range(2):
                pool.wait_ge(scattered[h], per_half * 16 * HALF)

    local_key = [g["local_key"], sb("local_key1", [P, SG], F32, c)]
    row_of = [g["row_of"], sb("row_of1", [P, SG], U32, c)]
    tile_f = sb("tile_f", [P, 2, GROUPS], F32, c)
    tiles_along = sb("tiles_along", [2 * GROUPS, P // 4, 4], F32, c)
    packed = sb("packed", [2 * GROUPS, P // 4], F32, c)
    packed_i = sb("packed_i", [2 * GROUPS, P // 4], I32, c)
    tile_key = sb("tile_key", [P, 2, GROUPS], F32, c)
    chunk_f = sb("chunk_f", [P, 2, GROUPS], F32, c)
    chunk_u = sb("chunk_u", [P, 2 * GROUPS], U32, c)
    scratch = sb("scratch", [P, NT], F32, c)
    rows_flat = sb("rows_flat", [P, 4, 2 * P], I32, c)
    rows = rows_flat[:, :, :].rearrange("p k (e w) -> p k e w", w=2)
    rows_f = sb("rows_f", [P, 2, 2, P], F32, c)
    ends = sb("ends", [P, GROUPS, 2], F32, c)
    beside = sb("beside", [P, GROUPS, 2], F32, c)
    outside = sb("outside", [1, 2], F32, c)
    cuts = sb("cuts", [P, GROUPS, 2, P], F32, c)
    cuts_made, ends_made, ends_out, beside_in, cuts_ready = (
        sem(n) for n in ("cuts_made", "ends_made", "ends_out", "beside_in", "cuts_ready"))
    chunk_ready, rows_loaded, rows_used, rows_made, turned, taken, own2, tiles_out, tiles_in = (
        sem(n) for n in ("chunk_ready", "rows_loaded", "rows_used", "rows_made", "turned", "taken", "tab_own2",
                         "tiles_out", "tiles_in"))
    tiles_turned = sem("tiles_turned")
    rows_at = [sem(f"rows_at{k}") for k in range(4)]
    n2 = 2 * GROUPS
    with nc.Block() as block:
        @block.gpsimd
        def _(pool):
            pool.wait_ge(chunk_ready, 1)
            for k in range(n2):
                q = k // GROUPS
                if k >= 4:
                    pool.wait_ge(rows_used, k - 3)
                pool.indirect_dma_start(
                    out=rows_flat[:, k % 4, :], out_offset=None,
                    in_=g["pairs"][q][:, :],
                    in_offset=bass.IndirectOffsetOnAxis(ap=chunk_u[:, k:k + 1], axis=0)).then_inc(rows_at[k % 4], 16)

        @block.vector
        def _(dve):
            ch = Chain(dve, own2)
            dve.memset(outside[:, :], -1.0).then_inc(ends_made, 1)
            for q in range(2):
                for s in range(GROUPS):
                    ch.link(dve.tensor_scalar(scratch[:, 0:48], border[:, q, 1:49], g["step_index"][:, s:s + 1], 0.0, ALU.is_le,
                                              ALU.add, accum_out=tile_f[:, q, s:s + 1]))
            for q in range(2):
                ch.link(dve.tensor_tensor(chunk_f[:, q, :], g["step_index"][:, :], tile_f[:, q, :], ALU.subtract))
            ch.link(dve.tensor_scalar_min(chunk_f[:, :, :], chunk_f[:, :, :], float(COLS - 1)))
            dve.tensor_copy(chunk_u[:, :], chunk_f[:, :, :].rearrange("p q s -> p (q s)")).then_inc(chunk_ready, 1)
            dve.wait_ge(tiles_turned, 1)
            ch.link(dve.tensor_copy(tiles_along[:, :, :].rearrange("q j w -> q (j w)"), ps[4][0:n2, 0:P]))
            ch.link(dve.scalar_tensor_tensor(out=packed[:, :], in0=tiles_along[:, :, 3], scalar=64.0, in1=tiles_along[:, :, 2], op0=ALU.mult, op1=ALU.add))
            ch.link(dve.scalar_tensor_tensor(out=packed[:, :], in0=packed[:, :], scalar=64.0, in1=tiles_along[:, :, 1], op0=ALU.mult, op1=ALU.add))
            ch.link(dve.scalar_tensor_tensor(out=packed[:, :], in0=packed[:, :], scalar=64.0, in1=tiles_along[:, :, 0], op0=ALU.mult, op1=ALU.add))
            dve.tensor_copy(packed_i[:, :], packed[:, :]).then_inc(chunk_ready, 1)
            ch.link(dve.tensor_scalar(tile_key[:, :, :], tile_f[:, :, :], float(P), None, ALU.mult))
            for k in range(n2):
                q, s = k // GROUPS, k % GROUPS
                dve.wait_ge(rows_at[k % 4], 16 * (k // 4 + 1))
                if k >= 2:
                    dve.wait_ge(turned, k - 1)
                dve.tensor_scalar(rows_f[:, k % 2, 0, :], rows[:, k % 4, :, 0], tile_key[:, q, s:s + 1], None,
                                  ALU.subtract).then_inc(rows_made, 1)
                dve.tensor_copy(rows_f[:, k % 2, 1, :], rows[:, k % 4, :, 1]).then_inc(rows_made, 1)
                if q == 1:
                    dve.tensor_copy(ends[:, s, :], rows[:, k % 4, 0:P:P - 1, 0]).then_inc(ends_made, 1)
                    dve.wait_ge(ends_made, s + 2)
                dve.wait_ge(rows_made, 2 * k + 2)
                dve.sem_inc(rows_used, 1)
                if q == 1:
                    here, before_ = rows_f[:, k % 2, 0, 1:P], rows_f[:, k % 2, 0, 0:P - 1]
                    dve.tensor_tensor(cuts[:, s, 0, 1:P], here, before_, ALU.not_equal).then_inc(cuts_made, 1)
                    dve.tensor_tensor(cuts[:, s, 1, 0:P - 1], here, before_, ALU.not_equal).then_inc(cuts_made, 1)
                dve.wait_ge(turned, k + 1)
                dve.tensor_copy(local_key[q][:, s * P:(s + 1) * P], ps[2 * (k % 2)][:, 0:P])
                dve.tensor_copy(row_of[q][:, s * P:(s + 1) * P], ps[2 * (k % 2) + 1][:, 0:P]).then_inc(taken, 1)
            ch.wait()
            dve.wait_ge(beside_in, 32)
            dve.tensor_tensor(cuts[:, :, 0, 0], ends[:, :, 0], beside[:, :, 0], ALU.not_equal).then_inc(cuts_made, 1)
            dve.tensor_tensor(cuts[:, :, 1, P - 1], ends[:, :, 1], beside[:, :, 1], ALU.not_equal).then_inc(cuts_made, 1)
            dve.wait_ge(cuts_made, 2 * GROUPS + 2)
            dve.tensor_scalar(cuts[:, :, :, :], cuts[:, :, :, :], -FAR, None, ALU.mult).then_inc(cuts_ready, 1)

        @block.tensor
        def _(pe):
            pe.wait_ge(chunk_ready, 1)
            pe.transpose(ps[4][0:n2, 0:P], tile_f[:, :, :].rearrange("p q s -> p (q s)"), ident[:, :]).then_inc(tiles_turned, 1)
            for k in range(n2):
                pe.wait_ge(rows_made, 2 * k + 2)
                if k >= 2:
                    pe.wait_ge(taken, k - 1)
                pe.transpose(ps[2 * (k % 2)][:, 0:P], rows_f[:, k % 2, 0, :], ident[:, :])
                pe.transpose(ps[2 * (k % 2) + 1][:, 0:P], rows_f[:, k % 2, 1, :], ident[:, :]).then_inc(turned, 1)

        @block.sync
        def _(sp):
            sp.wait_ge(chunk_ready, 2)
            sp.dma_start(g["four_tiles_dram"][:, :].rearrange("q (s p) -> (q s) p", p=P // 4), packed_i[:, :]).then_inc(tiles_out, 16)
            sp.wait_ge(tiles_out, 16)
            sp.dma_start(g["four_tiles"][:, :], g["four_tiles_dram"][0:1, :]).then_inc(tiles_in, 16)
            sp.wait_ge(taken, n2)
            sp.dma_start(g["key_by_dst"][:, :], local_key[1][:, :]).then_inc(tiles_in, 16)
            sp.dma_start(g["row_by_dst"][:, :], row_of[1][:, :]).then_inc(tiles_in, 16)
            sp.wait_ge(ends_made, GROUPS + 1)
            for a in range(2):
                sp.dma_start(g["ends_dram"][a:a + 1, 1:SG + 1].rearrange("a (s p) -> p (a s)", p=P), ends[:, :, a], allow_slow_non_contiguous=True).then_inc(ends_out, 16)
                sp.dma_start(g["ends_dram"][1 - a:2 - a, a * (SG + 1):a * (SG + 1) + 1], outside[:, a:a + 1]).then_inc(ends_out, 16)
            sp.wait_ge(ends_out, 64)
            for a in range(2):
                sp.dma_start(beside[:, :, a], g["ends_dram"][1 - a:2 - a, 2 * a:2 * a + SG].rearrange("a (s p) -> p (a s)", p=P), allow_slow_non_contiguous=True).then_inc(beside_in, 16)
            sp.wait_ge(cuts_ready, 1)
            for a in range(2):
                sp.dma_start(g["cuts_dram"][a:a + 1, :].rearrange("a (s p e) -> p (a s) e", p=P, e=P), cuts[:, :, a, :]).then_inc(tiles_in, 16)
            sp.wait_ge(tiles_in, 80)


def row_norm(g, c, name):
    nc, sb, sem, X = g["nc"], g["sb"], g["sem"], g["X"]
    stats = sb(name + "_stats", [P, NT, 6], F32, c)
    mean = sb(name + "_mean", [P, NT], F32, c)
    var = sb(name + "_var", [P, NT], F32, c)
    apart = sb(name + "_apart", [P, NT], F32, c)
    rstd = sb(name + "_rstd", [P, NT], F32, c)
    own, var_ready, std_ready = (sem(name + n) for n in ("_own", "_var_ready", "_std_ready"))

    def vector(dve):
        ch = Chain(dve, own)
        with dve.Fori(0, NT // 2) as i:
            for u in range(2):
                t = i * 2 + u
                dve.bn_stats(row(stats, t), row(X, t)).then_inc(own, 1)
        ch.enter(NT)
        ch.wait()
        ch.step(dve.tensor_tensor(mean[:, :], stats[:, :, 1], stats[:, :, 4], ALU.add))
        ch.step(dve.tensor_tensor(apart[:, :], stats[:, :, 1], stats[:, :, 4], ALU.subtract))
        ch.link(dve.tensor_tensor(var[:, :], stats[:, :, 2], stats[:, :, 5], ALU.add))
        ch.link(dve.tensor_scalar(mean[:, :], mean[:, :], 0.5, None, ALU.mult))
        ch.link(dve.tensor_tensor(apart[:, :], apart[:, :], apart[:, :], ALU.mult))
        ch.link(dve.tensor_scalar(apart[:, :], apart[:, :], 0.25, None, ALU.mult))
        dve.scalar_tensor_tensor(out=var[:, :], in0=var[:, :], scalar=1.0 / D, in1=apart[:, :], op0=ALU.mult, op1=ALU.add).then_inc(var_ready, 1)
        dve.wait_ge(std_ready, 1)
        ch.link(dve.reciprocal(rstd[:, :], rstd[:, :]))

    def scalar(act):
        act.wait_ge(var_ready, 1)
        act.activation(rstd[:, :], var[:, :], ACT.Sqrt, bias=g["eps_ln"][:, 0:1]).then_inc(std_ready, 1)

    return mean, rstd, vector, scalar


def rounds_of(eng, count):
    yield 0
    with eng.Fori(1, count) as i:
        yield i


def wait_from(eng, sem, value):
    if not isinstance(value, int) or value > 0:
        eng.wait_ge(sem, value)


def wait_apart(eng, sem, value, passed):
    if isinstance(value, int) and value <= 0:
        return
    eng.wait_ge(sem, value)
    eng.sem_inc(passed, 1)


def tiles_of_four(eng, four_tiles, j):
    word = eng.value_load(four_tiles[0:1, ds(j, 1)])
    return [((word >> (6 * k)) & 63).with_bounds(min_val=0, max_val=NT - 1) for k in range(4)]


def flat_row(eng, a, t):
    width = a.shape[2]
    at = eng.snap(eng.to_reg(t * width), min_val=0, max_val=(NT - 1) * width)
    return a[:, :, :].rearrange("p t d -> p (t d)")[:, ds(at, width)]


def row(a, t):
    return a[:, ds(t, 1), :].rearrange("p a d -> p (a d)")


def mixture(g, c, layer, part):
    nc, sb, sem, ps, X, Z, mix = (g[n] for n in ("nc", "sb", "sem", "ps", "X", "Z", "mix"))
    ident = g["ident"]
    own_part = part == "own"
    pre = f"{part}{layer}_"
    W0 = sb(pre + "W", [P, 2, K0, D], F32, c)
    stage = sb(pre + "stage", [P, 4, D], F32, c)
    zT = sb(pre + "zT", [P, 2, 2, P], F32, c)
    names = ("ready", "dve_now", "staged", "turned", "zt_ready", "logits_ready", "products", "exp_in", "exp_out",
             "mixed", "w_loaded")
    ready, dve_now, staged, turned, zt_ready, logits_ready, products, exp_in, exp_out, mixed, w_loaded = (
        sem(pre + n) for n in names)
    stored = [sem(pre + f"stored{u}") for u in range(4)]
    store_stage = own_part and layer == 0
    store_new = not own_part and layer == 0
    if own_part:
        envw = sb(pre + "envw", [P, 2, K0], F32, c)
        envb = sb(pre + "envb", [P, K0], F32, c)
        lg = sb(pre + "lg", [P, 2, K0], F32, c)
        ex = sb(pre + "ex", [P, 2, K0], F32, c)
        col = sb(pre + "col", [P, 2, 3], F32, c)
    if store_stage:
        mean, rstd, norm_vector, norm_scalar = row_norm(g, c, "ln0")
        shift = sb(pre + "shift", [P, NT], F32, c)
    if not own_part:
        per_count = sb(pre + "per_count", [P, NT], F32, c)
    first_chunk = 2 if own_part else 0
    MIXED_AHEAD = 2
    now_links = K0 + (2 if own_part else 0)

    def sync(sp):
        for k in range(K0):
            sp.dma_start(W0[:, :, k, :], g["L0_gnn_W"][layer, k].rearrange("(c p) d -> p c d", p=P)[:, first_chunk:first_chunk + 2, :]).then_inc(w_loaded, 16)
        if own_part:
            sp.dma_start(envw[:, :, :], g["L0_gnn_envW"][layer].rearrange("(c p) k -> p c k", p=P)).then_inc(w_loaded, 16)
            sp.dma_start(envb[:, :], g["L0_gnn_envb"][layer:layer + 1, :].broadcast_to([P, K0])).then_inc(w_loaded, 16)

        def store(t, slot, lap):
            if store_stage:
                wait_from(sp, staged, t + 1)
                sp.dma_start(g["z_rows"][0][ds(t * P, P), :], stage[:, slot, :]).then_inc(stored[slot], 16)
            else:
                wait_from(sp, mixed, t + 1 + MIXED_AHEAD)
                sp.dma_start(g["z_rows"][1][ds(t * P, P), :], row(Z, t)).then_inc(stored[slot], 16)

        if store_stage or store_new:
            laps(sp, store, NT)
            for slot in range(4):
                sp.wait_ge(stored[slot], 16 * ((NT - slot + 3) // 4))

    def vector(dve):
        chn = Chain(dve, dve_now)
        once = Chain(dve, ready)
        if store_stage:
            norm_vector(dve)
            once.link(dve.scalar_tensor_tensor(out=shift[:, :], in0=mean[:, :], scalar=-1.0, in1=rstd[:, :], op0=ALU.mult, op1=ALU.mult))
        if not own_part:
            once.link(dve.tensor_scalar_max(per_count[:, :], g["A"][:, :, D], 1.0))
            once.link(dve.reciprocal(per_count[:, :], per_count[:, :]))
        if own_part:
            dve.wait_ge(w_loaded, 16 * (K0 + 2))
        dve.sem_inc(mixed, MIXED_AHEAD)

        def mix_products(t, slot, lap):
            z, u = row(Z, t), slot % 2
            chn.enter(t * now_links)
            if own_part:
                wait_from(dve, logits_ready, t + 1)
                wait_from(dve, exp_out, t)
                chn.link(dve.tensor_tensor(lg[:, u, :], ps[6 + u][:, 0:K0], envb[:, :], ALU.add))
                dve.tensor_reduce(col[:, u, 0:1], lg[:, u, :], AX.X, ALU.max, negate=True).then_inc(exp_in, 1)
                wait_from(dve, exp_out, t + 1)
                chn.link(dve.reciprocal(col[:, u, 2:3], col[:, u, 1:2]))
                chn.link(dve.tensor_scalar(row(mix, t), ex[:, u, :], col[:, u, 2:3], None, ALU.mult))
            wait_from(dve, products, t + 1)
            for k in range(K0):
                z_in = stage[:, slot, :] if store_stage and k == 0 else z
                ins = dve.scalar_tensor_tensor(out=z, in0=ps[2 * u + k // 2][:, (k % 2) * D:(k % 2 + 1) * D],
                                               scalar=mix[:, ds(t, 1), k:k + 1].rearrange("p a k -> p (a k)"), in1=z_in,
                                               op0=ALU.mult, op1=ALU.add)
                if k == K0 - 1 and own_part:
                    ins.then_inc(mixed, 1)
                else:
                    chn.link(ins)
            if store_new:
                dve.tensor_scalar_max(z, z, 0.0).then_inc(mixed, 1)
            elif not own_part:
                dve.scalar_tensor_tensor(out=row(X, t), in0=z, scalar=0.0, in1=row(X, t), op0=ALU.max, op1=ALU.add).then_inc(mixed, 1)

        laps(dve, mix_products, NT)

    def scalar(act):
        if store_stage:
            norm_scalar(act)
        if not own_part or store_stage:
            act.wait_ge(ready, 1 if store_stage else 2)

        def put_stage(t, slot, lap):
            wait_from(act, mixed, t - 3 + MIXED_AHEAD)
            if store_stage:
                wait_from(act, stored[slot], lap * 16)
                act.activation(stage[:, slot, :], row(X, t), ACT.Identity, bias=shift[:, ds(t, 1)], scale=rstd[:, ds(t, 1)]).then_inc(staged, 1)
            elif own_part:
                act.copy(stage[:, slot, :], row(Z, t)).then_inc(staged, 1)
            else:
                act.activation(stage[:, slot, :], g["A"][:, ds(t, 1), 0:D].rearrange("p a d -> p (a d)"), ACT.Copy,
                               scale=per_count[:, ds(t, 1)]).then_inc(staged, 1)

        def copy_turned(t, slot, lap):
            u = slot % 2
            wait_from(act, turned, t + 1)
            wait_from(act, products, t - 1)
            act.copy(zT[:, u, :, :].rearrange("p k n -> p (k n)"), ps[4 + u][:, 0:2 * P]).then_inc(zt_ready, 1)

        def softmax(t, slot, lap):
            u = slot % 2
            if own_part:
                wait_from(act, exp_in, t + 1)
                act.activation(ex[:, u, :], lg[:, u, :], ACT.Exp, bias=col[:, u, 0:1], accum_out=col[:, u, 1:2]).then_inc(exp_out, 1)

        def step(t, slot, lap):
            if not isinstance(t, int) or t + 1 < NT:
                copy_turned(t + 1, (slot + 1) % 4, lap + (slot + 1) // 4)
            if not isinstance(t, int) or t + 2 < NT:
                put_stage(t + 2, (slot + 2) % 4, lap + (slot + 2) // 4)
            softmax(t, slot, lap)

        put_stage(0, 0, 0)
        put_stage(1, 1, 0)
        copy_turned(0, 0, 0)
        laps(act, step, NT)

    def tensor(pe):
        pe.wait_ge(w_loaded, 16 * (K0 + 2 * own_part))

        def turn(t, slot):
            u = slot % 2
            wait_from(pe, staged, t + 1)
            wait_from(pe, zt_ready, t - 1)
            for k in range(2):
                mm = pe.transpose(ps[4 + u][:, k * P:(k + 1) * P], stage[:, slot, k * P:(k + 1) * P], ident[:, :])
            mm.then_inc(turned, 1)

        def multiply(t, slot, lap):
            u = slot % 2
            if not isinstance(t, int) or t + 1 < NT:
                turn(t + 1, (slot + 1) % 4)
            wait_from(pe, zt_ready, t + 1)
            wait_from(pe, mixed, t - 1 + MIXED_AHEAD)
            if own_part:
                for k in range(2):
                    mm = pe.matmul(ps[6 + u][:, 0:K0], zT[:, u, k, :], envw[:, k, :], start=(k == 0), stop=(k == 1))
                mm.then_inc(logits_ready, 1)
            for h in range(2):
                for k in range(2):
                    mm = pe.matmul(ps[2 * u + h][:, :], zT[:, u, k, :],
                                   W0[:, k, 2 * h:2 * h + 2, :].rearrange("p k d -> p (k d)"),
                                   start=(k == 0), stop=(k == 1))
            mm.then_inc(products, 1)

        turn(0, 0)
        laps(pe, multiply, NT)

    return {"sync": sync, "vector": vector, "scalar": scalar, "tensor": tensor}


def run_block(nc, programs):
    with nc.Block() as block:
        if "sync" in programs:
            @block.sync
            def _(sp):
                programs["sync"](sp)

        if "vector" in programs:
            @block.vector
            def _(dve):
                programs["vector"](dve)

        if "scalar" in programs:
            @block.scalar
            def _(act):
                programs["scalar"](act)

        if "tensor" in programs:
            @block.tensor
            def _(pe):
                programs["tensor"](pe)

        if "gpsimd" in programs:
            @block.gpsimd
            def _(pool):
                programs["gpsimd"](pool)


def gather_sum(g, c, layer):
    nc, sb, sem, ps, A = g["nc"], g["sb"], g["sem"], g["ps"], g["A"]
    pre = f"sum{layer}_"
    ring_rows = sb(pre + "rows", [P, 2 * HALF, D + 1], F32, c)
    ring_index = sb(pre + "index", [P, 2, HALF], U32, c)
    place = sb(pre + "place", [P, 2, HALF, P], F32, c)
    indexed, placed, summed, cleared, dve_own = (
        sem(pre + n) for n in ("indexed", "placed", "summed", "cleared", "dve_own"))
    fetched = [sem(pre + f"fetched{h}") for h in range(2)]
    rounds = STEPS // (2 * HALF)
    pool_passed = sem(pre + "pool_passed")

    def gpsimd(pool):
        pool.wait_ge(cleared, 1)
        for i in rounds_of(pool, rounds):
            for h in range(2):
                wait_apart(pool, fetched[h], i * (16 * HALF), pool_passed)
                pool.tensor_copy(ring_index[:, h, :], g["row_of"][:, ds((i * 2 + h) * HALF, HALF)]).then_inc(indexed, 1)
                wait_apart(pool, indexed, i * 2 + h + 1, pool_passed)
                for k in range(HALF):
                    wait_apart(pool, summed, (i * 2 + h) * HALF + k + 1, pool_passed)
                    pool.indirect_dma_start(
                        out=ring_rows[:, h * HALF + k, 0:D], out_offset=None, in_=g["z_rows"][layer][:, :],
                        in_offset=bass.IndirectOffsetOnAxis(ap=ring_index[:, h, k:k + 1], axis=0)).then_inc(fetched[h], 16)

    def vector(dve):
        ch = Chain(dve, dve_own)
        dve.memset(ring_rows[:, :, D:D + 1], 1.0)
        dve.memset(A[:, :, :], 0.0).then_inc(cleared, 1)
        dve.wait_ge(cleared, 1)

        def places(half, h):
            wait_from(dve, summed, half * HALF + HALF)
            key = g["local_key"][:, ds(half * HALF, HALF)]
            dve.tensor_tensor(place[:, h, :, :], g["iota_row"][:, :].unsqueeze(1).broadcast_to([P, HALF, P]),
                              key.unsqueeze(2).broadcast_to([P, HALF, P]), ALU.is_equal).then_inc(placed, 1)

        dve.sem_inc(dve_own, HALF)
        places(0, 0)
        for i in rounds_of(dve, rounds):
            for h in range(2):
                places(i * 2 + h + 1, 1 - h)
                ch.enter((i * 2 + h) * HALF + HALF)
                for k in range(HALF):
                    s = (i * 2 + h) * HALF + k
                    if k % 4 == 0:
                        tiles = tiles_of_four(dve, g["four_tiles"], (i * 2 + h) * 2 + k // 4)
                    here = flat_row(dve, A, tiles[k % 4])
                    wait_from(dve, summed, s + 1 + 2 * HALF)
                    ch.wait()
                    ch.step(dve.tensor_tensor(here, ps[k][:, 0:D + 1], here, ALU.add))

    def tensor(pe):
        pe.sem_inc(summed, 2 * HALF)
        for i in rounds_of(pe, rounds):
            for h in range(2):
                wait_from(pe, fetched[h], (i + 1) * (16 * HALF))
                wait_from(pe, placed, i * 2 + h + 1)
                for k in range(HALF):
                    s = (i * 2 + h) * HALF + k
                    wait_from(pe, dve_own, s + 1)
                    pe.matmul(ps[k][:, 0:D + 1], place[:, h, k, :], ring_rows[:, h * HALF + k, :],
                              start=True, stop=True).then_inc(summed, 1)

    return {"gpsimd": gpsimd, "vector": vector, "tensor": tensor}


NH, DH, NG = 8, 64, 64
INNER = NH * DH
PAIRS = NH // 2


def four_slots(eng, body):
    for t in range(4):
        body(t, t)
    with eng.Fori(1, NT // 4 - 1) as i:
        for v in range(4):
            body(i * 4 + v, v)
    for t in range(4 * (NT // 4 - 1), NT):
        body(t, t % 4)


def slice_attention(g, c):
    nc, sb, sem, ps, X, ident, ones = (g[n] for n in ("nc", "sb", "sem", "ps", "X", "ident", "ones"))
    logit_w = sb("logit_w", [P, 2, INNER], F32, c)
    logit_b = sb("logit_b", [P, INNER], F32, c)
    slices = sb("slices", [P, PAIRS, D + 1], F32, c)
    back = sb("back", [P, PAIRS, D], F32, c)
    b_out = sb("b_out", [P, D], F32, c)
    wT = sb("wT", [P, PAIRS, (LASTT + 1) * P], F32, c)

    mean, rstd, norm_vector, norm_scalar = row_norm(g, c, "ln1")

    with ExitStack() as c2:
        wx = sb("wx", [P, 2, INNER], F32, c2)
        wxT = sb("wxT", [DH, 2, NH, P], F32, c2)
        ws = sb("ws", [DH, NG], F32, c2)
        bx = sb("bx", [DH, NH], F32, c2)
        bxb = sb("bxb", [DH, NH, P], F32, c2)
        bs = sb("bs", [P, NG], F32, c2)
        tb = sb("tb", [P, NH], F32, c2)
        loaded, turned, copied, multiplied, widened, own = (
            sem("slw_" + n) for n in ("loaded", "turned", "copied", "multiplied", "widened", "own"))
        with nc.Block() as block:
            @block.sync
            def _(sp):
                sp.dma_start(wx[:, :, :], g["L0_ffn_W_x"].rearrange("(c p) n -> p c n", p=P)).then_inc(loaded, 16)
                sp.dma_start(ws[:, :], g["L0_ffn_W_slice"]).then_inc(loaded, 16)
                with nc.allow_non_contiguous_dma(reason="512 numbers"):
                    sp.dma_start(bx[:, :], g["L0_ffn_b_x"].rearrange("(h d) -> d h", h=NH)).then_inc(loaded, 16)
                sp.dma_start(bs[:, :], g["L0_ffn_b_slice"].rearrange("(a n) -> a n", a=1).broadcast_to([P, NG])).then_inc(loaded, 16)
                sp.dma_start(tb[:, :], g["L0_ffn_temperature"].rearrange("a h b c -> a (h b c)").broadcast_to([P, NH])).then_inc(loaded, 16)
                sp.dma_start(b_out[:, :], g["L0_ffn_b_out"].rearrange("(a n) -> a n", a=1).broadcast_to([P, D])).then_inc(loaded, 16)
                sp.wait_ge(loaded, 96)

            @block.tensor
            def _(pe):
                pe.wait_ge(loaded, 96)
                for k in range(2):
                    for h in range(NH):
                        mm = pe.transpose(ps[2 * k + h // 4][0:DH, (h % 4) * P:(h % 4 + 1) * P], wx[:, k, h * DH:(h + 1) * DH], ident[:, :])
                mm.then_inc(turned, 1)
                pe.wait_ge(copied, 4)
                for k in range(2):
                    for h in range(NH):
                        pe.matmul(ps[4 + k][:, h * NG:(h + 1) * NG], wxT[:, k, h, :], ws[:, :], start=True, stop=True)
                pe.wait_ge(widened, 1)
                for h in range(NH):
                    mm = pe.matmul(ps[6][:, h * NG:(h + 1) * NG], bxb[:, h, :], ws[:, :], start=True, stop=True)
                mm.then_inc(multiplied, 1)

            @block.vector
            def _(dve):
                ch = Chain(dve, own)
                dve.wait_ge(loaded, 96)
                dve.tensor_copy(bxb[:, :, :], bx[:, :].unsqueeze(2).broadcast_to([DH, NH, P])).then_inc(widened, 1)
                ch.link(dve.tensor_scalar(tb[:, :], tb[:, :], 0.1, 5.0, ALU.max, ALU.min))
                ch.link(dve.reciprocal(tb[:, :], tb[:, :]))
                dve.wait_ge(turned, 1)
                for k in range(4):
                    dve.tensor_copy(wxT[:, k // 2, (k % 2) * 4:(k % 2) * 4 + 4, :].rearrange("d h p -> d (h p)"), ps[k][0:DH, :]).then_inc(copied, 1)
                dve.wait_ge(multiplied, 1)
                per_head = tb[:, :].unsqueeze(2).broadcast_to([P, NH, NG])
                for k in range(2):
                    dve.tensor_tensor(logit_w[:, k, :].rearrange("p (h g) -> p h g", h=NH),
                                      ps[4 + k][:, :].rearrange("p (h g) -> p h g", h=NH), per_head, ALU.mult)
                bias = logit_b[:, :].rearrange("p (h g) -> p h g", h=NH)
                ch.link(dve.tensor_tensor(bias, ps[6][:, :].rearrange("p (h g) -> p h g", h=NH),
                                          bs[:, :].unsqueeze(1).broadcast_to([P, NH, NG]), ALU.add))
                ch.link(dve.tensor_tensor(bias, bias, per_head, ALU.mult))
                norm_vector(dve)

            @block.scalar
            def _(act):
                norm_scalar(act)

    with ExitStack() as c2:
        stage = sb("sl_stage", [P, 4, D + 1], F32, c2)
        zT = sb("sl_zT", [P, 2, 2, P], F32, c2)
        lg = sb("sl_lg", [P, 2, INNER], F32, c2)
        w = sb("sl_w", [P, 2, INNER], F32, c2)
        top = sb("sl_top", [P, 2, NH], F32, c2)
        tot = sb("sl_tot", [P, 2, NH], F32, c2)
        zero = sb("sl_zero", [P, D + 1], F32, c2)
        staged, turned, zt_ready, logits, exp_in, exp_out, weights, summed, wt_done, wt_taken, own, totals, stage_own = (
            sem("sl_" + n) for n in ("staged", "turned", "zt_ready", "logits", "exp_in", "exp_out", "weights", "summed",
                                     "wt_done", "wt_taken", "own", "totals", "stage_own"))
        last = LASTT

        def vector(dve):
            dve.memset(zero[:, :], 0.0).then_inc(stage_own, 1)
            dve.memset(stage[:, :, D:D + 1], 1.0).then_inc(stage_own, 1)

            def stage_of(t, slot):
                wait_from(dve, summed, t - 3)
                dve.tensor_scalar(stage[:, slot, 0:D], row(X, t), mean[:, ds(t, 1)], rstd[:, ds(t, 1)], ALU.subtract,
                                  ALU.mult).then_inc(staged, 1)

            def exponents(t, u):
                ch = Chain(dve, own, t * 2)
                heads = lg[:, u, :].rearrange("p (h g) -> p h g", h=NH)
                wait_from(dve, logits, t + 1)
                ch.link(dve.tensor_tensor(lg[:, u, :], ps[u][:, :], logit_b[:, :], ALU.add))
                ch.link(dve.tensor_reduce(top[:, u, :], heads, AX.X, ALU.max))
                dve.tensor_tensor(heads, heads, top[:, u, :].unsqueeze(2).broadcast_to([P, NH, NG]), ALU.subtract).then_inc(exp_in, 1)

            def divide(t, u):
                ch = Chain(dve, totals, t)
                heads = lg[:, u, :].rearrange("p (h g) -> p h g", h=NH)
                wait_from(dve, exp_out, t + 1)
                ch.link(dve.tensor_reduce(tot[:, u, :], heads, AX.X, ALU.add))
                dve.reciprocal(tot[:, u, :], tot[:, u, :]).then_inc(stage_own, 1)
                wait_from(dve, stage_own, t + 3)
                wait_from(dve, summed, t - 1)
                dve.tensor_tensor(w[:, u, :].rearrange("p (h g) -> p h g", h=NH), heads,
                                  tot[:, u, :].unsqueeze(2).broadcast_to([P, NH, NG]), ALU.mult).then_inc(weights, 1)

            def body(t, slot):
                number = isinstance(t, int)
                if not number or t < last:
                    stage_of(t + 1, (slot + 1) % 4)
                if not number or t <= last:
                    if not number or t > 1:
                        wait_from(dve, weights, t - 1)
                    exponents(t, slot % 2)
                if not number or t > 0:
                    divide(t - 1, (slot - 1) % 2)

            stage_of(0, 0)
            four_slots(dve, body)

        def scalar(act):
            def take(t):
                wait_from(act, wt_done, t + 1)
                act.copy(wT[:, :, ds(t * P, P)], ps[6][:, :].rearrange("p (j n) -> p j n", j=PAIRS)).then_inc(wt_taken, 1)

            def zt(t, u):
                wait_from(act, turned, t + 1)
                act.copy(zT[:, u, :, :].rearrange("p k n -> p (k n)"), ps[7][:, 0:2 * P]).then_inc(zt_ready, 1)

            def body(t, slot):
                number = isinstance(t, int)
                if number and t > last:
                    take(last - 1)
                    return take(last)
                wait_from(act, exp_in, t + 1)
                act.activation(lg[:, slot % 2, :], lg[:, slot % 2, :], ACT.Exp).then_inc(exp_out, 1)
                if not number or t < last:
                    zt(t + 1, (slot + 1) % 2)
                if not number or t > 1:
                    take(t - 2)

            zt(0, 0)
            four_slots(act, body)

        def tensor(pe):
            pe.wait_ge(stage_own, 2)

            def turn(t, slot):
                wait_from(pe, staged, t + 1)
                wait_from(pe, zt_ready, t)
                for k in range(2):
                    mm = pe.transpose(ps[7][:, k * P:(k + 1) * P], stage[:, slot, k * P:(k + 1) * P], ident[:, :])
                mm.then_inc(turned, 1)

            def sums(t, slot):
                rows = NREST if isinstance(t, int) and t == last else P
                wait_from(pe, weights, t + 1)
                wait_from(pe, wt_taken, t)
                for j in range(PAIRS):
                    mm = pe.transpose(ps[6][:, j * P:(j + 1) * P], w[:, slot % 2, j * P:(j + 1) * P], ident[:, :])
                mm.then_inc(wt_done, 1)
                for j in range(PAIRS):
                    mm = pe.matmul(ps[2 + j][:, 0:D + 1], w[0:rows, slot % 2, j * P:(j + 1) * P], stage[0:rows, slot, :],
                                   start=False, stop=rows < P, skip_group_check=True)
                mm.then_inc(summed, 1)

            def body(t, slot):
                number = isinstance(t, int)
                if number and t > last:
                    sums(last - 1, (last - 1) % 4)
                    return sums(last, last % 4)
                wait_from(pe, zt_ready, t + 1)
                wait_from(pe, exp_in, t - 1)
                for k in range(2):
                    mm = pe.matmul(ps[slot % 2][:, :], zT[:, slot % 2, k, :], logit_w[:, k, :], start=(k == 0), stop=(k == 1))
                mm.then_inc(logits, 1)
                if not number or t < last:
                    turn(t + 1, (slot + 1) % 4)
                if not number or t > 1:
                    sums(t - 2, (slot - 2) % 4)

            for j in range(PAIRS):
                pe.matmul(ps[2 + j][:, 0:D + 1], zero[:, 0:P], zero[:, :], start=True, stop=False, skip_group_check=True)
            turn(0, 0)
            four_slots(pe, body)

        run_block(nc, {"vector": vector, "scalar": scalar, "tensor": tensor})

    with ExitStack() as c2:
        names = ("turned", "copied", "tokens", "norms", "tok_ready", "tok_turned", "tokT_ready", "qkv", "qkv_ready", "scored",
                 "exp_in", "exp_out", "attn", "attn_turned", "attnT_ready", "mixed", "mixed_ready", "backed", "back_ready",
                 "loaded", "moved", "own")
        s = {n: sem("sa_" + n) for n in names}
        yT = sb("sa_yT", [P, 2, INNER], F32, c2)
        norm_row = sb("sa_norm_row", [1, INNER], F32, c2)
        bfx = sb("sa_bfx", [1, INNER], F32, c2)
        wfx = sb("sa_wfx", [P, 2, INNER], F32, c2)
        wq, wk, wv = (sb(n, [DH, DH], F32, c2) for n in ("sa_wq", "sa_wk", "sa_wv"))
        wo = sb("sa_wo", [DH, NH, D], F32, c2)
        den = sb("sa_den", [NG, NH], F32, c2)
        tok, tokT, qT, kT, v, at, atT, mixT = (sb("sa_" + n, [DH, INNER], F32, c2)
                                               for n in ("tok", "tokT", "qT", "kT", "v", "at", "atT", "mixT"))
        peak = sb("sa_peak", [NG, NH], F32, c2)
        odd = slices[0:NG, :, 0:D]
        scale = float(DH) ** -0.5

        def h_(a, h):
            return a[:, h * DH:(h + 1) * DH]

        def by_head(a):
            return a.rearrange("p (h g) -> p h g", h=NH)

        def sync(sp):
            for dst, src in ((wfx[:, :, :], g["L0_ffn_W_fx"].rearrange("(c p) n -> p c n", p=P)), (wq[:, :], g["L0_ffn_W_q"]),
                             (wk[:, :], g["L0_ffn_W_k"]), (wv[:, :], g["L0_ffn_W_v"]),
                             (wo[:, :, :], g["L0_ffn_W_out"].rearrange("(h d) n -> d h n", d=DH)),
                             (bfx[:, :], g["L0_ffn_b_fx"].rearrange("(a n) -> a n", a=1))):
                sp.dma_start(dst, src).then_inc(s["loaded"], 16)
            sp.wait_ge(s["back_ready"], 1)
            sp.dma_start(back[NG:P, :, :], odd).then_inc(s["moved"], 16)
            sp.wait_ge(s["moved"], 16)

        def tensor(pe):
            pe.wait_ge(s["copied"], 1)
            for j in range(PAIRS):
                for k in range(2):
                    pe.transpose(ps[k][:, j * P:(j + 1) * P], slices[:, j, k * P:(k + 1) * P], ident[:, :])
                mm = pe.transpose(ps[6][0:1, j * P:(j + 1) * P], slices[:, j, D:D + 1], ident[:, :])
            mm.then_inc(s["turned"], 1)
            pe.wait_ge(s["copied"], 4)
            pe.wait_ge(s["loaded"], 96)
            for h in range(NH):
                for k in range(2):
                    pe.matmul(h_(ps[3][0:NG, :], h), h_(yT[:, k, :], h), h_(wfx[:, k, :], h), start=(k == 0), stop=False)
                pe.matmul(h_(ps[3][0:NG, :], h), h_(norm_row, h), h_(bfx, h), start=False, stop=True)
            for h in range(NH):
                mm = pe.matmul(ps[4][0:NG, h:h + 1], h_(norm_row, h), ones[0:1, 0:1], start=True, stop=True)
            mm.then_inc(s["tokens"], 1)
            pe.wait_ge(s["tok_ready"], 1)
            for h in range(NH):
                mm = pe.transpose(h_(ps[5][0:DH, :], h), h_(tok, h), ident[0:DH, 0:DH])
            mm.then_inc(s["tok_turned"], 1)
            pe.wait_ge(s["tokT_ready"], 1)
            pe.matmul(ps[0][0:DH, :], wq[:, :], tokT[:, :], start=True, stop=True)
            pe.matmul(ps[1][0:DH, :], wk[:, :], tokT[:, :], start=True, stop=True)
            for h in range(NH):
                mm = pe.matmul(h_(ps[2][0:NG, :], h), h_(tokT, h), wv[:, :], start=True, stop=True)
            mm.then_inc(s["qkv"], 1)
            pe.wait_ge(s["qkv_ready"], 3)
            for h in range(NH):
                mm = pe.matmul(h_(ps[3][0:NG, :], h), h_(qT, h), h_(kT, h), start=True, stop=True)
            mm.then_inc(s["scored"], 1)
            pe.wait_ge(s["attn"], 1)
            for h in range(NH):
                mm = pe.transpose(h_(ps[4][0:NG, :], h), h_(at, h), ident[0:NG, 0:NG])
            mm.then_inc(s["attn_turned"], 1)
            pe.wait_ge(s["attnT_ready"], 1)
            for h in range(NH):
                mm = pe.matmul(h_(ps[5][0:DH, :], h), h_(v, h), h_(atT, h), start=True, stop=True)
            mm.then_inc(s["mixed"], 1)
            pe.wait_ge(s["mixed_ready"], 1)
            for h in range(NH):
                mm = pe.matmul(ps[h % 2 * 2 + h // 4][0:NG, (h // 2 % 2) * D:(h // 2 % 2 + 1) * D], h_(mixT, h), wo[:, h, :], start=True, stop=True)
            mm.then_inc(s["backed"], 1)

        def vector(dve):
            ch = Chain(dve, s["own"])
            for j in range(PAIRS):
                ins = dve.tensor_copy(slices[:, j, :], ps[2 + j][:, 0:D + 1])
            ins.then_inc(s["copied"], 1)
            dve.wait_ge(s["turned"], 1)
            for k in range(2):
                dve.tensor_copy(yT[:, k, :], ps[k][:, :]).then_inc(s["copied"], 1)
            dve.tensor_copy(norm_row[:, :], ps[6][0:1, :]).then_inc(s["copied"], 1)
            dve.wait_ge(s["tokens"], 1)
            ch.link(dve.tensor_scalar(den[:, :], ps[4][0:NG, 0:NH], 1e-5, None, ALU.add))
            ch.link(dve.reciprocal(den[:, :], den[:, :]))
            dve.tensor_tensor(by_head(tok), by_head(ps[3][0:NG, :]), den[:, :].unsqueeze(2).broadcast_to([NG, NH, DH]), ALU.mult).then_inc(s["tok_ready"], 1)
            dve.wait_ge(s["tok_turned"], 1)
            dve.tensor_copy(tokT[:, :], ps[5][0:DH, :]).then_inc(s["tokT_ready"], 1)
            dve.wait_ge(s["qkv"], 1)
            for k, a in enumerate((qT, kT, v)):
                dve.tensor_copy(a[:, :], ps[k][0:DH, :]).then_inc(s["qkv_ready"], 1)
            dve.wait_ge(s["scored"], 1)
            ch.link(dve.tensor_reduce(peak[:, :], by_head(ps[3][0:NG, :]), AX.X, ALU.max))
            dve.tensor_tensor(by_head(at), by_head(ps[3][0:NG, :]), peak[:, :].unsqueeze(2).broadcast_to([NG, NH, NG]), ALU.subtract).then_inc(s["exp_in"], 1)
            dve.wait_ge(s["exp_out"], 1)
            ch.link(dve.tensor_reduce(peak[:, :], by_head(at), AX.X, ALU.add))
            ch.link(dve.reciprocal(peak[:, :], peak[:, :]))
            dve.tensor_tensor(by_head(at), by_head(at), peak[:, :].unsqueeze(2).broadcast_to([NG, NH, NG]), ALU.mult).then_inc(s["attn"], 1)
            dve.wait_ge(s["attn_turned"], 1)
            dve.tensor_copy(atT[:, :], ps[4][0:NG, :]).then_inc(s["attnT_ready"], 1)
            dve.wait_ge(s["mixed"], 1)
            dve.tensor_copy(mixT[:, :], ps[5][0:DH, :]).then_inc(s["mixed_ready"], 1)
            dve.wait_ge(s["backed"], 1)
            for b in range(4):
                to = (back[0:NG, :, :], odd)[b // 2]
                ch.link(dve.tensor_copy(to[:, 2 * (b % 2):2 * (b % 2) + 2, :], ps[b][0:NG, :].rearrange("p (j d) -> p j d", j=2)))
            dve.sem_inc(s["back_ready"], 1)

        def scalar(act):
            act.wait_ge(s["exp_in"], 1)
            act.activation(at[:, :], at[:, :], ACT.Exp, scale=scale).then_inc(s["exp_out"], 1)

        run_block(nc, {"sync": sync, "tensor": tensor, "vector": vector, "scalar": scalar})

    with ExitStack() as c2:
        here = sb("sb_here", [P, 2, PAIRS * P], F32, c2)
        here_ready, products, added, own = (sem("sb_" + n) for n in ("here_ready", "products", "added", "own"))
        tiles = LASTT + 1

        def each(eng, body):
            for i in rounds_of(eng, tiles // 2):
                for u in range(2):
                    body(i * 2 + u, u)
            if tiles % 2:
                body(tiles - 1, 0)

        def scalar(act):
            def body(t, u):
                wait_from(act, products, t)
                act.copy(here[:, u, :].rearrange("p (j n) -> p j n", j=PAIRS), wT[:, :, ds(t * P, P)]).then_inc(here_ready, 1)
            each(act, body)

        def tensor(pe):
            pe.sem_inc(products, 1)

            def body(t, u):
                wait_from(pe, here_ready, t + 1)
                wait_from(pe, added, t)
                for j in range(PAIRS):
                    mm = pe.matmul(ps[u][:, 0:D], here[:, u, j * P:(j + 1) * P], back[:, j, :], start=(j == 0), stop=(j == PAIRS - 1))
                mm.then_inc(products, 1)
            each(pe, body)

        def vector(dve):
            dve.sem_inc(added, 1)
            ch = Chain(dve, own)

            def body(t, u):
                ch.enter(t)
                wait_from(dve, products, t + 2)
                ch.link(dve.tensor_tensor(row(X, t), ps[u][:, 0:D], row(X, t), ALU.add))
                dve.tensor_tensor(row(X, t), row(X, t), b_out[:, :], ALU.add).then_inc(added, 1)
            each(dve, body)

        run_block(nc, {"scalar": scalar, "tensor": tensor, "vector": vector})


H1, F1 = 8, 32
HB = F1 + 1
HW = H1 * HB
RW = HW + H1


def graph_attention(g, c):
    nc, sb, sem, ps, X, ident = (g[n] for n in ("nc", "sb", "sem", "ps", "X", "ident"))
    banks01 = g["banks01"]
    h_rows = nc.dram_tensor("h_rows", [NT * P, RW], F32)
    dst_scores = sb("dst_scores", [P, NT, H1], F32, c)
    local_key = sb("key1", [P, SG], F32, c)
    row_of = sb("row1", [P, SG], U32, c)
    four_tiles = sb("four_tiles1", [1, SG // 4], I32, c)
    acc = sb("acc", [P, NT, HW], F32, c)

    with ExitStack() as c2:
        w = sb("ga_w", [P, 2, H1, F1], F32, c2)
        av = sb("ga_av", [P, 2, H1, F1], F32, c2)
        wa = sb("ga_wa", [P, 2, H1, F1], F32, c2)
        wall = sb("ga_wall", [P, 2, H1 * F1 + 2 * H1], F32, c2)
        stage = sb("ga_stage", [P, 4, D], F32, c2)
        shift = sb("ga_shift", [P, NT], F32, c2)
        zT = sb("ga_zT", [P, 2, 2, P], F32, c2)
        new = sb("ga_new", [P, 2, RW], F32, c2)
        loaded, shifted, folded, staged, turned, zt_ready, products, new_ready, taken, own = (
            sem("ga_" + n) for n in ("loaded", "shifted", "folded", "staged", "turned", "zt_ready", "products", "new_ready", "taken", "own"))
        stored = [sem(f"ga_stored{u}") for u in range(2)]
        mean, rstd, norm_vector, norm_scalar = row_norm(g, c2, "ln2")

        def sync(sp):
            for k in range(2):
                sp.dma_start(w[:, k, :, :], g["L1_gnn_W"].rearrange("h (c p) f -> c p h f", p=P)[k]).then_inc(loaded, 16)
            for k, a in enumerate(("L1_gnn_a_src", "L1_gnn_a_dst")):
                sp.dma_start(av[:, k, :, :].rearrange("p h f -> p (h f)"), g[a].rearrange("(a h) f -> a (h f)", a=1).broadcast_to([P, H1 * F1])).then_inc(loaded, 16)
            sp.dma_start(local_key[:, :], g["key_by_dst"][:, :]).then_inc(loaded, 16)
            sp.dma_start(row_of[:, :], g["row_by_dst"][:, :]).then_inc(loaded, 16)
            sp.dma_start(four_tiles[:, :], g["four_tiles_dram"][1:2, :]).then_inc(loaded, 16)
            with sp.Fori(0, NT // 2) as i:
                for u in range(2):
                    wait_from(sp, new_ready, (i * 2 + u + 1) * 2)
                    sp.dma_start(h_rows[ds((i * 2 + u) * P, P), :], new[:, u, :]).then_inc(stored[u], 16)
            for u in range(2):
                sp.wait_ge(stored[u], 16 * (NT // 2))

        def vector(dve):
            ch = Chain(dve, own)
            norm_vector(dve)
            ch.link(dve.scalar_tensor_tensor(out=shift[:, :], in0=mean[:, :], scalar=-1.0, in1=rstd[:, :], op0=ALU.mult, op1=ALU.mult))
            dve.sem_inc(shifted, 1)
            dve.memset(acc[:, :, :], 0.0)
            for u in range(2):
                ch.link(dve.memset(new[:, u, :], 1.0))
            dve.sem_inc(taken, 1)
            dve.wait_ge(loaded, 112)
            for k in range(2):
                dve.tensor_copy(wall[:, k, 0:H1 * F1], w[:, k, :, :].rearrange("p h f -> p (h f)")).then_inc(folded, 1)
                for q in range(2):
                    ch.link(dve.tensor_tensor(wa[:, k, :, :], w[:, k, :, :], av[:, q, :, :], ALU.mult))
                    at = H1 * F1 + q * H1
                    ch.link(dve.tensor_reduce(wall[:, k, at:at + H1], wa[:, k, :, :], AX.X, ALU.add))
            ch.wait()
            dve.sem_inc(folded, 1)

            def take(t, slot, lap):
                u = slot % 2
                wait_from(dve, products, t + 1)
                wait_from(dve, stored[u], (lap * 2 + slot // 2) * 16)
                dve.tensor_copy(new[:, u, 0:HW].rearrange("p (h b) -> p h b", b=HB)[:, :, 0:F1],
                                ps[u][:, 0:H1 * F1].rearrange("p (h f) -> p h f", f=F1)).then_inc(new_ready, 1)
                dve.tensor_copy(new[:, u, HW:RW], ps[u][:, H1 * F1:H1 * F1 + H1]).then_inc(new_ready, 1)
                dve.tensor_scalar(row(dst_scores, t), ps[u][:, H1 * F1 + H1:H1 * F1 + 2 * H1], 1.0, None, ALU.mult).then_inc(taken, 1)

            laps(dve, take, NT)

        def scalar(act):
            norm_scalar(act)
            act.wait_ge(shifted, 1)

            def put_stage(t, slot, lap):
                wait_from(act, turned, t - 3)
                act.activation(stage[:, slot, :], row(X, t), ACT.Identity, bias=shift[:, ds(t, 1)], scale=rstd[:, ds(t, 1)]).then_inc(staged, 1)

            def copy_turned(t, slot):
                u = slot % 2
                wait_from(act, turned, t + 1)
                wait_from(act, products, t - 1)
                act.copy(zT[:, u, :, :].rearrange("p k n -> p (k n)"), ps[4 + u][:, 0:2 * P]).then_inc(zt_ready, 1)

            def step(t, slot, lap):
                if not isinstance(t, int) or t + 1 < NT:
                    copy_turned(t + 1, (slot + 1) % 4)
                if not isinstance(t, int) or t + 2 < NT:
                    put_stage(t + 2, (slot + 2) % 4, lap + (slot + 2) // 4)

            put_stage(0, 0, 0)
            put_stage(1, 1, 0)
            copy_turned(0, 0)
            laps(act, step, NT)

        def tensor(pe):
            def turn(t, slot):
                wait_from(pe, staged, t + 1)
                wait_from(pe, zt_ready, t - 1)
                for k in range(2):
                    mm = pe.transpose(ps[4 + slot % 2][:, k * P:(k + 1) * P], stage[:, slot, k * P:(k + 1) * P], ident[:, :])
                mm.then_inc(turned, 1)

            def multiply(t, slot, lap):
                u = slot % 2
                if not isinstance(t, int) or t + 1 < NT:
                    turn(t + 1, (slot + 1) % 4)
                wait_from(pe, zt_ready, t + 1)
                wait_from(pe, taken, t)
                for k in range(2):
                    mm = pe.matmul(ps[u][:, 0:H1 * F1 + 2 * H1], zT[:, u, k, :], wall[:, k, :], start=(k == 0), stop=(k == 1))
                mm.then_inc(products, 1)

            pe.wait_ge(folded, 3)
            turn(0, 0)
            laps(pe, multiply, NT)

        run_block(nc, {"sync": sync, "vector": vector, "scalar": scalar, "tensor": tensor})

    pool_passed = sem("ge_pool_passed")
    with ExitStack() as c2:
        halves_count = STEPS // HALF
        HE = HALF * P
        BLOCKS = HALF + 1
        rows = sb("ge_rows", [P, 4, HALF, RW], F32, c2)
        index = sb("ge_index", [P, 4, HALF], U32, c2)
        place = sb("ge_place", [P, 4, HALF, P], F32, c2)
        placeT = sb("ge_placeT", [P, 2, 4, P], F32, c2)
        cuts = sb("ge_cuts", [H1, 2, 2, HE], F32, c2)
        goes_on = sb("ge_goes_on", [H1, halves_count + 2], F32, c2)
        upto_edge = sb("ge_upto_edge", [H1, 2, HE], F32, c2)
        run_peak = sb("ge_run_peak", [H1, BLOCKS * P], F32, c2)
        fresh = sb("ge_fresh", [H1, 1], F32, c2)
        at_dst = sb("ge_at_dst", [P, BLOCKS, H1], F32, c2)
        sc = sb("ge_sc", [P, 2, BLOCKS, H1], F32, c2)
        weight = sb("ge_weight", [P, HALF, H1], F32, c2)
        drop = sb("ge_drop", [P, H1], F32, c2)
        scale = sb("ge_scale", [P, H1], F32, c2)
        names = ("ready", "distances", "indexed", "placed", "src_turned", "places_turned", "placesT_ready", "runs_made", "dst_scored",
                 "dst_taken", "peaks_turned", "exp_in", "exp_out", "weighted", "summed", "drop_ready", "drop_placed",
                 "scale_ready", "scan_own", "scores_own", "adds", "scaled")
        (ready, distances, indexed, placed, src_turned, places_turned, placesT_ready, runs_made, dst_scored, dst_taken, peaks_turned,
         exp_in, exp_out, weighted, summed, drop_ready, drop_placed, scale_ready, scan_own, scores_own, adds, scaled) = (
            sem("ge_" + n) for n in names)
        fetched = [sem(f"ge_fetched{h}") for h in range(4)]
        cut_loaded = [sem(f"ge_cut_loaded{h}") for h in range(2)]
        goes_on_loaded = sem("ge_goes_on_loaded")
        turned_bank, small, sums = ps[2], ps[4], [ps[3]] + ps[5:8]
        PEAKS = BLOCKS * H1
        DROPS = 2 * BLOCKS * H1
        AHEAD = 4 * HALF
        ADDS_AHEAD = 3

        def gpsimd(pool):
            def gather(n, slot, lap):
                wait_apart(pool, fetched[slot], lap * (16 * HALF), pool_passed)
                pool.tensor_copy(index[:, slot, :], row_of[:, ds(n * HALF, HALF)]).then_inc(indexed, 1)
                wait_apart(pool, indexed, n + 1, pool_passed)
                for k in range(HALF):
                    wait_apart(pool, summed, n * HALF + k + 1, pool_passed)
                    pool.indirect_dma_start(out=rows[:, slot, k, :], out_offset=None, in_=h_rows[:, :],
                                            in_offset=bass.IndirectOffsetOnAxis(ap=index[:, slot, k:k + 1], axis=0)).then_inc(fetched[slot], 16)
            laps(pool, gather, halves_count + 2)

        def sync(sp):
            starts = g["cuts_dram"][0:1, 0:(halves_count + 2) * HE].rearrange("a (n e) -> a n e", e=HE)[:, :, 0]
            sp.dma_start(goes_on[:, :], starts.broadcast_to([H1, halves_count + 2]), allow_slow_non_contiguous=True).then_inc(goes_on_loaded, 16)

            def load_cuts(n, slot, lap):
                wait_from(sp, runs_made, n - 1)
                for a in range(2):
                    sp.dma_start(cuts[:, slot % 2, a, :], g["cuts_dram"][a:a + 1, ds(n * HE, HE)].broadcast_to([H1, HE])).then_inc(cut_loaded[slot % 2], 16)
            laps(sp, load_cuts, halves_count + 2)

        def tensor(pe):
            def turn_places(n, slot, q):
                wait_from(pe, placed, n + 1)
                wait_from(pe, placesT_ready, n * 2 + q)
                for k in range(4):
                    mm = pe.transpose(turned_bank[:, k * P:(k + 1) * P], place[:, slot, q * 4 + k, :], ident[:, :])
                mm.then_inc(places_turned, 1)

            def turn_src(n, slot, lap):
                wait_from(pe, fetched[slot], (lap + 1) * (16 * HALF))
                wait_from(pe, runs_made, n)
                for k in range(HALF):
                    mm = pe.matmul(banks01[0:H1, k * P:(k + 1) * P], rows[:, slot, k, HW:RW], ident[:, :], start=True, stop=True)
                mm.then_inc(src_turned, 1)

            def turn_peaks(n):
                wait_from(pe, scale_ready, n)
                wait_from(pe, runs_made, n + 1)
                for k in range(BLOCKS):
                    at = PEAKS + k * H1
                    mm = pe.matmul(small[:, at:at + H1], run_peak[:, k * P:(k + 1) * P], ident[0:H1, 0:H1], start=True, stop=True)
                mm.then_inc(peaks_turned, 1)

            def score_dst(n):
                for k in range(HALF):
                    if k % 4 == 0:
                        tiles = tiles_of_four(pe, four_tiles, n * 2 + k // 4)
                        wait_from(pe, placesT_ready, n * 2 + k // 4 + 1)
                    if k == 0:
                        pe.matmul(small[:, HALF * H1:BLOCKS * H1], placeT[:, 0, 0, :], row(dst_scores, tiles[0]), start=True, stop=True)
                    mm = pe.matmul(small[:, k * H1:(k + 1) * H1], placeT[:, k // 4, k % 4, :], row(dst_scores, tiles[k % 4]), start=True, stop=True)
                mm.then_inc(dst_scored, 1)

            def place_drop(n, slot):
                wait_from(pe, drop_ready, n + 1)
                pe.matmul(small[:, DROPS:DROPS + H1], place[0:1, slot, 0, :], drop[0:1, :], start=True, stop=True).then_inc(drop_placed, 1)

            def sum_rows(n, slot, some):
                for k in some:
                    wait_from(pe, adds, n * HALF + k)
                    pe.matmul(sums[k % 4][:, 0:HW], place[:, slot, k, :], rows[:, slot, k, 0:HW], start=True, stop=True).then_inc(summed, 1)

            def both(n, slot, lap):
                turn_places(n + 1, (slot + 1) % 4, 0)
                wait_from(pe, weighted, n + 1)
                sum_rows(n, slot, (0, 1))
                turn_places(n + 1, (slot + 1) % 4, 1)
                sum_rows(n, slot, (2, 3))
                turn_peaks(n + 1)
                score_dst(n + 1)
                sum_rows(n, slot, range(4, HALF))
                turn_src(n + 2, (slot + 2) % 4, lap + (slot + 2) // 4)
                place_drop(n + 1, (slot + 1) % 4)

            pe.sem_inc(summed, AHEAD)
            turn_places(0, 0, 0)
            turn_places(0, 0, 1)
            turn_src(0, 0, 0)
            turn_peaks(0)
            score_dst(0)
            turn_src(1, 1, 0)
            place_drop(0, 0)
            laps(pe, both, halves_count)

        def scalar(act):
            def put_places(n, slot):
                wait_from(act, summed, n * HALF + HALF)
                for k in range(HALF):
                    act.activation(place[:, slot, k, :], g["iota_row"][:, :], ACT.Abs, bias=local_key[:, ds(n * HALF + k, 1)]).then_inc(distances, 1)
                wait_from(act, distances, (n + 1) * HALF)
                act.activation(place[:, slot, :, :], place[:, slot, :, :], ACT.Relu, bias=g["ones"][:, 0:1], scale=-1.0).then_inc(placed, 1)

            def front(n, far):
                for q in range(2):
                    wait_from(act, places_turned, n * 2 + q + 1)
                    wait_from(act, dst_scored, n)
                    act.copy(placeT[:, q, :, :].rearrange("p k n -> p (k n)"), turned_bank[:, :]).then_inc(placesT_ready, 1)
                if far:
                    put_places(*far)
                wait_from(act, dst_scored, n + 1)
                act.copy(at_dst[:, :, :].rearrange("p s h -> p (s h)"), small[:, 0:PEAKS]).then_inc(dst_taken, 1)
                wait_from(act, exp_in, n + 1)
                act.activation(weight[:, :, :], sc[:, 0, 0:HALF, :], ACT.Exp).then_inc(exp_out, 1)
                wait_from(act, drop_placed, n + 1)
                act.activation(scale[:, :], small[:, DROPS:DROPS + H1], ACT.Exp).then_inc(scale_ready, 1)

            def both(n, slot, lap):
                front(n + 1, (n + 3, (slot + 3) % 4))

            act.wait_ge(ready, 5)
            for n in range(3):
                put_places(n, n)
            front(0, None)
            laps(act, both, halves_count)

        def vector(dve):
            def scan_runs(n, h, lap):
                ch = Chain(dve, scan_own, n * 3)
                wait_from(dve, src_turned, n + 1)
                wait_from(dve, cut_loaded[h], (lap + 1) * 32)
                wait_from(dve, peaks_turned, n)
                carried = upto_edge[:, 1 - h, HE - 1:HE]
                ch.link(dve.tensor_tensor_scan(upto_edge[:, h, :], cuts[:, h, 0, :], banks01[0:H1, :], carried, ALU.add, ALU.max))
                ch.link(dve.tensor_tensor_scan(run_peak[:, HE - 1::-1], cuts[:, h, 1, ::-1], upto_edge[:, h, ::-1], -FAR, ALU.add, ALU.max))
                ch.link(dve.tensor_scalar(fresh[:, :], run_peak[:, 0:1], goes_on[:, ds(n, 1)], None, ALU.add))
                dve.scalar_tensor_tensor(out=run_peak[:, HE:HE + 1], in0=carried, scalar=cuts[:, h, 0, 0:1], in1=fresh[:, :],
                                         op0=ALU.add, op1=ALU.max).then_inc(runs_made, 1)

            def edge_scores(n, slot):
                ch = Chain(dve, scores_own, n * 3)
                wait_from(dve, peaks_turned, n + 1)
                wait_from(dve, dst_taken, n + 1)
                ch.step(dve.tensor_tensor(sc[:, 0, 0:HALF, :], rows[:, slot, :, HW:RW], at_dst[:, 0:HALF, :], ALU.add))
                ch.link(dve.tensor_tensor(sc[:, 1, :, :].rearrange("p s h -> p (s h)"), small[:, PEAKS:DROPS],
                                          at_dst[:, :, :].rearrange("p s h -> p (s h)"), ALU.add))
                both_sc = sc[:, :, :, :].rearrange("p a s h -> p (a s h)")
                ch.link(dve.scalar_tensor_tensor(out=both_sc, in0=both_sc, scalar=0.2, in1=both_sc, op0=ALU.mult, op1=ALU.max))
                dve.tensor_tensor(sc[:, 0, 0:HALF, :], sc[:, 0, 0:HALF, :], sc[:, 1, 0:HALF, :], ALU.subtract).then_inc(exp_in, 1)
                dve.tensor_tensor(drop[:, :], sc[:, 1, HALF, :], sc[:, 1, 0, :], ALU.subtract).then_inc(drop_ready, 1)

            def weigh(n, slot):
                wait_from(dve, exp_out, n + 1)
                blocks = rows[:, slot, :, 0:HW].rearrange("p s (h b) -> p s h b", b=HB)
                dve.tensor_tensor(blocks, blocks, weight[:, :, :].unsqueeze(3).broadcast_to([P, HALF, H1, HB]), ALU.mult).then_inc(weighted, 1)

            def rescale(n, tile):
                blocks = row(acc, tile).rearrange("p (h b) -> p h b", b=HB)
                wait_from(dve, scale_ready, n + 1)
                wait_from(dve, adds, n * HALF + ADDS_AHEAD)
                dve.tensor_tensor(blocks, blocks, scale[:, :].unsqueeze(2).broadcast_to([P, H1, HB]), ALU.mult).then_inc(scaled, 1)
                wait_from(dve, scaled, n + 1)

            def add_sums(n, tiles, some):
                for k in some:
                    here = flat_row(dve, acc, tiles[k % 4])
                    if k % 2 == 0:
                        wait_from(dve, summed, n * HALF + k + 2 + AHEAD)
                    wait_from(dve, adds, n * HALF + k + ADDS_AHEAD)
                    dve.tensor_tensor(here, sums[k % 4][:, 0:HW], here, ALU.add).then_inc(adds, 1)

            def both(n, slot, lap):
                tiles = tiles_of_four(dve, four_tiles, n * 2)
                rescale(n, tiles[0])
                add_sums(n, tiles, (0, 1, 2, 3))
                edge_scores(n + 1, (slot + 1) % 4)
                tiles = tiles_of_four(dve, four_tiles, n * 2 + 1)
                add_sums(n, tiles, (4, 5))
                weigh(n + 1, (slot + 1) % 4)
                add_sums(n, tiles, (6, 7))
                scan_runs(n + 2, slot % 2, lap * 2 + slot // 2 + 1)

            dve.memset(upto_edge[:, 1, HE - 1:HE], -FAR).then_inc(ready, 1)
            dve.memset(run_peak[:, :], 0.0).then_inc(ready, 1)
            dve.memset(sc[:, :, :, :], 0.0).then_inc(ready, 1)
            dve.wait_ge(goes_on_loaded, 16)
            dve.tensor_scalar(goes_on[:, :], goes_on[:, :], -1.0, -FAR, ALU.mult, ALU.add).then_inc(ready, 1)
            dve.sem_inc(adds, ADDS_AHEAD)
            dve.tensor_scalar(local_key[:, :], local_key[:, :], -1.0, None, ALU.mult).then_inc(ready, 1)
            dve.wait_ge(ready, 5)
            scan_runs(0, 0, 0)
            edge_scores(0, 0)
            weigh(0, 0)
            scan_runs(1, 1, 0)
            laps(dve, both, halves_count)

        run_block(nc, {"gpsimd": gpsimd, "sync": sync, "tensor": tensor, "scalar": scalar, "vector": vector})

    with ExitStack() as c2:
        den = sb("gx_den", [P, NT, H1], F32, c2)
        many = 10
        out_rows = sb("gx_out", [P, many, D], F32, c2)
        own = sem("gx_own")

        def vector(dve):
            ch = Chain(dve, own)
            blocks = acc[:, :, :].rearrange("p t (h b) -> p t h b", b=HB)
            ch.link(dve.tensor_scalar(den[:, :, :], blocks[:, :, :, F1], 1e-8, None, ALU.add))
            ch.link(dve.reciprocal(den[:, :, :], den[:, :, :]))
            start = ch.n
            with dve.Fori(0, NT // many) as i:
                ch.enter(i * 2 + start)
                tiles = ds(i * many, many)
                ch.link(dve.tensor_tensor(out_rows[:, :, :].rearrange("p t (h f) -> p t h f", f=F1), blocks[:, tiles, :, 0:F1],
                                          den[:, tiles, :].unsqueeze(3).broadcast_to([P, many, H1, F1]), ALU.mult))
                ch.link(dve.tensor_tensor(X[:, tiles, :], X[:, tiles, :], out_rows[:, :, :], ALU.add))

        run_block(nc, {"vector": vector})


HID, NE = 1024, 8
HC = HID // P
XW = D + 5
ESTEPS = LASTT + 1 + NE - 1


def laps(eng, body, count):
    whole = (count - 1) // 4
    for t in range(4):
        body(t, t, 0)
    with eng.Fori(1, whole) as i:
        for v in range(4):
            body(i * 4 + v, v, i)
    for t in range(4 * whole, count):
        body(t, t % 4, t // 4)


def hidden(g, c, pre, count, stage, product, consume):
    nc, sb, sem, ps, ident, w1, b1 = (g[n] for n in ("nc", "sb", "sem", "ps", "ident", "w1", "b1"))
    rows = sb(pre + "rows", [P, 4, D], F32, c)
    zT = sb(pre + "zT", [P, 2, 2, P], F32, c)
    hT = sb(pre + "hT", [P, 2, HC, P], F32, c)
    staged, turned, zt_ready, h_done, gelu_done, produced, taken = (
        sem(pre + n) for n in ("staged", "turned", "zt_ready", "h_done", "gelu_done", "produced", "taken"))

    def after(slot, lap, by):
        return (slot + by) % 4, lap + (slot + by) // 4

    def vector(dve):
        def stage_of(t, slot, lap):
            wait_from(dve, turned, t - 3)
            stage(dve, t, slot, lap, rows[:, slot, :]).then_inc(staged, 1)

        def consume_of(t, slot, lap):
            wait_from(dve, produced, t + 1)
            consume(dve, t, slot, lap, lambda ins: ins.then_inc(taken, 1))

        def body(t, slot, lap):
            if not isinstance(t, int) or t + 2 < count:
                stage_of(t + 2, *after(slot, lap, 2))
            if not isinstance(t, int) or t > 0:
                consume_of(t - 1, (slot - 1) % 4, lap - (slot == 0))

        stage_of(0, 0, 0)
        stage_of(1, 1, 0)
        laps(dve, body, count)
        consume_of(count - 1, (count - 1) % 4, (count - 1) // 4)

    def scalar(act):
        def turn_copy(t, u):
            wait_from(act, turned, t + 1)
            wait_from(act, h_done, (t - 1) * 2)
            act.copy(zT[:, u, :, :].rearrange("p k n -> p (k n)"), ps[4 + u][:, 0:2 * P]).then_inc(zt_ready, 1)

        def body(t, slot, lap):
            u = slot % 2
            wait_from(act, produced, t - 1)
            for m in range(HC):
                if m % 4 == 0:
                    wait_from(act, h_done, t * 2 + m // 4 + 1)
                act.activation(hT[:, u, m, :], ps[2 * u + m // 4][:, (m % 4) * P:(m % 4 + 1) * P], ACT.Gelu,
                               bias=b1[:, m:m + 1]).then_inc(gelu_done, 1)
            if not isinstance(t, int) or t + 1 < count:
                turn_copy(t + 1, 1 - u)

        turn_copy(0, 0)
        laps(act, body, count)

    def tensor(pe):
        pe.wait_ge(g["w_loaded"], g["w_count"])

        def turn(t, slot):
            u = slot % 2
            wait_from(pe, staged, t + 1)
            wait_from(pe, zt_ready, t - 1)
            for k in range(2):
                mm = pe.transpose(ps[4 + u][:, k * P:(k + 1) * P], rows[:, slot, k * P:(k + 1) * P], ident[:, :])
            mm.then_inc(turned, 1)

        def produce(t, u):
            wait_from(pe, gelu_done, (t + 1) * HC)
            wait_from(pe, taken, t - 1)
            product(pe, t, u, hT[:, u, :, :]).then_inc(produced, 1)

        def body(t, slot, lap):
            u = slot % 2
            wait_from(pe, zt_ready, t + 1)
            wait_from(pe, gelu_done, (t - 1) * HC)
            for m in range(HC):
                for k in range(2):
                    mm = pe.matmul(ps[2 * u + m // 4][:, (m % 4) * P:(m % 4 + 1) * P], w1[:, k, m * P:(m + 1) * P], zT[:, u, k, :],
                                   start=(k == 0), stop=(k == 1))
                if m % 4 == 3:
                    mm.then_inc(h_done, 1)
            if not isinstance(t, int) or t + 1 < count:
                turn(t + 1, (slot + 1) % 4)
            if not isinstance(t, int) or t > 0:
                produce(t - 1, 1 - u)

        turn(0, 0)
        laps(pe, body, count)
        produce(count - 1, (count - 1) % 2)

    return {"vector": vector, "scalar": scalar, "tensor": tensor, "taken": taken}


def routed_network(g, c, out):
    nc, sb, sem, ps, X, ident = (g[n] for n in ("nc", "sb", "sem", "ps", "X", "ident"))
    routed_rows = nc.dram_tensor("routed_rows", [NT * P, XW], F32)
    tile_of_estep = nc.dram_tensor("tile_of_estep", [2, 64], I32)
    w1 = g["w1"] = sb("w1", [P, 2, HID], F32, c)
    b1 = g["b1"] = sb("b1", [P, HC], F32, c)
    wg = sb("wg", [P, HC, NE], F32, c)
    bg = sb("bg", [P, NE], F32, c)
    wd = sb("wd", [P, NE, HC, D], F32, c)
    bd = sb("bd", [P, NE, D], F32, c)
    gates = sb("gates", [P, NT, NE], F32, c)
    w_loaded = g["w_loaded"] = sem("ffn_w_loaded")
    g["w_count"] = 64
    expert_of = sb("expert_of", [P, 64], F32, c)
    step_tables = sb("step_tables", [1, 2, 64], I32, c)
    mean, rstd, norm_vector, norm_scalar = row_norm(g, c, "ln3")

    with ExitStack() as c2:
        def stage(dve, t, slot, lap, to):
            return dve.tensor_scalar(to, row(X, t), mean[:, ds(t, 1)], rstd[:, ds(t, 1)], ALU.subtract, ALU.mult)

        def product(pe, t, u, hT):
            for m in range(HC):
                mm = pe.matmul(ps[6 + u][:, 0:NE], hT[:, m, :], wg[:, m, :], start=(m == 0), stop=(m == HC - 1))
            return mm

        def consume(dve, t, slot, lap, signal):
            signal(dve.tensor_tensor(row(gates, t), ps[6 + slot % 2][:, 0:NE], bg[:, :], ALU.add))

        programs = hidden(g, c2, "fa_", NT, stage, product, consume)

        def vector(dve):
            norm_vector(dve)
            dve.wait_ge(w_loaded, 64)
            programs["vector"](dve)

        def scalar(act):
            norm_scalar(act)
            act.wait_ge(w_loaded, 64)
            programs["scalar"](act)

        def sync(sp):
            sp.dma_start(w1[:, :, :], g["L1_ffn_W1"].rearrange("(k p) n -> p k n", p=P)).then_inc(w_loaded, 16)
            with nc.allow_non_contiguous_dma(reason="1024 numbers"):
                sp.dma_start(b1[:, :], g["L1_ffn_b1"].rearrange("(m p) -> p m", p=P)).then_inc(w_loaded, 16)
            sp.dma_start(wg[:, :, :], g["L1_ffn_Wg"].rearrange("(m p) e -> p m e", p=P)).then_inc(w_loaded, 16)
            sp.dma_start(bg[:, :], g["L1_ffn_bg"].rearrange("(a e) -> a e", a=1).broadcast_to([P, NE])).then_inc(w_loaded, 16)
            sp.wait_ge(w_loaded, 64)
            for e in range(NE):
                sp.dma_start(wd[:, e, :, :], g["L1_ffn_Wd"][e].rearrange("(m p) d -> p m d", p=P)).then_inc(w_loaded, 16)
            sp.dma_start(bd[:, :, :].rearrange("p e d -> p (e d)"), g["L1_ffn_bd"].rearrange("(a e) d -> a (e d)", a=1).broadcast_to([P, NE * D])).then_inc(w_loaded, 16)
            sp.wait_ge(w_loaded, 64 + 16 * (NE + 1))

        run_block(nc, {"sync": sync, "vector": vector, "scalar": scalar, "tensor": programs["tensor"]})

    with ExitStack() as c2:
        NB = NE + 1
        top = sb("rt_top", [P, NT], F32, c2)
        tot = sb("rt_tot", [P, NT], F32, c2)
        cand = sb("rt_cand", [P, NT, NE], F32, c2)
        extra = sb("rt_extra", [P, NT, 5], F32, c2)
        pad = sb("rt_pad", [P, NT], F32, c2)
        mask = sb("rt_mask", [P, NT], F32, c2)
        mask_u = sb("rt_mask_u", [P, NT], U32, c2)
        count = sb("rt_count", [P, NB], F32, c2)
        total = sb("rt_total", [P, NB], F32, c2)
        upto_b = sb("rt_upto", [P, NB], F32, c2)
        base = sb("rt_base", [P, NB], F32, c2)
        border_i = sb("rt_border_i", [P, NB], I32, c2)
        border = sb("rt_border", [P, NB], F32, c2)
        rank = sb("rt_rank", [P, NT], F32, c2)
        pos = sb("rt_pos", [P, NT], F32, c2)
        pos_u = sb("rt_pos_u", [P, NT], U32, c2)
        steps_i = sb("rt_steps_i", [P, 2, 64], I32, c2)
        steps_f = sb("rt_steps_f", [P, 64], F32, c2)
        hit = sb("rt_hit", [P, 64], F32, c2)
        ring = sb("rt_ring", [P, 2, XW], F32, c2)
        ring_pos = sb("rt_ring_pos", [P, 2, 1], U32, c2)
        own, exp_in, exp_out, counted, totals, pos_ready, ring_ready, ring_at, steps_ready, tables_in = (
            sem("rt_" + n) for n in ("own", "exp_in", "exp_out", "counted", "totals", "pos_ready", "ring_ready", "ring_at",
                                     "steps_ready", "tables_in"))
        scattered = [sem(f"rt_scattered{u}") for u in range(2)]
        pool_passed = sem("rt_pool_passed")

        def vector(dve):
            ch = Chain(dve, own)
            ch.link(dve.tensor_reduce(top[:, :], gates[:, :, :], AX.X, ALU.max))
            dve.tensor_tensor(gates[:, :, :], gates[:, :, :], top[:, :].unsqueeze(2).broadcast_to([P, NT, NE]), ALU.subtract).then_inc(exp_in, 1)
            dve.wait_ge(exp_out, 1)
            ch.link(dve.tensor_reduce(tot[:, :], gates[:, :, :], AX.X, ALU.add))
            ch.link(dve.reciprocal(extra[:, :, 0], tot[:, :]))
            ch.link(dve.tensor_scalar(cand[:, :, :], gates[:, :, :], 1.0, float(NB), ALU.is_lt, ALU.mult))
            ch.link(dve.tensor_tensor(cand[:, :, :], cand[:, :, :], g["iota_row"][:, 0:NE].unsqueeze(1).broadcast_to([P, NT, NE]), ALU.add))
            ch.link(dve.tensor_reduce(extra[:, :, 1], cand[:, :, :], AX.X, ALU.min))
            ch.link(dve.tensor_scalar(extra[:, :, 2], g["iota_row"][:, 0:NT], float(P), None, ALU.mult))
            ch.link(dve.tensor_scalar(extra[:, :, 2], extra[:, :, 2], g["iota_part"][:, 0:1], None, ALU.add))
            ch.link(dve.tensor_scalar(pad[:, :], extra[:, :, 2], float(N), float(NE), ALU.is_ge, ALU.mult))
            ch.link(dve.tensor_tensor(extra[:, :, 1], extra[:, :, 1], pad[:, :], ALU.max))
            ch.step(dve.tensor_copy(extra[:, :, 3], mean[:, :]))
            ch.step(dve.tensor_copy(extra[:, :, 4], rstd[:, :]))
            for b in range(NB):
                ch.link(dve.tensor_scalar(mask[:, :], extra[:, :, 1], float(b), 0.0, ALU.is_equal, ALU.add, accum_out=count[:, b:b + 1]))
            dve.sem_inc(counted, 1)
            dve.wait_ge(totals, 1)
            ch.link(dve.tensor_copy(total[:, :], ps[0][:, 0:NB]))
            ch.link(dve.tensor_tensor_scan(upto_b[:, :], total[:, :], total[:, :], 0.0, ALU.add, ALU.bypass))
            ch.link(dve.tensor_tensor(upto_b[:, :], upto_b[:, :], total[:, :], ALU.subtract))
            ch.link(dve.scalar_tensor_tensor(out=base[:, :], in0=ps[1][:, 0:NB], scalar=-1.0, in1=upto_b[:, :], op0=ALU.add, op1=ALU.add))
            ch.link(dve.memset(pos[:, :], 0.0))
            for b in range(NB):
                ch.link(dve.tensor_scalar(mask_u[:, :], extra[:, :, 1], float(b), None, ALU.is_equal))
                ch.link(dve.tensor_tensor_scan(rank[:, :], mask_u[:, :], mask_u[:, :], base[:, b:b + 1], ALU.add, ALU.bypass))
                ch.link(dve.copy_predicated(pos[:, :], mask_u[:, :], rank[:, :]))
            dve.tensor_copy(pos_u[:, :], pos[:, :]).then_inc(pos_ready, 1)
            ch.link(dve.tensor_copy(border_i[:, :], upto_b[:, :]))
            ch.link(dve.tensor_scalar(border_i[:, :], border_i[:, :], 7, None, ALU.logical_shift_right))
            ch.link(dve.tensor_copy(border[:, :], border_i[:, :]))
            ch.link(dve.tensor_tensor(border[:, :], border[:, :], g["iota_row"][:, 0:NB], ALU.add))
            ch.link(dve.memset(expert_of[:, :], 0.0))
            for b in range(1, NE):
                ch.link(dve.tensor_scalar(hit[:, :], g["iota_row"][:, 0:64], border[:, b:b + 1], None, ALU.is_ge))
                ch.link(dve.tensor_tensor(expert_of[:, :], expert_of[:, :], hit[:, :], ALU.add))
            ch.link(dve.tensor_tensor(steps_f[:, :], g["iota_row"][:, 0:64], expert_of[:, :], ALU.subtract))
            ch.link(dve.tensor_copy(steps_i[:, 0, :], steps_f[:, :]))
            ch.link(dve.tensor_copy(steps_i[:, 1, :], expert_of[:, :]))
            ch.link(dve.tensor_scalar(steps_i[:, 0, :], steps_i[:, 0, :], P, None, ALU.mult))
            ch.link(dve.tensor_copy(step_tables[:, :, :], steps_i[0:1, :, :]))
            dve.sem_inc(steps_ready, 1)
            for i in rounds_of(dve, NT // 2):
                for u in range(2):
                    t = i * 2 + u
                    wait_from(dve, scattered[u], i * 16)
                    dve.tensor_copy(ring[:, u, 0:D], row(X, t)).then_inc(ring_ready, 1)
                    dve.tensor_copy(ring[:, u, D:XW], row(extra, t)).then_inc(ring_ready, 1)

        def scalar(act):
            act.wait_ge(exp_in, 1)
            act.activation(gates[:, :, :], gates[:, :, :], ACT.Exp).then_inc(exp_out, 1)

        def tensor(pe):
            pe.wait_ge(counted, 1)
            pe.matmul(ps[0][:, 0:NB], g["ones"][:, :], count[:, :], start=True, stop=True)
            pe.matmul(ps[1][:, 0:NB], g["before"][:, :], count[:, :], start=True, stop=True).then_inc(totals, 1)

        def gpsimd(pool):
            pool.wait_ge(pos_ready, 1)
            for i in rounds_of(pool, NT // 2):
                for u in range(2):
                    t = i * 2 + u
                    wait_apart(pool, scattered[u], i * 16, pool_passed)
                    pool.tensor_copy(ring_pos[:, u, :], pos_u[:, ds(t, 1)]).then_inc(ring_at, 1)
                    wait_apart(pool, ring_at, t + 1, pool_passed)
                    wait_apart(pool, ring_ready, t * 2 + 2, pool_passed)
                    pool.indirect_dma_start(out=routed_rows[:, :], out_offset=bass.IndirectOffsetOnAxis(ap=ring_pos[:, u, :], axis=0),
                                            in_=ring[:, u, :], in_offset=None).then_inc(scattered[u], 16)
            for u in range(2):
                pool.wait_ge(scattered[u], 16 * (NT // 2))

        run_block(nc, {"vector": vector, "scalar": scalar, "tensor": tensor, "gpsimd": gpsimd})

    with ExitStack() as c2:
        xr = sb("ex_rows", [P, 4, XW], F32, c2)
        result = sb("ex_result", [P, 2, D], F32, c2)
        target = sb("ex_target", [P, 2, 1], F32, c2)
        target_u = sb("ex_target_u", [P, 4, 1], U32, c2)
        own, result_ready, target_ready = (sem("ex_" + n) for n in ("own", "result_ready", "target_ready"))
        loaded = [sem(f"ex_loaded{k}") for k in range(4)]
        scattered = [sem(f"ex_scattered{u}") for u in range(2)]
        pool_passed = sem("ex_pool_passed")

        def pair_of(slot, lap):
            return lap * 2 + slot // 2

        def stage(dve, t, slot, lap, to):
            wait_from(dve, loaded[slot], (lap + 1) * 16)
            return dve.tensor_scalar(to, xr[:, slot, 0:D], xr[:, slot, D + 3:D + 4], xr[:, slot, D + 4:D + 5], ALU.subtract, ALU.mult)

        def product(pe, t, u, hT):
            e = pe.value_load(step_tables[0:1, 1, ds(t, 1)], min_val=0, max_val=NE - 1)
            for m in range(HC):
                w = wd[:, ds(e, 1), m, :].rearrange("p a d -> p (a d)")
                mm = pe.matmul(ps[6 + u][:, 0:D], hT[:, m, :], w, start=(m == 0), stop=(m == HC - 1))
            return mm

        def consume(dve, t, slot, lap, signal):
            u = slot % 2
            ch = Chain(dve, own, t * 3)
            e = dve.value_load(step_tables[0:1, 1, ds(t, 1)], min_val=0, max_val=NE - 1)
            ch.link(dve.tensor_scalar(target[:, u, :], xr[:, slot, D + 1:D + 2], expert_of[:, ds(t, 1)], float(NT * P), ALU.not_equal, ALU.mult))
            ch.link(dve.tensor_tensor(target[:, u, :], target[:, u, :], xr[:, slot, D + 2:D + 3], ALU.add))
            ch.link(dve.tensor_copy(target_u[:, slot, :], target[:, u, :]))
            wait_from(dve, scattered[u], pair_of(slot, lap) * 16)
            signal(dve.tensor_tensor(result[:, u, :], ps[6 + u][:, 0:D], bd[:, ds(e, 1), :].rearrange("p a d -> p (a d)"), ALU.add))
            wait_from(dve, programs["taken"], t + 1)
            dve.scalar_tensor_tensor(out=result[:, u, :], in0=result[:, u, :], scalar=xr[:, slot, D:D + 1], in1=xr[:, slot, 0:D],
                                     op0=ALU.mult, op1=ALU.add).then_inc(result_ready, 1)

        programs = hidden(g, c2, "fb_", ESTEPS, stage, product, consume)

        def sync(sp):
            def body(t, slot, lap):
                wait_from(sp, result_ready, t - 2)
                first = sp.value_load(step_tables[0:1, 0, ds(t, 1)], min_val=0, max_val=(NT - 1) * P)
                sp.dma_start(xr[:, slot, :], routed_rows[ds(first, P), :]).then_inc(loaded[slot], 16)
            laps(sp, body, ESTEPS)

        def gpsimd(pool):
            def body(t, slot, lap):
                wait_apart(pool, result_ready, t + 2, pool_passed)
                pool.indirect_dma_start(out=out[:, :], out_offset=bass.IndirectOffsetOnAxis(ap=target_u[:, slot, :], axis=0),
                                        in_=result[:, slot % 2, :], in_offset=None, bounds_check=N - 1, oob_is_err=False).then_inc(scattered[slot % 2], 16)
            laps(pool, body, ESTEPS)
            for u in range(2):
                pool.wait_ge(scattered[u], 16 * (ESTEPS // 2))

        def vector(dve):
            dve.sem_inc(result_ready, 1)
            hidden_vector(dve)

        hidden_vector = programs["vector"]
        programs = {**programs, "vector": vector, "sync": sync, "gpsimd": gpsimd}
        run_block(nc, programs)


INPUTS = ["x", "src", "dst", "L0_gnn_W", "L0_gnn_envW", "L0_gnn_envb", "L0_ffn_W_fx", "L0_ffn_b_fx", "L0_ffn_W_x", "L0_ffn_b_x",
          "L0_ffn_W_slice", "L0_ffn_b_slice", "L0_ffn_W_q", "L0_ffn_W_k", "L0_ffn_W_v", "L0_ffn_W_out", "L0_ffn_b_out",
          "L0_ffn_temperature", "L1_gnn_W", "L1_gnn_a_src", "L1_gnn_a_dst", "L1_ffn_W1", "L1_ffn_b1", "L1_ffn_Wg", "L1_ffn_bg",
          "L1_ffn_Wd", "L1_ffn_bd"]


def kernel(**inputs):
    import numpy as np
    import concourse.bacc as bacc
    from concourse.bass_utils import run_bass_kernel_spmd

    nc = bacc.Bacc("TRN2", target_bir_lowering=False, num_devices=1)
    arrays, args = {}, {}
    for name in INPUTS:
        arrays[f"in_{name}"] = a = np.ascontiguousarray(inputs[name])
        args[name] = nc.dram_tensor(f"in_{name}", a.shape, mybir.dt.from_np(a.dtype), kind="ExternalInput").ap()
    out = nc.dram_tensor("out", (N, D), F32, kind="ExternalOutput").ap()
    build(nc, out, **args)
    result = run_bass_kernel_spmd(nc, [arrays], core_ids=[0])
    return result.results[0]["out"]
```
